# Optimizing a Trainium2 kernel written in Bass

```python
import numpy as np
import jax
import jax.numpy as jnp

def _softmax(x, axis=-1):
    return jax.nn.softmax(x, axis=axis)

def _gelu(x):
    return jax.nn.gelu(x, approximate=True)

def _silu(x):
    return jax.nn.silu(x)

def _sigmoid(x):
    return jax.nn.sigmoid(x)

def _layernorm(x, axis=-1, eps=1e-05):
    m = jnp.mean(x, axis=axis, keepdims=True)
    v = jnp.var(x, axis=axis, keepdims=True)
    return (x - m) / jnp.sqrt(v + eps)

def _scatter_add(tgt, idx, src, axis=0):
    return tgt.at[idx].add(src)

def _segment_sum(src, seg, n):
    return jax.ops.segment_sum(src, seg, n)
kernel_name = 'mk_sandwich_d2_jaxref_r8_5852d9'

def setup_inputs(seed: int=0):
    np.random.seed(seed)
    _w = jnp.asarray

    def _L0_attn_setup():
        import jax, jax.numpy as jnp
        import numpy as np
        B, S, D = (2, 512, 256)
        H, DK, DV = (16, 128, 128)
        SEG = 64
        UPDATE = 'delta'
        CAUSAL = True
        key = jax.random.key(seed)
        ks = jax.random.split(key, 6)
        s = 0.02
        return {'x': jax.random.normal(ks[0], (B, S, D), jnp.float32), 'Wq': jax.random.normal(ks[1], (D, H * DK), jnp.float32) * s, 'Wk': jax.random.normal(ks[2], (D, H * DK), jnp.float32) * s, 'Wv': jax.random.normal(ks[3], (D, H * DV), jnp.float32) * s, 'Wo': jax.random.normal(ks[4], (H * DV, D), jnp.float32) * s, 'betas': jax.random.normal(ks[5], (1, H, 1, DV), jnp.float32)}
    _L0_attn_in = _L0_attn_setup()

    def _L0_ffn_setup():
        import jax, jax.numpy as jnp
        import numpy as np
        B, S, D, F, E, K = (2, 256, 256, 512, 8, 1)

        def _silu_mul(gu):
            g, u = jnp.split(gu, 2, axis=-1)
            return jax.nn.silu(g) * u

        def _moe_forward(hidden_states, router_w, w_gate_up, w_down, shared_gate_up, shared_down, top_k=K):
            b, s, d = hidden_states.shape
            x = hidden_states.reshape(-1, d)
            router_logits = x @ router_w.T
            topk_vals, topk_ids = jax.lax.top_k(router_logits, top_k)
            gate = jax.nn.sigmoid(topk_vals.astype(jnp.float32)).astype(x.dtype)
            xs = (x[:, None, :] * gate[:, :, None]).reshape(-1, d)
            ids_flat = topk_ids.reshape(-1)
            n_experts = w_gate_up.shape[0]

            def body(acc, inp):
                wg, wd, e = inp
                h = _silu_mul(xs @ wg)
                o = h @ wd
                mask = (ids_flat == e)[:, None]
                return (acc + jnp.where(mask, o, jnp.zeros((), o.dtype)), None)
            acc0 = jnp.zeros_like(xs)
            routed, _ = jax.lax.scan(body, acc0, (w_gate_up, w_down, jnp.arange(n_experts)))
            routed = routed.reshape(-1, top_k, d).sum(1)
            shared = _silu_mul(x @ shared_gate_up) @ shared_down
            return (routed + shared).reshape(b, s, d)
        key = jax.random.key(seed)
        ks = jax.random.split(key, 6)
        scale = 0.02
        return {'hidden_states': jax.random.normal(ks[0], (B, S, D), jnp.float32), 'router_w': jax.random.normal(ks[1], (E, D), jnp.float32) * scale, 'w_gate_up': jax.random.normal(ks[2], (E, D, 2 * F), jnp.float32) * scale, 'w_down': jax.random.normal(ks[3], (E, F, D), jnp.float32) * scale, 'shared_gate_up': jax.random.normal(ks[4], (D, 2 * F), jnp.float32) * scale, 'shared_down': jax.random.normal(ks[5], (F, D), jnp.float32) * scale}
    _L0_ffn_in = _L0_ffn_setup()

    def _L1_attn_setup():
        import jax, jax.numpy as jnp
        import numpy as np
        D = 256
        key = jax.random.key(seed)
        ks = jax.random.split(key, 5)
        scale = 1.0 / np.sqrt(D)
        x = jax.random.normal(ks[0], (4, 512, D), dtype=jnp.float32)
        Wq = jax.random.normal(ks[1], (D, D), dtype=jnp.float32) * scale
        Wk = jax.random.normal(ks[2], (D, D), dtype=jnp.float32) * scale
        Wv = jax.random.normal(ks[3], (D, D), dtype=jnp.float32) * scale
        Wo = jax.random.normal(ks[4], (D, D), dtype=jnp.float32) * scale
        return {'x': x, 'Wq': Wq, 'Wk': Wk, 'Wv': Wv, 'Wo': Wo}
    _L1_attn_in = _L1_attn_setup()

    def _L1_ffn_setup():
        import jax, jax.numpy as jnp
        import numpy as np
        key = jax.random.key(seed)
        k1, k2, k3, k4 = jax.random.split(key, 4)
        B, S, D_IN, D_OUT = (4, 512, 256, 256)
        x = jax.random.normal(k1, (B, S, D_IN), dtype=jnp.float32)
        weight = jax.random.normal(k2, (D_OUT, D_IN), dtype=jnp.float32) * 0.02
        scale_weight = jax.random.uniform(k3, (D_OUT,), dtype=jnp.float32, minval=0.5, maxval=1.5)
        bias = jax.random.normal(k4, (D_OUT,), dtype=jnp.float32) * 0.02
        return {'x': x, 'weight': weight, 'scale_weight': scale_weight, 'bias': bias}
    _L1_ffn_in = _L1_ffn_setup()
    _d = {'L0_attn_x': _L0_attn_in['x'], 'L0_attn_Wq': _L0_attn_in['Wq'], 'L0_attn_Wk': _L0_attn_in['Wk'], 'L0_attn_Wv': _L0_attn_in['Wv'], 'L0_attn_Wo': _L0_attn_in['Wo'], 'L0_attn_betas': _L0_attn_in['betas'], 'L0_ffn_router_w': _L0_ffn_in['router_w'], 'L0_ffn_w_gate_up': _L0_ffn_in['w_gate_up'], 'L0_ffn_w_down': _L0_ffn_in['w_down'], 'L0_ffn_shared_gate_up': _L0_ffn_in['shared_gate_up'], 'L0_ffn_shared_down': _L0_ffn_in['shared_down'], 'L1_attn_Wq': _L1_attn_in['Wq'], 'L1_attn_Wk': _L1_attn_in['Wk'], 'L1_attn_Wv': _L1_attn_in['Wv'], 'L1_attn_Wo': _L1_attn_in['Wo'], 'L1_ffn_weight': _L1_ffn_in['weight'], 'L1_ffn_scale_weight': _L1_ffn_in['scale_weight'], 'L1_ffn_bias': _L1_ffn_in['bias']}
    _x0 = _d['L0_attn_x']
    _d['L0_attn_x'] = jax.random.normal(jax.random.fold_in(jax.random.key(seed), 1), (4, 512, 256), dtype=_x0.dtype)
    del _x0
    return _d

def reference(L0_attn_x, L0_attn_Wq, L0_attn_Wk, L0_attn_Wv, L0_attn_Wo, L0_attn_betas, L0_ffn_router_w, L0_ffn_w_gate_up, L0_ffn_w_down, L0_ffn_shared_gate_up, L0_ffn_shared_down, L1_attn_Wq, L1_attn_Wk, L1_attn_Wv, L1_attn_Wo, L1_ffn_weight, L1_ffn_scale_weight, L1_ffn_bias):

    def _L0_attn_ref(x, Wq, Wk, Wv, Wo, betas):
        import jax, jax.numpy as jnp
        import numpy as np
        B, S, D = (2, 512, 256)
        H, DK, DV = (16, 128, 128)
        SEG = 64
        UPDATE = 'delta'
        CAUSAL = True
        Bsz, seq, _ = x.shape
        nseg = seq // SEG
        q = (x @ Wq).reshape(Bsz, seq, H, DK).transpose(0, 2, 1, 3)
        k = (x @ Wk).reshape(Bsz, seq, H, DK).transpose(0, 2, 1, 3)
        v = (x @ Wv).reshape(Bsz, seq, H, DV).transpose(0, 2, 1, 3)
        qs = q.reshape(Bsz, H, nseg, SEG, DK).transpose(2, 0, 1, 3, 4)
        ks_ = k.reshape(Bsz, H, nseg, SEG, DK).transpose(2, 0, 1, 3, 4)
        vs = v.reshape(Bsz, H, nseg, SEG, DV).transpose(2, 0, 1, 3, 4)
        causal_mask = jnp.tril(jnp.ones((SEG, SEG), bool))
        scale = DK ** 0.5
        beta = jax.nn.sigmoid(betas)

        def step(carry, seg):
            mem, z = carry
            qq, kk, vv = seg
            sigma_q = jax.nn.elu(qq) + 1.0
            scores = jnp.einsum('bhsk,bhtk->bhst', qq, kk) / scale
            if CAUSAL:
                scores = jnp.where(causal_mask, scores, -jnp.inf)
            att_dot = jax.nn.softmax(scores, axis=-1) @ vv
            att_mem = sigma_q @ mem / (sigma_q @ z)
            sigma_k = jax.nn.elu(kk) + 1.0
            if UPDATE == 'linear':
                mem_new = mem + jnp.einsum('bhsk,bhsv->bhkv', sigma_k, vv)
            else:
                delta = vv - sigma_k @ mem / (sigma_k @ z)
                mem_new = mem + jnp.einsum('bhsk,bhsv->bhkv', sigma_k, delta)
            z_new = z + sigma_k.sum(axis=-2, keepdims=True).transpose(0, 1, 3, 2)
            att = beta * att_mem + (1.0 - beta) * att_dot
            out = att.reshape(Bsz, SEG, H * DV) @ Wo
            return ((mem_new, z_new), out)
        mem0 = jnp.zeros((Bsz, H, DK, DV), x.dtype)
        z0 = jnp.ones((Bsz, H, DK, 1), x.dtype) / DK
        _, outs = jax.lax.scan(step, (mem0, z0), (qs, ks_, vs))
        return outs.transpose(1, 0, 2, 3).reshape(Bsz, seq, D)

    def _L0_ffn_ref(hidden_states, router_w, w_gate_up, w_down, shared_gate_up, shared_down):
        import jax, jax.numpy as jnp
        import numpy as np
        B, S, D, F, E, K = (2, 256, 256, 512, 8, 1)

        def _silu_mul(gu):
            g, u = jnp.split(gu, 2, axis=-1)
            return jax.nn.silu(g) * u

        def _moe_forward(hidden_states, router_w, w_gate_up, w_down, shared_gate_up, shared_down, top_k=K):
            b, s, d = hidden_states.shape
            x = hidden_states.reshape(-1, d)
            router_logits = x @ router_w.T
            topk_vals, topk_ids = jax.lax.top_k(router_logits, top_k)
            gate = jax.nn.sigmoid(topk_vals.astype(jnp.float32)).astype(x.dtype)
            xs = (x[:, None, :] * gate[:, :, None]).reshape(-1, d)
            ids_flat = topk_ids.reshape(-1)
            n_experts = w_gate_up.shape[0]

            def body(acc, inp):
                wg, wd, e = inp
                h = _silu_mul(xs @ wg)
                o = h @ wd
                mask = (ids_flat == e)[:, None]
                return (acc + jnp.where(mask, o, jnp.zeros((), o.dtype)), None)
            acc0 = jnp.zeros_like(xs)
            routed, _ = jax.lax.scan(body, acc0, (w_gate_up, w_down, jnp.arange(n_experts)))
            routed = routed.reshape(-1, top_k, d).sum(1)
            shared = _silu_mul(x @ shared_gate_up) @ shared_down
            return (routed + shared).reshape(b, s, d)
        return _moe_forward(hidden_states, router_w, w_gate_up, w_down, shared_gate_up, shared_down)

    def _L1_attn_ref(x, Wq, Wk, Wv, Wo):
        import jax, jax.numpy as jnp
        import numpy as np
        D = 256
        q = jnp.einsum('bsd,ed->bse', x, Wq)
        k = jnp.einsum('bsd,ed->bse', x, Wk)
        v = jnp.einsum('bsd,ed->bse', x, Wv)
        seq = x.shape[-2]
        denom = jnp.sqrt(jnp.float32(x.shape[-1])) / seq
        kvt = jnp.cumsum(k * v, axis=-2) * denom
        vhat = q * kvt
        return jnp.einsum('bse,fe->bsf', vhat, Wo)

    def _L1_ffn_ref(x, weight, scale_weight, bias):
        import jax, jax.numpy as jnp
        import numpy as np
        w = weight * scale_weight[:, None]
        out = jnp.einsum('bsi,oi->bso', x, w) + bias
        return out
    x = L0_attn_x
    x = x + _layernorm(_L0_attn_ref(_layernorm(x, axis=-1), L0_attn_Wq, L0_attn_Wk, L0_attn_Wv, L0_attn_Wo, L0_attn_betas), axis=-1)
    x = x + _layernorm(_L0_ffn_ref(_layernorm(x, axis=-1), L0_ffn_router_w, L0_ffn_w_gate_up, L0_ffn_w_down, L0_ffn_shared_gate_up, L0_ffn_shared_down), axis=-1)
    x = x + _layernorm(_L1_attn_ref(_layernorm(x, axis=-1), L1_attn_Wq, L1_attn_Wk, L1_attn_Wv, L1_attn_Wo), axis=-1)
    x = x + _layernorm(_L1_ffn_ref(_layernorm(x, axis=-1), L1_ffn_weight, L1_ffn_scale_weight, L1_ffn_bias), axis=-1)
    return x

_drawn_inputs = setup_inputs


def setup_inputs(seed=0):
    import zlib

    import numpy as np

    out = dict(_drawn_inputs(seed))
    spreads = {}
    factors = {}
    for name, (base, spread) in spreads.items():
        noise = np.random.default_rng([zlib.crc32(name.encode()), seed]).standard_normal(out[name].shape)
        drawn = base * np.exp(spread * noise) if base else spread * noise
        out[name] = jnp.asarray(drawn.astype(out[name].dtype))
    for name, factor in factors.items():
        out[name] = (out[name] * factor).astype(out[name].dtype)
    return out
```

```python
from contextlib import ExitStack

import concourse.bass as bass
from concourse import mybir

P = 128
B, S, D = 4, 512, 256
H, DK, SEG = 16, 128, 64
NSEG = S // SEG
NJ = S // P
NT = B * NJ
DC = D // P
MEM = DK + 1
EPS = 1e-5
E, F = 8, 512
FC = F // P
JOBS = NT + E - 1
LNS = 4 * NJ + 3 * B
DENOM = float(D) ** 0.5 / S
SCALE = float(DK) ** -0.5
MASKED = -1e30

ALU = mybir.AluOpType
ACT = mybir.ActivationFunctionType
AX = mybir.AxisListType
F32 = mybir.dt.float32
ds = bass.ds


QK_AT = [0, 2, 3, 4]
SC_AT = [1, 3, 4, 5]
V_AT = [5, 5, 6, 6]
PT_AT = [3, 5, 6, 7]
SUM_AT = [2, 4, 5, 6]


def plan_banks():
    full = []
    for i in range(NSEG):
        for b in range(B):
            if QK_AT[b] == i:
                full += [("q", b), ("k", b)]
        for b in range(B):
            if SC_AT[b] == i:
                full += [("sk", b), ("sc", b)]
        full += [("V", b) for b in range(B) if V_AT[b] == i]
        full += [("PT", b) for b in range(B) if PT_AT[b] == i]
        if i == 1:
            full += [("Wo",)]
        if i % 2:
            full += [("PV", (i - 1) // 2)]
        else:
            full += [("attT", (i - 2) // 2 if i else NJ - 1)]
    used, turn, bank = [0] * 4, {}, {}
    for n in range(-1, H + 1):
        for at, name in enumerate(full):
            kind = name[0]
            if kind in ("q", "k", "sk", "sc", "V", "PT"):
                there = n + 1 < H
            elif kind == "Wo" or name == ("attT", NJ - 1):
                there = n >= 1
            else:
                there = 0 <= n < H
            if there:
                bank[name] = at % 4
                turn[n, name] = used[at % 4]
                used[at % 4] += 1
    return bank, turn, [sum(at % 4 == k for at in range(len(full))) for k in range(4)]


class Body:
    BANK, TURN, USES = plan_banks()

    def __init__(self, first, loop=None):
        self.first, self.loop = first, loop
        self.par = first % 2
        self.chain = loop is not None or 0 <= first < H
        self.heads_on = loop is not None or first + 1 < H
        self.tail = loop is not None or first >= 1

    def count(self, per_body, c=0):
        v = per_body * self.first + c
        return v if self.loop is None else v + 2 * per_body * self.loop

    def turn(self, name, back=0):
        v = self.TURN[self.first - back, name]
        if self.loop is None:
            return v
        uses = self.USES[self.BANK[name]]
        assert v + uses == self.TURN[self.first - back + 1, name]
        return v + 2 * uses * self.loop


def sandwich(nc, dram, out):
    with ExitStack() as ctx:
        def sb(name, shape, dt=F32):
            return ctx.enter_context(nc.sbuf_tensor(name, shape, dt))

        def sem(name):
            return ctx.enter_context(nc.semaphore(name))

        def sems(name, n):
            return [sem(f"{name}{i}") for i in range(n)]

        work = [ctx.enter_context(nc.psum_tensor(f"work{i}", [P, 512], F32)) for i in range(4)]
        readp = [ctx.enter_context(nc.psum_tensor(f"readp{i}", [P, 2, 256], F32)) for i in range(2)]
        memp = [ctx.enter_context(nc.psum_tensor(f"memp{i}", [P, 2, 256], F32)) for i in range(2)]

        ident = sb("ident", [P, P])
        mask = sb("mask", [P, SEG])
        seed_l = sb("seed_l", [P, P])
        seed_r = sb("seed_r", [P, 2, MEM])
        stats = sb("stats", [P, NT, 6])
        mv = sb("mv", [P, NT, 2])
        vareps = sb("vareps", [P, NT])
        rstd = sb("rstd", [P, NT])
        minushalf = sb("minushalf", [P, NJ])
        rden = sb("rden", [P, 2, B])
        rowmax = sb("rowmax", [P, 2, NJ])
        rowsum = sb("rowsum", [P, B, NJ])
        rinv = sb("rinv", [P, 2, B, NJ])
        wqkv = sb("wqkv", [P, 2, 3, DC, DK])
        mem = sb("mem", [P, B, MEM + 1])
        delta = sb("delta", [P, B, MEM + 1])
        Y = sb("Y", [P, H, D])
        arena = sb("arena", [P, 45568])
        at = [0]

        def carve(*shape):
            n = 1
            for x in shape:
                n *= x
            v = arena[:, at[0]:at[0] + n]
            at[0] += n
            assert at[0] <= 45568
            if len(shape) == 1:
                return v
            names = "abcd"[:len(shape)]
            return v.rearrange(f"p ({' '.join(names)}) -> p {' '.join(names)}", **dict(zip(names, shape)))

        xT = carve(DC, B, S)
        raw = carve(2, B, S)
        plus1 = carve(2, S)
        sqk = carve(2, B, NSEG, P)
        skt = carve(2, B, NJ, P)
        vb = carve(2, B, NJ, P)
        v1 = carve(2, B, NJ, P)
        pt = carve(2, B, NJ, P)
        pbd = carve(B, NJ, P)
        sm = carve(2, NJ, SEG)
        fromm = carve(2, B, P)
        attT = carve(B, NJ, P)
        bB = carve(H * P)
        wo = carve(H, D)
        xin = sqk[:, 1].rearrange("p b s c -> p (b s c)").rearrange("p (b j d) -> p b j d", b=B, j=NJ)
        xnorm = raw.rearrange("p a b s -> p (a b s)").rearrange("p (b j d) -> p b j d", b=B, j=NJ)
        braw = skt[:, 1].rearrange("p b j c -> p (b j c)")
        b1 = vb[:, 1].rearrange("p b j c -> p (b j c)")


        at[0] = 0
        x1 = carve(NT, D)
        wgu = carve(E + 1, DC, 2 * F)
        wdn = carve(E + 1, FC, D)
        shared = carve(NT, D)
        xrow = carve(2, D)
        xj = carve(2, D)
        hrow = carve(2, F)
        sgate = carve(2, F)
        hcol = carve(2, F)
        yj = carve(2, D)
        tri = carve(P)
        ones = carve(P)
        rwT = carve(DC, E)
        rwraw = carve(D)
        onehot = carve(NT, E)
        down8 = carve(E)
        logit = carve(NT, E)
        istop = carve(NT, E)
        toplogit = carve(NT)
        chosen = carve(NT)
        gate = carve(NT)
        before = carve(NT, E)
        total = carve(E, NT)
        running = carve(E, NT)
        resets = carve(E, NT)
        count8 = carve(E)
        tiles8 = carve(E)
        tilesf = carve(E)
        ends = carve(E)
        starts = carve(E)
        posf = carve(NT)
        pos = carve(NT)
        jobno = carve(JOBS + 1)
        later = carve(JOBS + 1, E)
        jobe = carve(JOBS + 1)
        jobi = carve(JOBS + 1)
        lnst = carve(4, 6)
        lnm = carve(LNS * 4, 2)
        lnv = carve(LNS * 4)
        lnr = carve(LNS * 4)
        wqkvT = wqkv[:].rearrange("p a b c d -> p (a b c d)").rearrange("p (w c d) -> p w c d", w=3, c=DC)
        wofT = carve(2, DC, D)
        bias = carve(D)
        wscale = carve(DC)
        l1raw = shared.rearrange("p t d -> p (t d)")[:, 0:5 * DC * D].rearrange("p (w c d) -> p w c d", w=5, c=DC)
        at[0] = NT * D
        x2T = carve(DC, B * S)
        x2n = carve(2, NJ, D)
        x3 = carve(2, NJ, D)
        xn3 = carve(2, NJ, D)
        x3T = carve(2, NJ, D)
        kbuf = carve(2, S)
        kv = carve(2, S)
        kvt = carve(2, S)
        vh = carve(2, DC, S)
        lnout = carve(2, NJ, D)
        x4 = carve(2, NJ, D)
        xs_d = nc.dram_tensor("rows_by_expert", [JOBS * P, D], F32).ap()
        ys_d = nc.dram_tensor("outputs_by_expert", [JOBS * P, D], F32).ap()
        x2_d = nc.dram_tensor("residual", [B * S, D], F32).ap()

        loaded_x = sems("loaded_x", B)
        loaded_beta = sem("loaded_beta")
        consts = sem("consts")
        beta_e = sem("beta_e")
        beta_step = sem("beta_step")
        x_stats = sem("x_stats")
        x_var = sem("x_var")
        x_rstd = sem("x_rstd")
        x_normed = sem("x_normed")
        xT_written = sems("xT_written", 4)
        xT_copied = sem("xT_copied")
        w_loaded = sems("w_loaded", 2)
        wo_loaded = sem("wo_loaded")
        vb_ready = sem("vb_ready")
        filled = sems("filled", 4)
        freed = sems("freed", 4)
        proj_done = sem("proj_done")
        raw_ready = sem("raw_ready")
        plus1_done = sem("plus1_done")
        sigma_done = sem("sigma_done")
        score_masked = sem("score_masked")
        max_ready = sem("max_ready")
        score_shifted = sem("score_shifted")
        probs_ready = sem("probs_ready")
        sum_ready = sem("sum_ready")
        rinv_ready = sem("rinv_ready")
        mem_written = sems("mem_written", 2)
        mem_copied = sems("mem_copied", 2)
        read_done = sems("read_done", 2)
        rden_ready = sems("rden_ready", 2)
        fromm_ready = sems("fromm_ready", 2)
        delta_ready = sems("delta_ready", 2)
        att_ready = sem("att_ready")
        attn_done = sem("attn_done")

        x_v = dram["L0_attn_x"].rearrange("b (j p) d -> b p j d", p=P)
        w_v = [dram[f"L0_attn_W{c}"].rearrange("(c p) n -> p c n", p=P) for c in "qkv"]
        wo_v = dram["L0_attn_Wo"].rearrange("(c p) n -> p c n", p=P)
        beta_v = dram["L0_attn_betas"].rearrange("a h b d -> (a h b) d").rearrange("h d -> (h d)")

        xs_zeroed = sem("xs_zeroed")
        small_loaded = sem("small_loaded")
        l1_loaded = sem("l1_loaded")
        shared_loaded = sem("shared_loaded")
        experts_loaded = sem("experts_loaded")
        post_consts = sem("post_consts")
        ln_step = sem("ln_step")
        ln_var = sem("ln_var")
        ln_rstd = sem("ln_rstd")
        x1_ready = sem("x1_ready")
        l1_turned = sem("l1_turned")
        l1_copied = sem("l1_copied")
        wscaled = sem("wscaled")
        xrow_ready = sem("xrow_ready")
        x_turned = sem("x_turned")
        xj_copied = sem("xj_copied")
        x_used = sem("x_used")
        logit_copied = sem("logit_copied")
        top_done = sem("top_done")
        gate_exp = sem("gate_exp")
        route_step = sem("route_step")
        onehot_ready = sem("onehot_ready")
        ranks_done = sem("ranks_done")
        xs_ready = sem("xs_ready")
        xs_scattered = sem("xs_scattered")
        silu_done = sem("silu_done")
        h_ready = sem("h_ready")
        hT_turned = sem("hT_turned")
        hT_copied = sem("hT_copied")
        down_done = sem("down_done")
        y_out = sem("y_out")
        x2_stored = sem("x2_stored")
        xn2_ready = sem("xn2_ready")
        x2_turned = sem("x2_turned")
        x2T_copied = sem("x2T_copied")
        o_done = sem("o_done")
        o_used = sem("o_used")
        x3_ready = sem("x3_ready")
        xn3_ready = sem("xn3_ready")
        t3_done = sem("t3_done")
        x3T_copied = sem("x3T_copied")
        f_done = sem("f_done")
        f_used = sem("f_used")
        x4_ready = sem("x4_ready")
        kv_step = sem("kv_step")
        x1_loaded = sems("x1_loaded", NJ)
        xs_loaded = sems("xs_loaded", 2)
        y_stored = sems("y_stored", 2)
        y_gathered = sems("y_gathered", NJ)
        x2n_loaded = sems("x2n_loaded", 2)
        k_copied = sems("k_copied", 2)
        qkv_done = sems("qkv_done", 2)
        vh_done = sems("vh_done", 2)
        x4_stored = sems("x4_stored", 2)

        by_head = "b (i h r) d -> h (b i) r d"
        x_h = dram["L0_attn_x"].rearrange(by_head, h=H, r=4)
        x2_h = x2_d.rearrange("(g h r) d -> h g r d", h=H, r=4)
        flat = [readp[r][:].rearrange("p a c -> p (a c)") for r in range(2)]
        mflat = [memp[r][:].rearrange("p a c -> p (a c)") for r in range(2)]
        posi = pos.bitcast(mybir.dt.uint32)
        SHARED, ROUTED = NT, 2 * NT

        block = ctx.enter_context(nc.Block())

        def own(i):
            return slice(SEG * (i % 2), SEG * (i % 2) + SEG)

        def sigma_places(m, b, qk):
            pairs = sqk[:, m, b].rearrange("p s c -> p (s c)").rearrange("p (j x) -> p j x", j=NJ)
            if qk:
                return pairs[:, :, SEG:3 * SEG]
            return pairs.rearrange("p j (a c) -> p j a c", a=4)[:, :, 0:4:3]

        def like(x, qk):
            x = x.rearrange("p (j x) -> p j x", j=NJ)
            return x if qk else x.rearrange("p j (a c) -> p j a c", a=2)

        def bodies(eng, body):
            body(Body(-1))
            body(Body(0))
            with eng.Fori(0, (H - 2) // 2) as turn:
                body(Body(1, turn))
                body(Body(2, turn))
            body(Body(H - 1))
            body(Body(H))

        @block.sync
        def _(sp):
            for b in range(B):
                sp.dma_start(xin[:, b], x_v[b]).then_inc(loaded_x[b], 16)
            sp.wait_ge(consts, 12)
            xs_t = xs_d.rearrange("(t p) d -> p t d", p=P)
            sp.dma_start(xs_t[:, 0:NT], Y[:]).then_inc(xs_zeroed, 16)
            sp.dma_start(xs_t[:, NT:JOBS], Y[:, 0:JOBS - NT]).then_inc(xs_zeroed, 16)
            sp.dma_start(braw, beta_v.partition_broadcast(P)).then_inc(loaded_beta, 16)

            def load_w(g, par):
                for c in range(3):
                    sp.dma_start(wqkv[:, par, c], w_v[c][:, :, ds(g * DK, DK)]).then_inc(w_loaded[par], 16)

            load_w(0, 0)
            load_w(1, 1)
            sp.dma_start(wo, wo_v).then_inc(wo_loaded, 16)

            def load_next(g, par):
                sp.wait_ge(proj_done, g - 1)
                load_w(g, par)

            with sp.Fori(0, (H - 2) // 2) as turn:
                load_next(turn * 2 + 2, 0)
                load_next(turn * 2 + 3, 1)

            sp.wait_ge(attn_done, 1)
            for t in range(NT):
                sp.dma_start(x1[:, t], x_h[t]).then_inc(x1_loaded[t // 4], 16)
            sp.dma_start(rwraw[0:E, :], dram["L0_ffn_router_w"]).then_inc(small_loaded, 16)
            sp.dma_start(bias, dram["L1_ffn_bias"].partition_broadcast(P)).then_inc(small_loaded, 16)
            with nc.allow_non_contiguous_dma("256 numbers"):
                sp.dma_start(wscale, dram["L1_ffn_scale_weight"].rearrange("(c p) -> p c", p=P)).then_inc(small_loaded, 16)
            for w, name in enumerate(["L1_attn_Wq", "L1_attn_Wk", "L1_attn_Wv", "L1_attn_Wo", "L1_ffn_weight"]):
                sp.dma_start(l1raw[:, w], dram[name].rearrange("(c p) n -> p c n", p=P)).then_inc(l1_loaded, 16)
            sp.dma_start(wgu[:, E], dram["L0_ffn_shared_gate_up"].rearrange("(c p) n -> p c n", p=P)).then_inc(shared_loaded, 16)
            sp.dma_start(wdn[:, E], dram["L0_ffn_shared_down"].rearrange("(c p) n -> p c n", p=P)).then_inc(shared_loaded, 16)
            for e in range(E):
                sp.dma_start(wgu[:, e], dram["L0_ffn_w_gate_up"][e].rearrange("(c p) n -> p c n", p=P)).then_inc(experts_loaded, 16)
                sp.dma_start(wdn[:, e], dram["L0_ffn_w_down"][e].rearrange("(c p) n -> p c n", p=P)).then_inc(experts_loaded, 16)

            sp.wait_ge(xs_scattered, 16 * NT)

            def load_rows(j, par):
                sp.wait_ge(x_turned, j + ROUTED - 1)
                sp.dma_start(xrow[:, par], xs_d[ds(j * P, P), :]).then_inc(xs_loaded[par], 16)

            with sp.Fori(0, JOBS // 2) as pair:
                load_rows(pair * 2, 0)
                load_rows(pair * 2 + 1, 1)
            load_rows(JOBS - 1, 0)

            for g in range(NJ):
                sp.wait_ge(x1_ready, NJ + g + 1)
                for t in range(4 * g, 4 * g + 4):
                    sp.dma_start(x2_h[t], x1[:, t]).then_inc(x2_stored, 16)
            sp.wait_ge(x2_stored, 16 * NT)
            x2_v = x2_d.rearrange("(b j p) d -> b p j d", j=NJ, p=P)
            out_v = out.rearrange("b (j p) d -> b p j d", p=P)
            for b in range(2):
                sp.dma_start(x2n[:, b], x2_v[b]).then_inc(x2n_loaded[b], 16)
            for b in range(B):
                sp.wait_ge(x4_ready, b + 1)
                sp.dma_start(out_v[b], x4[:, b % 2]).then_inc(x4_stored[b % 2], 16)
                if b + 2 < B:
                    sp.dma_start(x2n[:, b % 2], x2_v[b + 2]).then_inc(x2n_loaded[b % 2], 16)
            for par in range(2):
                sp.wait_ge(x4_stored[par], 16 * (B // 2))

        @block.gpsimd
        def _(pool):
            pool.memset(ident[:], 0.0).then_inc(consts, 1)
            pool.memset(mask[:], 0.0).then_inc(consts, 1)
            pool.memset(seed_l[:], 1.0 / (DK * P)).then_inc(consts, 1)
            pool.memset(seed_r[:], 0.0).then_inc(consts, 1)
            pool.memset(minushalf[:], -0.5).then_inc(consts, 1)
            pool.memset(delta[:], 1.0).then_inc(consts, 1)
            pool.memset(Y[:], 0.0).then_inc(consts, 1)
            pool.memset(pbd, 0.0).then_inc(consts, 1)
            pool.wait_ge(consts, 8)
            pool.affine_select(out=ident[:], in_=ident[:], compare_op=ALU.not_equal, fill=1.0, base=0,
                               pattern=[[-1, P]], channel_multiplier=1).then_inc(consts, 1)
            for half in range(2):
                pool.wait_ge(consts, 9 + half)
                pool.affine_select(out=mask[SEG * half:SEG * half + SEG, :], in_=mask[SEG * half:SEG * half + SEG, :],
                                   compare_op=ALU.is_ge, fill=MASKED, base=0,
                                   pattern=[[-1, SEG]], channel_multiplier=1).then_inc(consts, 1)
            pool.wait_ge(consts, 11)
            pool.memset(seed_r[:, :, DK:MEM], 1.0).then_inc(consts, 1)
            for b in range(B):
                pool.wait_ge(x_var, b + 1)
                pool.tensor_tensor(rstd[:, b * NJ:(b + 1) * NJ], vareps[:, b * NJ:(b + 1) * NJ], minushalf[:],
                                   ALU.pow).then_inc(x_rstd, 1)

            def body(n):
                if not n.heads_on:
                    return
                for b in range(B):
                    for qk in range(2):
                        t = 2 * b + qk
                        pool.wait_ge(raw_ready, n.count(2 * B, 2 * B + t + 1))
                        if n.first >= 0 or t >= 2:
                            pool.wait_ge(sigma_done, n.count(2 * B, 2 * B + t - 1))
                        pool.tensor_tensor(plus1[:, t % 2], raw[:, qk, b], seed_r[:, 0, DK:MEM].to_broadcast([P, S]),
                                           ALU.add).then_inc(plus1_done, 1)

            pool.wait_ge(consts, 12)
            bodies(pool, body)

            pool.wait_ge(attn_done, 1)
            pool.memset(tri, 1.0).then_inc(post_consts, 1)
            pool.memset(ones, 1.0).then_inc(post_consts, 1)
            pool.memset(resets, 1.0).then_inc(post_consts, 1)
            pool.iota(chosen[:, 0:E].bitcast(mybir.dt.int32), [[-1, E]], base=E, channel_multiplier=0).then_inc(post_consts, 1)
            pool.iota(jobi.bitcast(mybir.dt.int32), [[1, JOBS + 1]], base=0, channel_multiplier=0).then_inc(post_consts, 1)
            pool.wait_ge(post_consts, 5)
            pool.tensor_copy(down8, chosen[:, 0:E].bitcast(mybir.dt.int32)).then_inc(post_consts, 1)
            pool.tensor_copy(jobno, jobi.bitcast(mybir.dt.int32)).then_inc(post_consts, 1)
            pool.memset(resets[:, :, 0], 0.0).then_inc(post_consts, 1)
            pool.affine_select(out=tri, in_=tri, compare_op=ALU.is_ge, fill=0.0, base=-1,
                               pattern=[[1, P]], channel_multiplier=-1).then_inc(post_consts, 1)

            def rstds(k):
                pool.wait_ge(ln_var, k + 1)
                pool.tensor_tensor(lnr[:, 4 * k:4 * k + 4], lnv[:, 4 * k:4 * k + 4], minushalf[:],
                                   ALU.pow).then_inc(ln_rstd, 1)

            for k in range(2 * NJ):
                rstds(k)
            pool.wait_ge(xs_zeroed, 32)
            for t in range(NT):
                pool.wait_ge(xs_ready, t + 1)
                pool.indirect_dma_start(out=xs_d, out_offset=bass.IndirectOffsetOnAxis(posi[:, t:t + 1], 0),
                                        in_=Y[:, t], in_offset=None).then_inc(xs_scattered, 16)

            def store_y(j, par):
                pool.wait_ge(y_out, j + NT + 1)
                pool.dma_start(ys_d[ds(j * P, P), :], yj[:, par]).then_inc(y_stored[par], 16)

            with pool.Fori(0, JOBS // 2) as pair:
                store_y(pair * 2, 0)
                store_y(pair * 2 + 1, 1)
            store_y(JOBS - 1, 0)
            pool.wait_ge(y_stored[0], 16 * ((JOBS + 1) // 2))
            pool.wait_ge(y_stored[1], 16 * (JOBS // 2))
            for t in range(NT):
                pool.indirect_dma_start(out=Y[:, t], out_offset=None, in_=ys_d,
                                        in_offset=bass.IndirectOffsetOnAxis(posi[:, t:t + 1], 0))\
                    .then_inc(y_gathered[t // 4], 16)
            for k in range(2 * NJ, LNS):
                rstds(k)

        @block.vector
        def _(dve):
            for b in range(B):
                dve.wait_ge(loaded_x[b], 16)
                for j in range(NJ):
                    dve.bn_stats(stats[:, b * NJ + j], xin[:, b, j]).then_inc(x_stats, 1)
                for j in range(NJ):
                    t = b * NJ + j
                    dve.wait_ge(x_stats, NJ * 2 * b + j + 1)
                    dve.bn_aggr(mv[:, t], stats[:, t]).then_inc(x_stats, 1)
                dve.wait_ge(x_stats, NJ * 2 * (b + 1))
                dve.tensor_scalar(vareps[:, b * NJ:(b + 1) * NJ], mv[:, b * NJ:(b + 1) * NJ, 1], EPS, None,
                                  ALU.add).then_inc(x_var, 1)
            for b in range(B):
                dve.wait_ge(x_rstd, b + 1)
                for j in range(NJ):
                    t = b * NJ + j
                    dve.tensor_scalar(xnorm[:, b, j], xin[:, b, j], mv[:, t, 0:1], rstd[:, t:t + 1],
                                      ALU.subtract, ALU.mult).then_inc(x_normed, 1)
            dve.wait_ge(beta_e, 1)
            dve.tensor_scalar(b1, b1, 1.0, None, ALU.add).then_inc(beta_step, 1)
            dve.wait_ge(beta_step, 1)
            dve.reciprocal(bB, b1).then_inc(beta_step, 1)
            dve.wait_ge(beta_step, 2)
            dve.wait_ge(consts, 12)

            def combine(n, j, back):
                m = (n.par + back) % 2
                name = ("PV", j)
                dve.wait_ge(filled[n.BANK[name]], n.turn(name, back) + 1)
                for r in range(2):
                    dve.wait_ge(fromm_ready[r], n.count(NSEG, 2 * j + 2 - NSEG * back))
                dve.wait_ge(rinv_ready, n.count(B, B - B * back))
                w = work[n.BANK[name]]
                for b in range(B):
                    ins = dve.scalar_tensor_tensor(out=fromm[:, j % 2, b], in0=w[:, b * P:(b + 1) * P],
                                                   scalar=rinv[:, m, b, j:j + 1], in1=fromm[:, j % 2, b],
                                                   op0=ALU.mult, op1=ALU.add)
                    if b == B - 2:
                        ins.then_inc(att_ready, 1)
                ins.then_inc(freed[n.BANK[name]], 1)

            def deltas(n, i):
                o, k = own(i), own(i + 1)
                for r in range(2):
                    dve.wait_ge(read_done[r], n.count(NSEG, i + 1))
                    dve.reciprocal(rden[:, i % 2, 2 * r:2 * r + 2], readp[r][:, :, DK]).then_inc(rden_ready[r], 1)
                    if i == NSEG - 1:
                        continue
                    dve.wait_ge(rden_ready[r], n.count(NSEG, i + 1))
                    for bb in range(2):
                        b = 2 * r + bb
                        ins = dve.scalar_tensor_tensor(out=delta[o, b, 0:DK], in0=readp[r][k, bb, 0:DK],
                                                       scalar=rden[k, i % 2, b:b + 1], in1=vb[o, n.par, b, i // 2],
                                                       op0=ALU.mult, op1=ALU.subtract, reverse1=True)
                    ins.then_inc(delta_ready[r], 1)

            def scores_shift(n, b):
                name = ("sc", b)
                w = work[n.BANK[name]][:, 0:NJ * SEG].rearrange("p (j c) -> p j c", j=NJ)
                dve.wait_ge(filled[n.BANK[name]], n.turn(name) + 1)
                dve.tensor_tensor(sm[:, b % 2], w, mask[:].unsqueeze(1).to_broadcast([P, NJ, SEG]),
                                  ALU.add).then_inc(freed[n.BANK[name]], 1)
                dve.wait_ge(freed[n.BANK[name]], n.turn(name) + 1)
                dve.tensor_reduce(rowmax[:, b % 2], sm[:, b % 2], AX.X, ALU.max).then_inc(max_ready, 1)
                dve.wait_ge(max_ready, n.count(B, B + b + 1))
                dve.tensor_tensor(sm[:, b % 2], sm[:, b % 2],
                                  rowmax[:, b % 2].unsqueeze(2).to_broadcast([P, NJ, SEG]),
                                  ALU.subtract).then_inc(score_shifted, 1)

            def row_sums(n, b):
                dve.wait_ge(probs_ready, n.count(B, B + b + 1))
                dve.tensor_reduce(rowsum[:, b], pbd[:, b], AX.X, ALU.add).then_inc(sum_ready, 1)
                dve.wait_ge(sum_ready, n.count(B, B + b + 1))
                dve.reciprocal(rinv[:, 1 - n.par, b], rowsum[:, b]).then_inc(rinv_ready, 1)

            def values(n, b):
                name = ("V", b)
                g = n.first + 1 if n.loop is None else n.first + 1 + 2 * n.loop
                w = work[n.BANK[name]][:].rearrange("p (j c) -> p j c", j=NJ)
                dve.wait_ge(filled[n.BANK[name]], n.turn(name) + 1)
                dve.tensor_tensor(vb[:, 1 - n.par, b], w, bB[:, ds(g * P, P)].unsqueeze(1).to_broadcast([P, NJ, P]),
                                  ALU.mult).then_inc(vb_ready, 1)
                dve.wait_ge(vb_ready, n.count(B, B + b + 1))
                dve.tensor_tensor(v1[:, 1 - n.par, b], w, vb[:, 1 - n.par, b], ALU.subtract).then_inc(freed[n.BANK[name]], 1)

            def sigmas(n, b):
                for qk in range(2):
                    t = 2 * b + qk
                    name = ("qk"[qk], b)
                    dve.wait_ge(freed[n.BANK[name]], n.turn(name) + 1)
                    dve.wait_ge(plus1_done, n.count(2 * B, 2 * B + t + 1))
                    y = sigma_places(1 - n.par, b, qk)
                    more = like(plus1[:, t % 2], qk)
                    for a, c in [(y, more)] if qk else [(y[:, :, e], more[:, :, e]) for e in range(2)]:
                        ins = dve.scalar_tensor_tensor(out=a, in0=a, scalar=1.0, in1=c, op0=ALU.min, op1=ALU.max)
                    ins.then_inc(sigma_done, 1)

            def body(n):
                for i in range(NSEG):
                    if i % 2 == 0:
                        if i == 0 and n.tail:
                            combine(n, NJ - 1, 1)
                        elif i and n.chain:
                            combine(n, (i - 2) // 2, 0)
                    if n.chain:
                        deltas(n, i)
                    for b in range(B):
                        if n.heads_on and SC_AT[b] == i:
                            scores_shift(n, b)
                    for b in range(B):
                        if n.heads_on and V_AT[b] == i:
                            values(n, b)
                    for b in range(B):
                        if n.heads_on and SUM_AT[b] == i:
                            row_sums(n, b)
                    for b in range(B):
                        if n.heads_on and QK_AT[b] == i:
                            sigmas(n, b)

            bodies(dve, body)

            dve.wait_ge(attn_done, 1)
            done = [0, 0]

            def step(ins):
                done[0] += 1
                ins.then_inc(ln_step, 1)

            def ln_stats(tiles):
                k = done[1]
                for x in range(4):
                    step(dve.bn_stats(lnst[:, x], tiles[:, x]))
                for x in range(4):
                    dve.wait_ge(ln_step, done[0] - 3)
                    step(dve.bn_aggr(lnm[:, 4 * k + x], lnst[:, x]))
                dve.wait_ge(ln_step, done[0])
                dve.tensor_scalar(lnv[:, 4 * k:4 * k + 4], lnm[:, 4 * k:4 * k + 4, 1], EPS, None,
                                  ALU.add).then_inc(ln_var, 1)
                done[1] += 1

            def ln_apply(to, tiles, k, signal=None):
                dve.wait_ge(ln_rstd, k + 1)
                for x in range(4):
                    ins = dve.tensor_scalar(to[:, x], tiles[:, x], lnm[:, 4 * k + x, 0:1],
                                            lnr[:, 4 * k + x:4 * k + x + 1], ALU.subtract, ALU.mult)
                    if signal is not None:
                        ins.then_inc(signal, 1)
                    elif x == 3:
                        step(ins)

            def group(a, g):
                return a[:, 4 * g:4 * g + 4]

            def residual(g, k):
                ln_apply(group(Y, g), group(Y, g), k)
                dve.wait_ge(ln_step, done[0])
                dve.tensor_tensor(group(x1, g), group(x1, g), group(Y, g), ALU.add).then_inc(x1_ready, 1)
                dve.wait_ge(x1_ready, k % NJ + 1 + (NJ if k >= 2 * NJ else 0))
                ln_stats(group(x1, g))

            for g in range(NJ):
                ln_stats(group(Y, g))
            for g in range(NJ):
                dve.wait_ge(x1_loaded[g], 64)
                residual(g, g)
            dve.wait_ge(ln_rstd, 2 * NJ)
            dve.wait_ge(post_consts, 9)
            dve.wait_ge(l1_loaded, 16 * 5)
            dve.wait_ge(small_loaded, 48)
            for c in range(DC):
                dve.tensor_scalar(l1raw[:, 4, c], l1raw[:, 4, c], wscale[:, c:c + 1], None, ALU.mult).then_inc(wscaled, 1)

            def norm_row(u, t, par):
                if not (isinstance(u, int) and u < 2):
                    dve.wait_ge(x_turned, u - 1)
                dve.tensor_scalar(xrow[:, par], x1[:, ds(t, 1)].rearrange("p a d -> p (a d)"),
                                  lnm[:, ds(t + 4 * NJ, 1), 0], lnr[:, ds(t + 4 * NJ, 1)],
                                  ALU.subtract, ALU.mult).then_inc(xrow_ready, 1)

            def top(t, par):
                dve.wait_ge(x_used, t + 1)
                dve.tensor_copy(logit[:, ds(t, 1)].rearrange("p a e -> p (a e)"),
                                mflat[par][:, 0:E]).then_inc(logit_copied, 1)

            norm_row(0, 0, 0)
            for t in range(2):
                norm_row(t + 1, t + 1, (t + 1) % 2)
                top(t, t % 2)
            with dve.Fori(1, NT // 2 - 1) as pair:
                for par in range(2):
                    norm_row(pair * 2 + (par + 1), pair * 2 + (par + 1), 1 - par)
                    top(pair * 2 + par, par)
            for t in range(NT - 2, NT):
                norm_row(t + 1, (t + 1) % NT, (t + 1) % 2)
                top(t, t % 2)
            norm_row(SHARED + 1, 1, 1)

            r = [0]

            def chain(ins):
                r[0] += 1
                ins.then_inc(route_step, 1)
                dve.wait_ge(route_step, r[0])

            def wide(a, n, axis):
                shape = [P, E, n] if axis == 2 else [P, n, E]
                return a.unsqueeze(axis).to_broadcast(shape)

            dve.wait_ge(logit_copied, NT)
            dve.tensor_reduce(toplogit, logit, AX.X, ALU.max).then_inc(top_done, 1)
            dve.wait_ge(top_done, 1)
            chain(dve.tensor_tensor(istop, logit, toplogit.unsqueeze(2).to_broadcast([P, NT, E]), ALU.is_equal))
            chain(dve.tensor_tensor(istop, istop, wide(down8, NT, 1), ALU.mult))
            chain(dve.tensor_reduce(chosen, istop, AX.X, ALU.max))
            dve.tensor_tensor(onehot, wide(down8, NT, 1), chosen.unsqueeze(2).to_broadcast([P, NT, E]),
                              ALU.is_equal).then_inc(onehot_ready, 1)
            dve.wait_ge(gate_exp, 1)
            chain(dve.tensor_scalar(gate, gate, 1.0, None, ALU.add))
            chain(dve.reciprocal(gate, gate))
            chain(dve.tensor_tensor(gate, gate, lnr[:, 4 * NJ:8 * NJ], ALU.mult))
            dve.wait_ge(onehot_ready, 1)
            dve.wait_ge(ranks_done, 2)
            chain(dve.tensor_copy(total, mflat[1][:, 0:NT * E].rearrange("p (t e) -> p e t", e=E)))
            line = "p e t -> p (e t)"
            chain(dve.tensor_tensor_scan(running.rearrange(line), resets.rearrange(line), total.rearrange(line), 0.0,
                                         ALU.mult, ALU.add))
            chain(dve.tensor_copy(count8, running[:, :, NT - 1]))
            chain(dve.tensor_tensor(running, running, total, ALU.subtract))
            ti = tiles8.bitcast(mybir.dt.int32)
            chain(dve.tensor_scalar(ti, count8, float(P - 1), None, ALU.add))
            chain(dve.tensor_scalar(ti, ti, 7, None, ALU.arith_shift_right))
            chain(dve.tensor_copy(tilesf, ti))
            chain(dve.tensor_tensor_scan(ends, ones[:, 0:E], tilesf, 0.0, ALU.mult, ALU.add))
            chain(dve.tensor_tensor(starts, ends, tilesf, ALU.subtract))
            chain(dve.tensor_scalar(starts, starts, float(P), None, ALU.mult))
            chain(dve.tensor_tensor(running, running, wide(starts, NT, 2), ALU.add))
            chain(dve.tensor_tensor(before, mflat[0][:, 0:NT * E].rearrange("p (t e) -> p t e", e=E),
                                    running.rearrange("p e t -> p t e"), ALU.add))
            chain(dve.tensor_tensor(before, before, onehot, ALU.mult))
            chain(dve.tensor_reduce(posf, before, AX.X, ALU.add))
            chain(dve.tensor_copy(posi, posf))
            for t in range(NT):
                dve.tensor_scalar(Y[:, t], x1[:, t], lnm[:, 4 * NJ + t, 0:1], gate[:, t:t + 1],
                                  ALU.subtract, ALU.mult).then_inc(xs_ready, 1)
            chain(dve.tensor_tensor(later, jobno.unsqueeze(2).to_broadcast([P, JOBS + 1, E]), wide(ends, JOBS + 1, 1),
                                    ALU.is_ge))
            chain(dve.tensor_reduce(jobe, later, AX.X, ALU.add))
            chain(dve.tensor_scalar(jobi.bitcast(mybir.dt.int32), jobe, float(E - 1), None, ALU.min))

            def hidden(n, par):
                dve.wait_ge(silu_done, n + 1)
                dve.tensor_tensor(hrow[:, par], sgate[:, par], work[2 * par + 1][:], ALU.mult).then_inc(h_ready, 1)

            hidden(0, 0)
            with dve.Fori(0, (NT - 2) // 2) as pair:
                for par in range(2):
                    n = pair * 2 + (par + 1)
                    norm_row(n + (SHARED + 1), n + 1, par)
                    hidden(n, 1 - par)
            hidden(NT - 1, 1)
            with dve.Fori(0, JOBS // 2) as pair:
                for par in range(2):
                    hidden(pair * 2 + (NT + par), par)
            hidden(NT + JOBS - 1, 0)

            dve.wait_ge(y_out, NT)
            for g in range(NJ):
                dve.wait_ge(y_gathered[g], 64)
                step(dve.tensor_tensor(group(Y, g), group(Y, g), group(shared, g), ALU.add))
                dve.wait_ge(ln_step, done[0])
                ln_stats(group(Y, g))
            for g in range(NJ):
                residual(g, 2 * NJ + g)
            for g in range(NJ):
                ln_apply(group(Y, g), group(x1, g), 3 * NJ + g, xn2_ready)

            def running_sums(b, e):
                c = 3 * (2 * b + e)
                dve.wait_ge(k_copied[e], b + 1)
                dve.wait_ge(qkv_done[e], 3 * b + 3)
                qb, kb, vbk = (work[0:3] if e == 0 else [work[3], flat[0], flat[1]])
                dve.tensor_tensor(kv[:, e], kbuf[:, e], vbk[:, 0:S], ALU.mult).then_inc(kv_step, 1)
                dve.wait_ge(kv_step, 2 * (2 * b + e) + 1)
                dve.tensor_tensor_scan(kvt[:, e], ones[:, 0:1].to_broadcast([P, S]), kv[:, e], 0.0,
                                       ALU.mult, ALU.add).then_inc(kv_step, 1)
                dve.wait_ge(kv_step, 2 * (2 * b + e) + 2)
                dve.scalar_tensor_tensor(out=vh[:, b % 2, e], in0=kvt[:, e], scalar=DENOM, in1=qb[:, 0:S],
                                         op0=ALU.mult, op1=ALU.mult).then_inc(vh_done[e], 1)

            running_sums(0, 0)
            running_sums(0, 1)
            for b in range(B):
                m = b % 2
                pair = lambda jj: mflat[jj][:, 0:2 * D].rearrange("p (x d) -> p x d", x=2)
                k = done[1]
                for x in range(NJ):
                    if x % 2 == 0:
                        dve.wait_ge(o_done, 2 * b + x // 2 + 1)
                    step(dve.bn_stats(lnst[:, x], pair(x // 2)[:, x % 2]))
                for x in range(NJ):
                    dve.wait_ge(ln_step, done[0] - 3)
                    step(dve.bn_aggr(lnm[:, 4 * k + x], lnst[:, x]))
                dve.wait_ge(ln_step, done[0])
                dve.tensor_scalar(lnv[:, 4 * k:4 * k + 4], lnm[:, 4 * k:4 * k + 4, 1], EPS, None,
                                  ALU.add).then_inc(ln_var, 1)
                done[1] += 1
                dve.wait_ge(ln_rstd, k + 1)
                for x in range(NJ):
                    dve.tensor_scalar(lnout[:, m, x], pair(x // 2)[:, x % 2], lnm[:, 4 * k + x, 0:1],
                                      lnr[:, 4 * k + x:4 * k + x + 1], ALU.subtract, ALU.mult).then_inc(o_used, 1)
                dve.wait_ge(o_used, NJ * (b + 1))
                dve.wait_ge(x2n_loaded[m], 16 * (b // 2 + 1))
                dve.tensor_tensor(x3[:, m], lnout[:, m], x2n[:, m], ALU.add).then_inc(x3_ready, 1)
                dve.wait_ge(x3_ready, b + 1)
                ln_stats(x3[:, m])
                ln_apply(xn3[:, m], x3[:, m], k + 1, xn3_ready)
                if b + 1 < B:
                    running_sums(b + 1, 0)
                    running_sums(b + 1, 1)
                for jj in range(2):
                    dve.wait_ge(f_done, 2 * b + jj + 1)
                    dve.tensor_tensor(lnout[:, m, 2 * jj:2 * jj + 2], pair(jj), bias.unsqueeze(1).to_broadcast([P, 2, D]),
                                      ALU.add).then_inc(f_used, 1)
                dve.wait_ge(f_used, 2 * b + 2)
                ln_stats(lnout[:, m])
                ln_apply(lnout[:, m], lnout[:, m], k + 2)
                dve.wait_ge(ln_step, done[0])
                if b >= 2:
                    dve.wait_ge(x4_stored[m], 16 * (b // 2))
                dve.tensor_tensor(x4[:, m], lnout[:, m], x3[:, m], ALU.add).then_inc(x4_ready, 1)

        @block.scalar
        def _(act):
            act.wait_ge(loaded_beta, 16)
            act.activation(b1, braw, ACT.Exp, scale=-1.0).then_inc(beta_e, 1)
            for b in range(B):
                for c in range(DC):
                    g = b * DC + c
                    act.wait_ge(xT_written[g % 4], g // 4 + 1)
                    act.copy(xT[:, c, b], work[g % 4][:]).then_inc(xT_copied, 1)
            act.wait_ge(consts, 12)

            def copy_out(n, name, dst):
                k = n.BANK[name]
                act.wait_ge(filled[k], n.turn(name) + 1)
                w = work[k][:]
                if len(dst.shape) == 3:
                    w = w.rearrange("p (j c) -> p j c", j=dst.shape[1])
                act.copy(dst, w).then_inc(freed[k], 1)

            def project_copies(n, b):
                for qk in range(2):
                    name = ("qk"[qk], b)
                    k = n.BANK[name]
                    act.wait_ge(filled[k], n.turn(name) + 1)
                    act.copy(raw[:, qk, b], work[k][:]).then_inc(raw_ready, 1)
                    act.activation(sigma_places(1 - n.par, b, qk), like(work[k][:], qk), ACT.Exp)\
                        .then_inc(freed[k], 1)

            def from_memory(n, i):
                o = own(i)
                for r in range(2):
                    act.wait_ge(rden_ready[r], n.count(NSEG, i + 1))
                    for bb in range(2):
                        b = 2 * r + bb
                        ins = act.activation(fromm[o, (i // 2) % 2, b], readp[r][o, bb, 0:DK], ACT.Copy,
                                             scale=rden[o, i % 2, b:b + 1])
                    ins.then_inc(fromm_ready[r], 1)

            def mem_copy(n, i):
                for r in range(2):
                    act.wait_ge(mem_written[r], n.count(NSEG, i + 2))
                    act.copy(mem[:, 2 * r:2 * r + 2, 0:MEM], memp[r][:, :, 0:MEM]).then_inc(mem_copied[r], 1)

            def body(n):
                m = 1 - n.par
                for i in range(NSEG):
                    if n.chain:
                        from_memory(n, i)
                    if n.heads_on:
                        for b in range(B):
                            if QK_AT[b] == i:
                                project_copies(n, b)
                        for b in range(B):
                            if SC_AT[b] == i:
                                copy_out(n, ("sk", b), skt[:, m, b])
                        for b in range(B):
                            if PT_AT[b] == i:
                                copy_out(n, ("PT", b), pt[:, m, b])
                    if i == 1 and n.tail:
                        act.wait_ge(xs_zeroed, 32)
                        name = ("Wo",)
                        act.wait_ge(filled[n.BANK[name]], n.turn(name) + 1)
                        g = n.first - 1 if n.loop is None else n.first - 1 + 2 * n.loop
                        ins = act.copy(Y[:, ds(g, 1), :].rearrange("p a d -> p (a d)"), work[n.BANK[name]][:, 0:D])
                        ins.then_inc(freed[n.BANK[name]], 1)
                    if i == 0 and n.tail:
                        copy_out(n, ("attT", NJ - 1), attT[:, :, NJ - 1])
                    elif i and i % 2 == 0 and n.chain:
                        j = (i - 2) // 2
                        copy_out(n, ("attT", j), attT[:, :, j])
                    for b in range(B):
                        if n.heads_on and SC_AT[b] == i:
                            act.wait_ge(score_shifted, n.count(B, B + b + 1))
                            for half in range(2):
                                o = slice(SEG * half, SEG * half + SEG)
                                ins = act.activation(pbd[o, b, :, SEG * half:SEG * half + SEG], sm[o, b % 2], ACT.Exp,
                                                     scale=SCALE)
                            ins.then_inc(probs_ready, 1)
                    if n.chain and (i < NSEG - 1 or n.heads_on):
                        mem_copy(n, i)
                if n.first == -1:
                    mem_copy(n, NSEG - 1)

            bodies(act, body)
            act.copy(rowmax[:, 0], rowmax[:, 1]).then_inc(attn_done, 1)

            act.wait_ge(attn_done, 1)
            for w in range(5):
                act.wait_ge(l1_turned, w + 1)
                to = wqkvT[:, w] if w < 3 else wofT[:, w - 3]
                act.copy(to.rearrange("p c d -> p (c d)"), work[w % 4][:]).then_inc(l1_copied, 1)
            act.wait_ge(l1_turned, 6)
            act.copy(rwT.rearrange("p c e -> p (c e)"), work[1][:, 0:DC * E]).then_inc(l1_copied, 1)

            def row_turned(u, par):
                act.wait_ge(x_turned, u + 1)
                if not (isinstance(u, int) and u < 2):
                    act.wait_ge(x_used, u - 1)
                act.copy(xj[:, par], flat[par][:, 0:D]).then_inc(xj_copied, 1)

            for u in range(2):
                row_turned(u, u % 2)
            with act.Fori(1, NT // 2) as pair:
                for par in range(2):
                    row_turned(pair * 2 + par, par)
            row_turned(SHARED, 0)
            act.wait_ge(top_done, 1)
            act.activation(gate, toplogit, ACT.Exp, scale=-1.0).then_inc(gate_exp, 1)

            def silu(n, par):
                act.wait_ge(x_used, n + NT + 1)
                act.activation(sgate[:, par], work[2 * par][:], ACT.Silu).then_inc(silu_done, 1)

            def turned_hidden(n, par):
                act.wait_ge(hT_turned, n + 1)
                act.copy(hcol[:, par], mflat[0][:, 0:F]).then_inc(hT_copied, 1)

            def give_shared(n):
                act.wait_ge(down_done, n + 1)
                act.copy(shared[:, ds(n, 1)].rearrange("p a d -> p (a d)"), mflat[1][:, 0:D]).then_inc(y_out, 1)

            row_turned(SHARED + 1, 1)
            silu(0, 0)
            with act.Fori(0, (NT - 2) // 2) as pair:
                for par in range(2):
                    n = pair * 2 + (par + 1)
                    turned_hidden(n - 1, par)
                    silu(n, 1 - par)
                    give_shared(n - 1)
                    row_turned(n + (SHARED + 1), par)
            turned_hidden(NT - 2, 0)
            silu(NT - 1, 1)
            give_shared(NT - 2)
            turned_hidden(NT - 1, 1)
            give_shared(NT - 1)
            row_turned(ROUTED, 0)
            row_turned(ROUTED + 1, 1)
            silu(NT, 0)
            def routed_tile(pair, par):
                n = pair * 2 + (NT + par + 1)
                turned_hidden(n - 1, par)
                silu(n, 1 - par)
                act.wait_ge(down_done, n)
                if not isinstance(pair, int):
                    act.wait_ge(y_stored[par], pair * 16)
                act.copy(yj[:, par], mflat[1][:, 0:D]).then_inc(y_out, 1)
                row_turned(n + (SHARED + 1), par)

            for par in range(2):
                routed_tile(0, par)
            with act.Fori(1, (JOBS - 1) // 2 - 1) as pair:
                for par in range(2):
                    routed_tile(pair, par)
            for j in range(JOBS - 2, JOBS + 1):
                n = NT + j
                par = (j - 1) % 2
                turned_hidden(n - 1, par)
                if j < JOBS:
                    silu(n, 1 - par)
                act.wait_ge(down_done, n)
                act.wait_ge(y_stored[par], 16 * ((j - 1) // 2))
                act.copy(yj[:, par], mflat[1][:, 0:D]).then_inc(y_out, 1)
                if j + 1 < JOBS:
                    row_turned(n + SHARED + 1, par)

            x2T_v = x2T.rearrange("p c (g t r) -> p t c g r", t=NT, r=4)
            for t in range(NT):
                act.wait_ge(x2_turned, t + 1)
                act.copy(x2T_v[:, t], flat[t % 2][:, 0:D].rearrange("p (c g r) -> p c g r", c=DC, r=4))\
                    .then_inc(x2T_copied, 1)

            def keys(b, e):
                act.wait_ge(qkv_done[e], 3 * b + 1)
                act.copy(kbuf[:, e], (work[1] if e == 0 else flat[0])[:, 0:S]).then_inc(k_copied[e], 1)

            keys(0, 0)
            keys(0, 1)
            for b in range(B):
                if b + 1 < B:
                    keys(b + 1, 0)
                for jj in range(2):
                    act.wait_ge(t3_done, 2 * b + jj + 1)
                    act.copy(x3T[:, b % 2, 2 * jj:2 * jj + 2].rearrange("p j d -> p (j d)"),
                             mflat[jj][:, 0:2 * D]).then_inc(x3T_copied, 1)
                if b + 1 < B:
                    keys(b + 1, 1)

        @block.tensor
        def _(pe):
            pe.wait_ge(consts, 12)
            for b in range(B):
                pe.wait_ge(x_normed, NJ * (b + 1))
                for c in range(DC):
                    g = b * DC + c
                    if g >= 4:
                        pe.wait_ge(xT_copied, g - 3)
                    for j in range(NJ):
                        ins = pe.transpose(work[g % 4][:, j * P:(j + 1) * P], xnorm[:, b, j, c * P:(c + 1) * P], ident[:])
                    ins.then_inc(xT_written[g % 4], 1)
            pe.wait_ge(xT_copied, DC * B)

            def into(n, name, back=0):
                k = n.BANK[name]
                v = n.turn(name, back)
                if not (isinstance(v, int) and v == 0):
                    pe.wait_ge(freed[k], v)
                return work[k], filled[k]

            def consumed(n, name, back=0):
                k = n.BANK[name]
                pe.wait_ge(freed[k], n.turn(name, back) + 1)

            def project_qk(n, b):
                m = 1 - n.par
                for qk in range(2):
                    w, done = into(n, ("qk"[qk], b))
                    if b == 0 and qk == 0:
                        pe.wait_ge(w_loaded[m], weights_count(n))
                    for c in range(DC):
                        ins = pe.matmul(w[:], wqkv[:, m, qk, c], xT[:, c, b], start=(c == 0), stop=(c == DC - 1))
                    ins.then_inc(done, 1)

            def weights_count(n):
                k = (n.first + 1) // 2 + 1
                return 48 * k if n.loop is None else 48 * k + 48 * n.loop

            def project_v(n, b):
                m = 1 - n.par
                w, done = into(n, ("V", b))
                for j in range(NJ):
                    for c in range(DC):
                        ins = pe.matmul(w[:, j * P:(j + 1) * P], xT[:, c, b, j * P:(j + 1) * P], wqkv[:, m, 2, c],
                                        start=(c == 0), stop=(c == DC - 1))
                ins.then_inc(done, 1)

            def turn_keys(n, b):
                m = 1 - n.par
                pe.wait_ge(sigma_done, n.count(2 * B, 2 * B + 2 * b + 2))
                w, done = into(n, ("sk", b))
                pairs = sqk[:, m, b].rearrange("p s c -> p (s c)").rearrange("p (j x) -> p j x", j=NJ)
                for j in range(NJ):
                    ins = pe.transpose(w[:, j * P:(j + 1) * P], pairs[:, j, SEG:3 * SEG], ident[:])
                ins.then_inc(done, 1)

            def scores(n, b):
                consumed(n, ("k", b))
                w, done = into(n, ("sc", b))
                for i in range(NSEG):
                    c = slice(i * SEG, (i + 1) * SEG)
                    ins = pe.matmul(w[own(i), (i // 2) * SEG:(i // 2 + 1) * SEG], raw[:, 0, b, c], raw[:, 1, b, c],
                                    start=True, stop=True)
                ins.then_inc(done, 1)

            def turn_probs(n, b):
                pe.wait_ge(probs_ready, n.count(B, B + b + 1))
                w, done = into(n, ("PT", b))
                for j in range(NJ):
                    ins = pe.transpose(w[:, j * P:(j + 1) * P], pbd[:, b, j], ident[:])
                    if b == B - 1 and j == 0:
                        ins.then_inc(proj_done, 1)
                ins.then_inc(done, 1)

            def probs_values(n, j):
                w, done = into(n, ("PV", j))
                for b in range(B):
                    ins = pe.matmul(w[:, b * P:(b + 1) * P], pt[:, n.par, b, j], v1[:, n.par, b, j], start=True, stop=True)
                ins.then_inc(done, 1)

            def turn_att(n, j, back):
                pe.wait_ge(att_ready, n.count(NJ, j + 1 - NJ * back))
                consumed(n, ("PV", j), back)
                w, done = into(n, ("attT", j))
                for b in range(B):
                    ins = pe.transpose(w[:, b * P:(b + 1) * P], fromm[:, j % 2, b], ident[:])
                ins.then_inc(done, 1)

            def project_out(n):
                consumed(n, ("attT", NJ - 1))
                if n.first == 1:
                    pe.wait_ge(wo_loaded, 16)
                w, done = into(n, ("Wo",))
                tokens = attT.rearrange("p b j (r c) -> p c (b j r)", c=H)
                for c in range(H):
                    ins = pe.matmul(w[:, 0:D], tokens[:, c], wo[:, c], start=(c == 0), stop=(c == H - 1))
                ins.then_inc(done, 1)

            def seed():
                for r in range(2):
                    pe.matmul(memp[r][:, :, 0:MEM], seed_l[:], seed_r[:], start=True, stop=False,
                              skip_group_check=True).then_inc(mem_written[r], 1)

            def read_memories(n, i):
                for r in range(2):
                    pe.wait_ge(mem_copied[r], n.count(NSEG, i + 1))
                    if not (n.first == 0 and i == 0):
                        pe.wait_ge(fromm_ready[r], n.count(NSEG, i))
                    for bb in range(2):
                        b = 2 * r + bb
                        ins = pe.matmul(readp[r][:, bb, 0:MEM], sqk[:, n.par, b, i], mem[:, b, 0:MEM],
                                        start=True, stop=True)
                    ins.then_inc(read_done[r], 1)

            def update_memories(n, i):
                for r in range(2):
                    pe.wait_ge(delta_ready[r], n.count(NSEG - 1, i + 1))
                    for bb in range(2):
                        b = 2 * r + bb
                        ins = pe.matmul(memp[r][:, bb, 0:MEM], skt[own(i), n.par, b, i // 2], delta[own(i), b, 0:MEM],
                                        start=False, stop=False, skip_group_check=True)
                    ins.then_inc(mem_written[r], 1)

            def body(n):
                for i in range(NSEG):
                    if n.chain:
                        read_memories(n, i)
                    if n.heads_on:
                        for b in range(B):
                            if QK_AT[b] == i:
                                project_qk(n, b)
                        for b in range(B):
                            if SC_AT[b] == i:
                                turn_keys(n, b)
                                scores(n, b)
                        for b in range(B):
                            if V_AT[b] == i:
                                project_v(n, b)
                        for b in range(B):
                            if PT_AT[b] == i:
                                turn_probs(n, b)
                    if i == 1 and n.tail:
                        project_out(n)
                    if i == 0 and n.tail:
                        turn_att(n, NJ - 1, 1)
                    elif i and i % 2 == 0 and n.chain:
                        turn_att(n, (i - 2) // 2, 0)
                    if n.chain and i < NSEG - 1:
                        update_memories(n, i)
                    elif i == NSEG - 1 and n.heads_on:
                        seed()
                    if i % 2 and n.chain:
                        probs_values(n, (i - 1) // 2)

            bodies(pe, body)

            pe.wait_ge(attn_done, 1)
            pe.wait_ge(l1_loaded, 16 * 5)
            for w in range(5):
                if w == 4:
                    pe.wait_ge(wscaled, DC)
                    pe.wait_ge(l1_copied, 1)
                for c in range(DC):
                    for r in range(DC):
                        ins = pe.transpose(work[w % 4][:, c * D + r * P:c * D + (r + 1) * P],
                                           l1raw[:, w, r, c * P:(c + 1) * P], ident[:])
                ins.then_inc(l1_turned, 1)
            pe.wait_ge(small_loaded, 48)
            pe.wait_ge(l1_copied, 2)
            for c in range(DC):
                ins = pe.transpose(work[1][:, c * E:(c + 1) * E], rwraw[0:E, c * P:(c + 1) * P], ident[0:E, 0:E])
            ins.then_inc(l1_turned, 1)
            pe.wait_ge(l1_copied, 6)

            def turn_row(u, par):
                if not (isinstance(u, int) and u < 2):
                    pe.wait_ge(xj_copied, u - 1)
                for c in range(DC):
                    ins = pe.transpose(flat[par][:, c * P:(c + 1) * P], xrow[:, par, c * P:(c + 1) * P], ident[:])
                ins.then_inc(x_turned, 1)

            def turn_norm(u, par):
                pe.wait_ge(xrow_ready, u + 1)
                turn_row(u, par)

            def logits(t, par):
                pe.wait_ge(xj_copied, t + 1)
                if not (isinstance(t, int) and t < 2):
                    pe.wait_ge(logit_copied, t - 1)
                for c in range(DC):
                    ins = pe.matmul(mflat[par][:, 0:E], xj[:, par, c * P:(c + 1) * P], rwT[:, c], start=(c == 0),
                                    stop=(c == DC - 1))
                ins.then_inc(x_used, 1)

            turn_norm(0, 0)
            for t in range(2):
                turn_norm(t + 1, (t + 1) % 2)
                logits(t, t % 2)
            with pe.Fori(1, NT // 2 - 1) as pair:
                for par in range(2):
                    turn_norm(pair * 2 + (par + 1), 1 - par)
                    logits(pair * 2 + par, par)
            for t in range(NT - 2, NT):
                turn_norm(t + 1, (t + 1) % 2)
                logits(t, t % 2)

            def gate_up(n, par, e):
                pe.wait_ge(xj_copied, n + NT + 1)
                if not (isinstance(n, int) and n < 2):
                    pe.wait_ge(h_ready, n - 1)
                for half in range(2):
                    for c in range(DC):
                        ins = pe.matmul(work[2 * par + half][:], xj[:, par, c * P:(c + 1) * P],
                                        wgu[:, e, c, half * F:(half + 1) * F] if isinstance(e, int) else
                                        wgu_flat[:, ds(e * (DC * 2 * F) + (c * 2 * F + half * F), F)],
                                        start=(c == 0), stop=(c == DC - 1))
                ins.then_inc(x_used, 1)

            def turn_hidden(n, par):
                pe.wait_ge(h_ready, n + 1)
                if not (isinstance(n, int) and n == 0):
                    pe.wait_ge(hT_copied, n)
                for k in range(FC):
                    ins = pe.transpose(mflat[0][:, k * P:(k + 1) * P], hrow[:, par, k * P:(k + 1) * P], ident[:])
                ins.then_inc(hT_turned, 1)

            def down(n, par, e):
                pe.wait_ge(hT_copied, n + 1)
                if not (isinstance(n, int) and n == 0):
                    pe.wait_ge(y_out, n)
                for k in range(FC):
                    ins = pe.matmul(mflat[1][:, 0:D], hcol[:, par, k * P:(k + 1) * P],
                                    wdn[:, e, k] if isinstance(e, int) else
                                    wdn_flat[:, ds(e * (FC * D) + k * D, D)],
                                    start=(k == 0), stop=(k == FC - 1))
                ins.then_inc(down_done, 1)

            wgu_flat = wgu.rearrange("p e c n -> p (e c n)")
            wdn_flat = wdn.rearrange("p e k n -> p (e k n)")
            pe.wait_ge(shared_loaded, 32)
            gate_up(0, 0, E)
            turn_norm(SHARED + 1, 1)
            pe.wait_ge(onehot_ready, 1)
            pe.wait_ge(post_consts, 9)
            hot = onehot.rearrange("p t e -> p (t e)")
            pe.matmul(mflat[0][:, 0:NT * E], tri, hot, start=True, stop=True).then_inc(ranks_done, 1)
            pe.matmul(mflat[1][:, 0:NT * E], ones, hot, start=True, stop=True).then_inc(ranks_done, 1)
            pe.wait_ge(xs_ready, 1)
            def shared_tile(n, par):
                turn_hidden(n - 1, par)
                gate_up(n, 1 - par, E)
                down(n - 1, par, E)
                turn_norm(n + (SHARED + 1), par)

            for par in range(2):
                shared_tile(par + 1, par)
            with pe.Fori(1, (NT - 2) // 2) as pair:
                for par in range(2):
                    shared_tile(pair * 2 + (par + 1), par)
            turn_hidden(NT - 2, 0)
            gate_up(NT - 1, 1, E)
            down(NT - 2, 0, E)
            turn_hidden(NT - 1, 1)
            down(NT - 1, 1, E)

            pe.wait_ge(experts_loaded, 32 * E)
            jobi_i = jobi.bitcast(mybir.dt.int32)

            def expert(j):
                return pe.value_load(jobi_i[0:1, ds(j, 1)], min_val=0, max_val=E - 1)

            def turn_sorted(j, par):
                pe.wait_ge(xs_loaded[par], loads(j))
                turn_row(j + ROUTED, par)

            loads = lambda j: 16 * (j // 2 + 1)
            turn_sorted(0, 0)
            turn_sorted(1, 1)
            gate_up(NT, 0, expert(0))
            with pe.Fori(0, (JOBS - 1) // 2 - 1) as pair:
                for par in range(2):
                    j = pair * 2 + (par + 1)
                    turn_hidden(j + (NT - 1), par)
                    gate_up(j + NT, 1 - par, expert(j))
                    down(j + (NT - 1), par, expert(j - 1))
                    pe.wait_ge(xs_loaded[par], pair * 16 + 32)
                    turn_row(j + (ROUTED + 1), par)
            for j in range(JOBS - 2, JOBS + 1):
                par = (j - 1) % 2
                turn_hidden(j + NT - 1, par)
                if j < JOBS:
                    gate_up(j + NT, 1 - par, expert(j))
                down(j + NT - 1, par, expert(j - 1))
                if j + 1 < JOBS:
                    turn_sorted(j + 1, par)

            pe.wait_ge(xj_copied, 2 * NT + JOBS)
            for t in range(NT):
                pe.wait_ge(xn2_ready, t + 1)
                if t >= 2:
                    pe.wait_ge(x2T_copied, t - 1)
                for c in range(DC):
                    ins = pe.transpose(flat[t % 2][:, c * P:(c + 1) * P], Y[:, t, c * P:(c + 1) * P], ident[:])
                ins.then_inc(x2_turned, 1)

            def project(b, e):
                banks = [work[0], work[1], work[2]] if e == 0 else [work[3], flat[0], flat[1]]
                if b:
                    pe.wait_ge(vh_done[e], b)
                for w in (1, 2, 0):
                    for c in range(DC):
                        ins = pe.matmul(banks[w][:, 0:S], wqkvT[:, w, c, e * P:(e + 1) * P],
                                        x2T[:, c, b * S:(b + 1) * S], start=(c == 0), stop=(c == DC - 1))
                    ins.then_inc(qkv_done[e], 1)

            pe.wait_ge(x2T_copied, NT)
            project(0, 0)
            project(0, 1)
            pe.wait_ge(y_out, NT + JOBS)
            for b in range(B):
                m = b % 2
                for e in range(2):
                    pe.wait_ge(vh_done[e], b + 1)
                for jj in range(2):
                    if b:
                        pe.wait_ge(f_used, 2 * b)
                    for x in range(2):
                        for e in range(2):
                            j = 2 * jj + x
                            ins = pe.matmul(mflat[jj][:, x * D:(x + 1) * D], vh[:, m, e, j * P:(j + 1) * P], wofT[:, 0, e],
                                            start=(e == 0), stop=(e == 1))
                    ins.then_inc(o_done, 1)
                if b + 1 < B:
                    project(b + 1, 0)
                for jj in range(2):
                    pe.wait_ge(xn3_ready, NJ * b + 2 * jj + 2)
                    pe.wait_ge(o_used, NJ * b + 2 * jj + 2)
                    for x in range(2):
                        for c in range(DC):
                            ins = pe.transpose(mflat[jj][:, (x * DC + c) * P:(x * DC + c + 1) * P],
                                               xn3[:, m, 2 * jj + x, c * P:(c + 1) * P], ident[:])
                    ins.then_inc(t3_done, 1)
                if b + 1 < B:
                    project(b + 1, 1)
                for jj in range(2):
                    pe.wait_ge(x3T_copied, 2 * b + jj + 1)
                    for x in range(2):
                        for c in range(DC):
                            ins = pe.matmul(mflat[jj][:, x * D:(x + 1) * D], x3T[:, m, 2 * jj + x, c * P:(c + 1) * P],
                                            wofT[:, 1, c], start=(c == 0), stop=(c == DC - 1))
                    ins.then_inc(f_done, 1)


_INS = ["L0_attn_x", "L0_attn_Wq", "L0_attn_Wk", "L0_attn_Wv", "L0_attn_Wo", "L0_attn_betas", "L0_ffn_router_w",
        "L0_ffn_w_gate_up", "L0_ffn_w_down", "L0_ffn_shared_gate_up", "L0_ffn_shared_down", "L1_attn_Wq",
        "L1_attn_Wk", "L1_attn_Wv", "L1_attn_Wo", "L1_ffn_weight", "L1_ffn_scale_weight", "L1_ffn_bias"]
_OUTS = [((B, S, D), "float32")]


def kernel(**inputs):
    import numpy as _np
    import concourse.bacc as _bacc
    from concourse import mybir as _mybir
    from concourse.bass_utils import run_bass_kernel_spmd as _run

    nc = _bacc.Bacc("TRN2", target_bir_lowering=False, num_devices=1)
    arrays, dram = {}, {}
    for name in _INS:
        a = _np.ascontiguousarray(inputs[name])
        arrays[f"in_{name}_dram"] = a
        dram[name] = nc.dram_tensor(f"in_{name}_dram", a.shape, _mybir.dt.from_np(a.dtype), kind="ExternalInput").ap()
    (shape, dtype), = _OUTS
    out = nc.dram_tensor("out_0_dram", shape, _mybir.dt.from_np(_np.dtype(dtype)), kind="ExternalOutput").ap()
    sandwich(nc, dram, out)
    return _run(nc, [arrays], core_ids=[0]).results[0]["out_0_dram"]
```

```python
from contextlib import ExitStack

import concourse.bass as bass
from concourse import mybir

P = 128
B, S, D = 4, 512, 256
H, DK, SEG = 16, 128, 64
NSEG = S // SEG
NJ = S // P
NT = B * NJ
DC = D // P
MEM = DK + 1
EPS = 1e-5
E, F = 8, 512
FC = F // P
JOBS = NT + E - 1
EARLY = NT // 2
LATE = EARLY + JOBS
NJOBS = NT + JOBS
LNS = 4 * NJ + 3 * B
DENOM = float(D) ** 0.5 / S
SCALE = float(DK) ** -0.5
MASKED = -1e30

ALU = mybir.AluOpType
ACT = mybir.ActivationFunctionType
AX = mybir.AxisListType
F32 = mybir.dt.float32
ds = bass.ds


QK_AT = [0, 2, 3, 4]
SC_AT = [1, 3, 4, 5]
V_AT = [5, 5, 6, 6]
PT_AT = [3, 5, 6, 7]
SUM_AT = [2, 4, 5, 6]


def plan_banks():
    full = []
    for i in range(NSEG):
        for b in range(B):
            if QK_AT[b] == i:
                full += [("q", b), ("k", b)]
        for b in range(B):
            if SC_AT[b] == i:
                full += [("sk", b), ("sc", b)]
        full += [("V", b) for b in range(B) if V_AT[b] == i]
        full += [("PT", b) for b in range(B) if PT_AT[b] == i]
        if i == 1:
            full += [("Wo",)]
        if i % 2:
            full += [("PV", (i - 1) // 2)]
        else:
            full += [("attT", (i - 2) // 2 if i else NJ - 1)]
    used, turn, bank = [0] * 4, {}, {}
    for n in range(-1, H + 1):
        for at, name in enumerate(full):
            kind = name[0]
            if kind in ("q", "k", "sk", "sc", "V", "PT"):
                there = n + 1 < H
            elif kind == "Wo" or name == ("attT", NJ - 1):
                there = n >= 1
            else:
                there = 0 <= n < H
            if there:
                bank[name] = at % 4
                turn[n, name] = used[at % 4]
                used[at % 4] += 1
    return bank, turn, [sum(at % 4 == k for at in range(len(full))) for k in range(4)]


class Body:
    BANK, TURN, USES = plan_banks()

    def __init__(self, first, loop=None):
        self.first, self.loop = first, loop
        self.par = first % 2
        self.chain = loop is not None or 0 <= first < H
        self.heads_on = loop is not None or first + 1 < H
        self.tail = loop is not None or first >= 1

    def count(self, per_body, c=0):
        v = per_body * self.first + c
        return v if self.loop is None else v + 2 * per_body * self.loop

    def turn(self, name, back=0):
        v = self.TURN[self.first - back, name]
        if self.loop is None:
            return v
        uses = self.USES[self.BANK[name]]
        assert v + uses == self.TURN[self.first - back + 1, name]
        return v + 2 * uses * self.loop


def sandwich(nc, dram, out):
    with ExitStack() as ctx:
        def sb(name, shape, dt=F32):
            return ctx.enter_context(nc.sbuf_tensor(name, shape, dt))

        def sem(name):
            return ctx.enter_context(nc.semaphore(name))

        def sems(name, n):
            return [sem(f"{name}{i}") for i in range(n)]

        work = [ctx.enter_context(nc.psum_tensor(f"work{i}", [P, 512], F32)) for i in range(4)]
        readp = [ctx.enter_context(nc.psum_tensor(f"readp{i}", [P, 2, 256], F32)) for i in range(2)]
        memp = [ctx.enter_context(nc.psum_tensor(f"memp{i}", [P, 2, 256], F32)) for i in range(2)]

        ident = sb("ident", [P, P])
        mask = sb("mask", [P, SEG])
        seed_l = sb("seed_l", [P, P])
        seed_r = sb("seed_r", [P, 2, MEM])
        stats = sb("stats", [P, NT, 6])
        mv = sb("mv", [P, NT, 2])
        vareps = sb("vareps", [P, NT])
        rstd = sb("rstd", [P, NT])
        minushalf = sb("minushalf", [P, NJ])
        rden = sb("rden", [P, 2, B])
        rowmax = sb("rowmax", [P, 2, NJ])
        rowsum = sb("rowsum", [P, B, NJ])
        rinv = sb("rinv", [P, 2, B, NJ])
        wqkv = sb("wqkv", [P, 2, 3, DC, DK])
        mem = sb("mem", [P, B, MEM + 1])
        delta = sb("delta", [P, B, MEM + 1])
        Y = sb("Y", [P, H, D])
        arena = sb("arena", [P, 45568])
        at = [0]

        def carve(*shape):
            n = 1
            for x in shape:
                n *= x
            v = arena[:, at[0]:at[0] + n]
            at[0] += n
            assert at[0] <= 45568
            if len(shape) == 1:
                return v
            names = "abcd"[:len(shape)]
            return v.rearrange(f"p ({' '.join(names)}) -> p {' '.join(names)}", **dict(zip(names, shape)))

        xT = carve(DC, B, S)
        raw = carve(2, B, S)
        plus1 = carve(2, S)
        sqk = carve(2, B, NSEG, P)
        skt = carve(2, B, NJ, P)
        vb = carve(2, B, NJ, P)
        v1 = carve(2, B, NJ, P)
        pt = carve(2, B, NJ, P)
        pbd = carve(B, NJ, P)
        sm = carve(2, NJ, SEG)
        fromm = carve(2, B, P)
        attT = carve(B, NJ, P)
        bB = carve(H * P)
        wo = carve(H, D)
        xin = sqk[:, 1].rearrange("p b s c -> p (b s c)").rearrange("p (b j d) -> p b j d", b=B, j=NJ)
        xnorm = raw.rearrange("p a b s -> p (a b s)").rearrange("p (b j d) -> p b j d", b=B, j=NJ)
        braw = skt[:, 1].rearrange("p b j c -> p (b j c)")
        b1 = vb[:, 1].rearrange("p b j c -> p (b j c)")


        at[0] = 0
        x1 = carve(NT, D)
        wgu = carve(E + 1, DC, 2 * F)
        wdn = carve(E + 1, FC, D)
        shared = carve(NT, D)
        xrow = carve(2, D)
        xj = carve(2, D)
        hrow = carve(2, F)
        sgate = carve(2, F)
        hcol = carve(2, F)
        yj = carve(2, D)
        tri = carve(P)
        ones = carve(P)
        rwT = carve(DC, E)
        rwraw = carve(D)
        onehot = carve(NT, E)
        down8 = carve(E)
        logit = carve(NT, E)
        istop = carve(NT, E)
        toplogit = carve(NT)
        chosen = carve(NT)
        gate = carve(NT)
        before = carve(NT, E)
        total = carve(E, NT)
        running = carve(E, NT)
        resets = carve(E, NT)
        count8 = carve(E)
        tiles8 = carve(E)
        tilesf = carve(E)
        ends = carve(E)
        starts = carve(E)
        posf = carve(NT)
        pos = carve(NT)
        jobno = carve(JOBS + 1)
        later = carve(JOBS + 1, E)
        jobe = carve(JOBS + 1)
        jobi = carve(JOBS + 1)
        lnst = carve(4, 6)
        lnm = carve(LNS * 4, 2)
        lnv = carve(LNS * 4)
        lnr = carve(LNS * 4)
        wqkvT = wqkv[:].rearrange("p a b c d -> p (a b c d)").rearrange("p (w c d) -> p w c d", w=3, c=DC)
        wofT = carve(2, DC, D)
        bias = carve(D)
        wscale = carve(DC)
        l1raw = shared.rearrange("p t d -> p (t d)")[:, 0:5 * DC * D].rearrange("p (w c d) -> p w c d", w=5, c=DC)
        at[0] = NT * D
        x2T = carve(DC, B * S)
        x2n = carve(2, NJ, D)
        x3 = carve(2, NJ, D)
        xn3 = carve(2, NJ, D)
        x3T = carve(2, NJ, D)
        kbuf = carve(2, S)
        kv = carve(2, S)
        kvt = carve(2, S)
        vh = carve(2, DC, S)
        lnout = carve(2, NJ, D)
        x4 = carve(2, NJ, D)
        xs_d = nc.dram_tensor("rows_by_expert", [JOBS * P, D], F32).ap()
        ys_d = nc.dram_tensor("outputs_by_expert", [JOBS * P, D], F32).ap()
        x2_d = nc.dram_tensor("residual", [B * S, D], F32).ap()

        loaded_x = sems("loaded_x", B)
        loaded_beta = sem("loaded_beta")
        consts = sem("consts")
        beta_e = sem("beta_e")
        beta_step = sem("beta_step")
        x_stats = sem("x_stats")
        x_var = sem("x_var")
        x_rstd = sem("x_rstd")
        x_normed = sem("x_normed")
        xT_written = sems("xT_written", 4)
        xT_copied = sem("xT_copied")
        w_loaded = sems("w_loaded", 2)
        wo_loaded = sem("wo_loaded")
        vb_ready = sem("vb_ready")
        filled = sems("filled", 4)
        freed = sems("freed", 4)
        proj_done = sem("proj_done")
        raw_ready = sem("raw_ready")
        plus1_done = sem("plus1_done")
        sigma_done = sem("sigma_done")
        score_masked = sem("score_masked")
        max_ready = sem("max_ready")
        score_shifted = sem("score_shifted")
        probs_ready = sem("probs_ready")
        sum_ready = sem("sum_ready")
        rinv_ready = sem("rinv_ready")
        mem_written = sems("mem_written", 2)
        mem_copied = sems("mem_copied", 2)
        read_done = sems("read_done", 2)
        rden_ready = sems("rden_ready", 2)
        fromm_ready = sems("fromm_ready", 2)
        delta_ready = sems("delta_ready", 2)
        att_ready = sem("att_ready")
        attn_done = sem("attn_done")

        x_v = dram["L0_attn_x"].rearrange("b (j p) d -> b p j d", p=P)
        w_v = [dram[f"L0_attn_W{c}"].rearrange("(c p) n -> p c n", p=P) for c in "qkv"]
        wo_v = dram["L0_attn_Wo"].rearrange("(c p) n -> p c n", p=P)
        beta_v = dram["L0_attn_betas"].rearrange("a h b d -> (a h b) d").rearrange("h d -> (h d)")

        xs_zeroed = sem("xs_zeroed")
        small_loaded = sem("small_loaded")
        l1_loaded = sem("l1_loaded")
        shared_loaded = sem("shared_loaded")
        experts_loaded = sem("experts_loaded")
        post_consts = sem("post_consts")
        ln_step = sem("ln_step")
        ln_var = sem("ln_var")
        ln_rstd = sem("ln_rstd")
        x1_ready = sem("x1_ready")
        l1_turned = sem("l1_turned")
        l1_copied = sem("l1_copied")
        wscaled = sem("wscaled")
        xrow_ready = sem("xrow_ready")
        x_turned = sem("x_turned")
        xj_copied = sem("xj_copied")
        x_used = sem("x_used")
        logit_copied = sem("logit_copied")
        top_done = sem("top_done")
        gate_exp = sem("gate_exp")
        route_step = sem("route_step")
        onehot_ready = sem("onehot_ready")
        ranks_done = sem("ranks_done")
        xs_ready = sem("xs_ready")
        xs_scattered = sem("xs_scattered")
        silu_done = sem("silu_done")
        h_ready = sem("h_ready")
        hT_turned = sem("hT_turned")
        hT_copied = sem("hT_copied")
        down_done = sem("down_done")
        y_out = sem("y_out")
        x2_stored = sem("x2_stored")
        xn2_ready = sem("xn2_ready")
        x2_turned = sem("x2_turned")
        x2T_copied = sem("x2T_copied")
        o_done = sem("o_done")
        o_used = sem("o_used")
        x3_ready = sem("x3_ready")
        xn3_ready = sem("xn3_ready")
        t3_done = sem("t3_done")
        x3T_copied = sem("x3T_copied")
        f_done = sem("f_done")
        f_used = sem("f_used")
        x4_ready = sem("x4_ready")
        kv_step = sem("kv_step")
        x1_loaded = sems("x1_loaded", NJ)
        xs_loaded = sems("xs_loaded", 2)
        y_stored = sems("y_stored", 2)
        y_gathered = sems("y_gathered", NT // 2)
        x2n_loaded = sems("x2n_loaded", 2)
        k_copied = sems("k_copied", 2)
        qkv_done = sems("qkv_done", 2)
        vh_done = sems("vh_done", 2)
        x4_stored = sems("x4_stored", 2)

        by_head = "b (i h r) d -> h (b i) r d"
        x_h = dram["L0_attn_x"].rearrange(by_head, h=H, r=4)
        x2_h = x2_d.rearrange("(g h r) d -> h g r d", h=H, r=4)
        flat = [readp[r][:].rearrange("p a c -> p (a c)") for r in range(2)]
        mflat = [memp[r][:].rearrange("p a c -> p (a c)") for r in range(2)]
        posi = pos.bitcast(mybir.dt.uint32)
        SHARED, ROUTED = NT, NT + EARLY

        X2_LAG = 4

        def late_groups():
            for i in range(NT // 2 + 1):
                if i:
                    yield "x2", i - 1
                if i < NT // 2:
                    yield "moe", i

        def slot(kind, p):
            return {"moe": 2 * NT, "x2": 3 * NT}[kind] + 2 * p

        block = ctx.enter_context(nc.Block())

        def own(i):
            return slice(SEG * (i % 2), SEG * (i % 2) + SEG)

        def sigma_places(m, b, qk):
            pairs = sqk[:, m, b].rearrange("p s c -> p (s c)").rearrange("p (j x) -> p j x", j=NJ)
            if qk:
                return pairs[:, :, SEG:3 * SEG]
            return pairs.rearrange("p j (a c) -> p j a c", a=4)[:, :, 0:4:3]

        def like(x, qk):
            x = x.rearrange("p (j x) -> p j x", j=NJ)
            return x if qk else x.rearrange("p j (a c) -> p j a c", a=2)

        def bodies(eng, body):
            body(Body(-1))
            body(Body(0))
            with eng.Fori(0, (H - 2) // 2) as turn:
                body(Body(1, turn))
                body(Body(2, turn))
            body(Body(H - 1))
            body(Body(H))

        @block.sync
        def _(sp):
            for b in range(B):
                sp.dma_start(xin[:, b], x_v[b]).then_inc(loaded_x[b], 16)
            sp.wait_ge(consts, 12)
            xs_t = xs_d.rearrange("(t p) d -> p t d", p=P)
            sp.dma_start(xs_t[:, 0:NT], Y[:]).then_inc(xs_zeroed, 16)
            sp.dma_start(xs_t[:, NT:JOBS], Y[:, 0:JOBS - NT]).then_inc(xs_zeroed, 16)
            sp.dma_start(braw, beta_v.partition_broadcast(P)).then_inc(loaded_beta, 16)

            def load_w(g, par):
                for c in range(3):
                    sp.dma_start(wqkv[:, par, c], w_v[c][:, :, ds(g * DK, DK)]).then_inc(w_loaded[par], 16)

            load_w(0, 0)
            load_w(1, 1)
            sp.dma_start(wo, wo_v).then_inc(wo_loaded, 16)

            def load_next(g, par):
                sp.wait_ge(proj_done, g - 1)
                load_w(g, par)

            with sp.Fori(0, (H - 2) // 2) as turn:
                load_next(turn * 2 + 2, 0)
                load_next(turn * 2 + 3, 1)

            sp.wait_ge(attn_done, 1)
            for t in range(NT):
                sp.dma_start(x1[:, t], x_h[t]).then_inc(x1_loaded[t // 4], 16)
            sp.dma_start(rwraw[0:E, :], dram["L0_ffn_router_w"]).then_inc(small_loaded, 16)
            sp.dma_start(bias, dram["L1_ffn_bias"].partition_broadcast(P)).then_inc(small_loaded, 16)
            with nc.allow_non_contiguous_dma("256 numbers"):
                sp.dma_start(wscale, dram["L1_ffn_scale_weight"].rearrange("(c p) -> p c", p=P)).then_inc(small_loaded, 16)
            for w, name in enumerate(["L1_attn_Wq", "L1_attn_Wk", "L1_attn_Wv", "L1_attn_Wo", "L1_ffn_weight"]):
                sp.dma_start(l1raw[:, w], dram[name].rearrange("(c p) n -> p c n", p=P)).then_inc(l1_loaded, 16)
            sp.dma_start(wgu[:, E], dram["L0_ffn_shared_gate_up"].rearrange("(c p) n -> p c n", p=P)).then_inc(shared_loaded, 16)
            sp.dma_start(wdn[:, E], dram["L0_ffn_shared_down"].rearrange("(c p) n -> p c n", p=P)).then_inc(shared_loaded, 16)
            for e in range(E):
                sp.dma_start(wgu[:, e], dram["L0_ffn_w_gate_up"][e].rearrange("(c p) n -> p c n", p=P)).then_inc(experts_loaded, 16)
                sp.dma_start(wdn[:, e], dram["L0_ffn_w_down"][e].rearrange("(c p) n -> p c n", p=P)).then_inc(experts_loaded, 16)

            sp.wait_ge(xs_scattered, 16 * NT)

            def load_rows(j, par):
                sp.wait_ge(x_turned, j + ROUTED - 1)
                sp.dma_start(xrow[:, par], xs_d[ds(j * P, P), :]).then_inc(xs_loaded[par], 16)

            with sp.Fori(0, JOBS // 2) as pair:
                load_rows(pair * 2, 0)
                load_rows(pair * 2 + 1, 1)
            load_rows(JOBS - 1, 0)

            for p in range(NT // 2):
                sp.wait_ge(x1_ready, NJ + p + 1)
                for t in (2 * p, 2 * p + 1):
                    sp.dma_start(x2_h[t], x1[:, t]).then_inc(x2_stored, 16)
            sp.wait_ge(x2_stored, 16 * NT)
            x2_v = x2_d.rearrange("(b j p) d -> b p j d", j=NJ, p=P)
            out_v = out.rearrange("b (j p) d -> b p j d", p=P)
            for b in range(2):
                sp.dma_start(x2n[:, b], x2_v[b]).then_inc(x2n_loaded[b], 16)
            for b in range(B):
                sp.wait_ge(x4_ready, b + 1)
                sp.dma_start(out_v[b], x4[:, b % 2]).then_inc(x4_stored[b % 2], 16)
                if b + 2 < B:
                    sp.dma_start(x2n[:, b % 2], x2_v[b + 2]).then_inc(x2n_loaded[b % 2], 16)
            for par in range(2):
                sp.wait_ge(x4_stored[par], 16 * (B // 2))

        @block.gpsimd
        def _(pool):
            pool.memset(ident[:], 0.0).then_inc(consts, 1)
            pool.memset(mask[:], 0.0).then_inc(consts, 1)
            pool.memset(seed_l[:], 1.0 / (DK * P)).then_inc(consts, 1)
            pool.memset(seed_r[:], 0.0).then_inc(consts, 1)
            pool.memset(minushalf[:], -0.5).then_inc(consts, 1)
            pool.memset(delta[:], 1.0).then_inc(consts, 1)
            pool.memset(Y[:], 0.0).then_inc(consts, 1)
            pool.memset(pbd, 0.0).then_inc(consts, 1)
            pool.wait_ge(consts, 8)
            pool.affine_select(out=ident[:], in_=ident[:], compare_op=ALU.not_equal, fill=1.0, base=0,
                               pattern=[[-1, P]], channel_multiplier=1).then_inc(consts, 1)
            for half in range(2):
                pool.wait_ge(consts, 9 + half)
                pool.affine_select(out=mask[SEG * half:SEG * half + SEG, :], in_=mask[SEG * half:SEG * half + SEG, :],
                                   compare_op=ALU.is_ge, fill=MASKED, base=0,
                                   pattern=[[-1, SEG]], channel_multiplier=1).then_inc(consts, 1)
            pool.wait_ge(consts, 11)
            pool.memset(seed_r[:, :, DK:MEM], 1.0).then_inc(consts, 1)
            for b in range(B):
                pool.wait_ge(x_var, b + 1)
                pool.tensor_tensor(rstd[:, b * NJ:(b + 1) * NJ], vareps[:, b * NJ:(b + 1) * NJ], minushalf[:],
                                   ALU.pow).then_inc(x_rstd, 1)

            def body(n):
                if not n.heads_on:
                    return
                for b in range(B):
                    for qk in range(2):
                        t = 2 * b + qk
                        pool.wait_ge(raw_ready, n.count(2 * B, 2 * B + t + 1))
                        if n.first >= 0 or t >= 2:
                            pool.wait_ge(sigma_done, n.count(2 * B, 2 * B + t - 1))
                        pool.tensor_tensor(plus1[:, t % 2], raw[:, qk, b], seed_r[:, 0, DK:MEM].to_broadcast([P, S]),
                                           ALU.add).then_inc(plus1_done, 1)

            pool.wait_ge(consts, 12)
            bodies(pool, body)

            pool.wait_ge(attn_done, 1)
            pool.memset(tri, 1.0).then_inc(post_consts, 1)
            pool.memset(ones, 1.0).then_inc(post_consts, 1)
            pool.memset(resets, 1.0).then_inc(post_consts, 1)
            pool.iota(chosen[:, 0:E].bitcast(mybir.dt.int32), [[-1, E]], base=E, channel_multiplier=0).then_inc(post_consts, 1)
            pool.iota(jobi.bitcast(mybir.dt.int32), [[1, JOBS + 1]], base=0, channel_multiplier=0).then_inc(post_consts, 1)
            pool.wait_ge(post_consts, 5)
            pool.tensor_copy(down8, chosen[:, 0:E].bitcast(mybir.dt.int32)).then_inc(post_consts, 1)
            pool.tensor_copy(jobno, jobi.bitcast(mybir.dt.int32)).then_inc(post_consts, 1)
            pool.memset(resets[:, :, 0], 0.0).then_inc(post_consts, 1)
            pool.affine_select(out=tri, in_=tri, compare_op=ALU.is_ge, fill=0.0, base=-1,
                               pattern=[[1, P]], channel_multiplier=-1).then_inc(post_consts, 1)

            groups = [0]

            def rstds(k, n=4):
                groups[0] += 1
                pool.wait_ge(ln_var, groups[0])
                pool.tensor_tensor(lnr[:, k:k + n], lnv[:, k:k + n], minushalf[:, 0:n], ALU.pow).then_inc(ln_rstd, 1)

            for k in range(0, 2 * NT, 4):
                rstds(k)
            pool.wait_ge(xs_zeroed, 32)
            for t in range(NT):
                pool.wait_ge(xs_ready, t + 1)
                pool.indirect_dma_start(out=xs_d, out_offset=bass.IndirectOffsetOnAxis(posi[:, t:t + 1], 0),
                                        in_=Y[:, t], in_offset=None).then_inc(xs_scattered, 16)

            def store_y(j, par):
                pool.wait_ge(y_out, j + EARLY + 1)
                pool.dma_start(ys_d[ds(j * P, P), :], yj[:, par]).then_inc(y_stored[par], 16)

            with pool.Fori(0, JOBS // 2) as pair:
                store_y(pair * 2, 0)
                store_y(pair * 2 + 1, 1)
            store_y(JOBS - 1, 0)
            pool.wait_ge(y_stored[0], 16 * ((JOBS + 1) // 2))
            pool.wait_ge(y_stored[1], 16 * (JOBS // 2))
            for t in range(NT):
                pool.indirect_dma_start(out=Y[:, t], out_offset=None, in_=ys_d,
                                        in_offset=bass.IndirectOffsetOnAxis(posi[:, t:t + 1], 0))\
                    .then_inc(y_gathered[t // 2], 16)
            for kind, p in late_groups():
                rstds(slot(kind, p), 2)
            for k in range(4 * NT, 4 * LNS, 4):
                rstds(k)

        @block.vector
        def _(dve):
            for b in range(B):
                dve.wait_ge(loaded_x[b], 16)
                for j in range(NJ):
                    dve.bn_stats(stats[:, b * NJ + j], xin[:, b, j]).then_inc(x_stats, 1)
                for j in range(NJ):
                    t = b * NJ + j
                    dve.wait_ge(x_stats, NJ * 2 * b + j + 1)
                    dve.bn_aggr(mv[:, t], stats[:, t]).then_inc(x_stats, 1)
                dve.wait_ge(x_stats, NJ * 2 * (b + 1))
                dve.tensor_scalar(vareps[:, b * NJ:(b + 1) * NJ], mv[:, b * NJ:(b + 1) * NJ, 1], EPS, None,
                                  ALU.add).then_inc(x_var, 1)
            for b in range(B):
                dve.wait_ge(x_rstd, b + 1)
                for j in range(NJ):
                    t = b * NJ + j
                    dve.tensor_scalar(xnorm[:, b, j], xin[:, b, j], mv[:, t, 0:1], rstd[:, t:t + 1],
                                      ALU.subtract, ALU.mult).then_inc(x_normed, 1)
            dve.wait_ge(beta_e, 1)
            dve.tensor_scalar(b1, b1, 1.0, None, ALU.add).then_inc(beta_step, 1)
            dve.wait_ge(beta_step, 1)
            dve.reciprocal(bB, b1).then_inc(beta_step, 1)
            dve.wait_ge(beta_step, 2)
            dve.wait_ge(consts, 12)

            def combine(n, j, back):
                m = (n.par + back) % 2
                name = ("PV", j)
                dve.wait_ge(filled[n.BANK[name]], n.turn(name, back) + 1)
                for r in range(2):
                    dve.wait_ge(fromm_ready[r], n.count(NSEG, 2 * j + 2 - NSEG * back))
                dve.wait_ge(rinv_ready, n.count(B, B - B * back))
                w = work[n.BANK[name]]
                for b in range(B):
                    ins = dve.scalar_tensor_tensor(out=fromm[:, j % 2, b], in0=w[:, b * P:(b + 1) * P],
                                                   scalar=rinv[:, m, b, j:j + 1], in1=fromm[:, j % 2, b],
                                                   op0=ALU.mult, op1=ALU.add)
                    if b == B - 2:
                        ins.then_inc(att_ready, 1)
                ins.then_inc(freed[n.BANK[name]], 1)

            def deltas(n, i):
                o, k = own(i), own(i + 1)
                for r in range(2):
                    dve.wait_ge(read_done[r], n.count(NSEG, i + 1))
                    dve.reciprocal(rden[:, i % 2, 2 * r:2 * r + 2], readp[r][:, :, DK]).then_inc(rden_ready[r], 1)
                    if i == NSEG - 1:
                        continue
                    dve.wait_ge(rden_ready[r], n.count(NSEG, i + 1))
                    for bb in range(2):
                        b = 2 * r + bb
                        ins = dve.scalar_tensor_tensor(out=delta[o, b, 0:DK], in0=readp[r][k, bb, 0:DK],
                                                       scalar=rden[k, i % 2, b:b + 1], in1=vb[o, n.par, b, i // 2],
                                                       op0=ALU.mult, op1=ALU.subtract, reverse1=True)
                    ins.then_inc(delta_ready[r], 1)

            def scores_shift(n, b):
                name = ("sc", b)
                w = work[n.BANK[name]][:, 0:NJ * SEG].rearrange("p (j c) -> p j c", j=NJ)
                dve.wait_ge(filled[n.BANK[name]], n.turn(name) + 1)
                dve.tensor_tensor(sm[:, b % 2], w, mask[:].unsqueeze(1).to_broadcast([P, NJ, SEG]),
                                  ALU.add).then_inc(freed[n.BANK[name]], 1)
                dve.wait_ge(freed[n.BANK[name]], n.turn(name) + 1)
                dve.tensor_reduce(rowmax[:, b % 2], sm[:, b % 2], AX.X, ALU.max).then_inc(max_ready, 1)
                dve.wait_ge(max_ready, n.count(B, B + b + 1))
                dve.tensor_tensor(sm[:, b % 2], sm[:, b % 2],
                                  rowmax[:, b % 2].unsqueeze(2).to_broadcast([P, NJ, SEG]),
                                  ALU.subtract).then_inc(score_shifted, 1)

            def row_sums(n, b):
                dve.wait_ge(probs_ready, n.count(B, B + b + 1))
                dve.tensor_reduce(rowsum[:, b], pbd[:, b], AX.X, ALU.add).then_inc(sum_ready, 1)
                dve.wait_ge(sum_ready, n.count(B, B + b + 1))
                dve.reciprocal(rinv[:, 1 - n.par, b], rowsum[:, b]).then_inc(rinv_ready, 1)

            def values(n, b):
                name = ("V", b)
                g = n.first + 1 if n.loop is None else n.first + 1 + 2 * n.loop
                w = work[n.BANK[name]][:].rearrange("p (j c) -> p j c", j=NJ)
                dve.wait_ge(filled[n.BANK[name]], n.turn(name) + 1)
                dve.tensor_tensor(vb[:, 1 - n.par, b], w, bB[:, ds(g * P, P)].unsqueeze(1).to_broadcast([P, NJ, P]),
                                  ALU.mult).then_inc(vb_ready, 1)
                dve.wait_ge(vb_ready, n.count(B, B + b + 1))
                dve.tensor_tensor(v1[:, 1 - n.par, b], w, vb[:, 1 - n.par, b], ALU.subtract).then_inc(freed[n.BANK[name]], 1)

            def sigmas(n, b):
                for qk in range(2):
                    t = 2 * b + qk
                    name = ("qk"[qk], b)
                    dve.wait_ge(freed[n.BANK[name]], n.turn(name) + 1)
                    dve.wait_ge(plus1_done, n.count(2 * B, 2 * B + t + 1))
                    y = sigma_places(1 - n.par, b, qk)
                    more = like(plus1[:, t % 2], qk)
                    for a, c in [(y, more)] if qk else [(y[:, :, e], more[:, :, e]) for e in range(2)]:
                        ins = dve.scalar_tensor_tensor(out=a, in0=a, scalar=1.0, in1=c, op0=ALU.min, op1=ALU.max)
                    ins.then_inc(sigma_done, 1)

            def body(n):
                for i in range(NSEG):
                    if i % 2 == 0:
                        if i == 0 and n.tail:
                            combine(n, NJ - 1, 1)
                        elif i and n.chain:
                            combine(n, (i - 2) // 2, 0)
                    if n.chain:
                        deltas(n, i)
                    for b in range(B):
                        if n.heads_on and SC_AT[b] == i:
                            scores_shift(n, b)
                    for b in range(B):
                        if n.heads_on and V_AT[b] == i:
                            values(n, b)
                    for b in range(B):
                        if n.heads_on and SUM_AT[b] == i:
                            row_sums(n, b)
                    for b in range(B):
                        if n.heads_on and QK_AT[b] == i:
                            sigmas(n, b)

            bodies(dve, body)

            dve.wait_ge(attn_done, 1)
            done = [0, 0, 0]

            def step(ins):
                done[0] += 1
                ins.then_inc(ln_step, 1)

            def ln_stats(tiles, k=None, n=4):
                if k is None:
                    k = done[2]
                    done[2] += n
                for x in range(n):
                    step(dve.bn_stats(lnst[:, x], tiles[:, x]))
                for x in range(n):
                    dve.wait_ge(ln_step, done[0] - n + 1)
                    step(dve.bn_aggr(lnm[:, k + x], lnst[:, x]))
                dve.wait_ge(ln_step, done[0])
                dve.tensor_scalar(lnv[:, k:k + n], lnm[:, k:k + n, 1], EPS, None, ALU.add).then_inc(ln_var, 1)
                done[1] += 1
                return k, done[1]

            def ln_apply(to, tiles, stats, signal=None, n=4):
                k, count = stats
                dve.wait_ge(ln_rstd, count)
                for x in range(n):
                    ins = dve.tensor_scalar(to[:, x], tiles[:, x], lnm[:, k + x, 0:1],
                                            lnr[:, k + x:k + x + 1], ALU.subtract, ALU.mult)
                    if signal is not None:
                        ins.then_inc(signal, 1)
                    elif x == n - 1:
                        step(ins)

            def group(a, g):
                return a[:, 4 * g:4 * g + 4]

            of_y = [ln_stats(group(Y, g)) for g in range(NJ)]
            for g in range(NJ):
                dve.wait_ge(x1_loaded[g], 64)
                ln_apply(group(Y, g), group(Y, g), of_y[g])
                dve.wait_ge(ln_step, done[0])
                dve.tensor_tensor(group(x1, g), group(x1, g), group(Y, g), ALU.add).then_inc(x1_ready, 1)
                dve.wait_ge(x1_ready, g + 1)
                ln_stats(group(x1, g))
            dve.wait_ge(ln_rstd, 2 * NJ)
            dve.wait_ge(post_consts, 9)
            dve.wait_ge(l1_loaded, 16 * 5)
            dve.wait_ge(small_loaded, 48)
            for c in range(DC):
                dve.tensor_scalar(l1raw[:, 4, c], l1raw[:, 4, c], wscale[:, c:c + 1], None, ALU.mult).then_inc(wscaled, 1)

            def norm_row(u, t, par):
                if not (isinstance(u, int) and u < 2):
                    dve.wait_ge(x_turned, u - 1)
                dve.tensor_scalar(xrow[:, par], x1[:, ds(t, 1)].rearrange("p a d -> p (a d)"),
                                  lnm[:, ds(t + 4 * NJ, 1), 0], lnr[:, ds(t + 4 * NJ, 1)],
                                  ALU.subtract, ALU.mult).then_inc(xrow_ready, 1)

            def top(t, par):
                dve.wait_ge(x_used, t + 1)
                dve.tensor_copy(logit[:, ds(t, 1)].rearrange("p a e -> p (a e)"),
                                mflat[par][:, 0:E]).then_inc(logit_copied, 1)

            norm_row(0, 0, 0)
            for t in range(2):
                norm_row(t + 1, t + 1, (t + 1) % 2)
                top(t, t % 2)
            with dve.Fori(1, NT // 2 - 1) as pair:
                for par in range(2):
                    norm_row(pair * 2 + (par + 1), pair * 2 + (par + 1), 1 - par)
                    top(pair * 2 + par, par)
            for t in range(NT - 2, NT):
                norm_row(t + 1, (t + 1) % NT, (t + 1) % 2)
                top(t, t % 2)
            norm_row(SHARED + 1, 1, 1)

            r = [0]

            def chain(ins):
                r[0] += 1
                ins.then_inc(route_step, 1)
                dve.wait_ge(route_step, r[0])

            def wide(a, n, axis):
                shape = [P, E, n] if axis == 2 else [P, n, E]
                return a.unsqueeze(axis).to_broadcast(shape)

            dve.wait_ge(logit_copied, NT)
            dve.tensor_reduce(toplogit, logit, AX.X, ALU.max).then_inc(top_done, 1)
            dve.wait_ge(top_done, 1)
            chain(dve.tensor_tensor(istop, logit, toplogit.unsqueeze(2).to_broadcast([P, NT, E]), ALU.is_equal))
            chain(dve.tensor_tensor(istop, istop, wide(down8, NT, 1), ALU.mult))
            chain(dve.tensor_reduce(chosen, istop, AX.X, ALU.max))
            dve.tensor_tensor(onehot, wide(down8, NT, 1), chosen.unsqueeze(2).to_broadcast([P, NT, E]),
                              ALU.is_equal).then_inc(onehot_ready, 1)
            dve.wait_ge(gate_exp, 1)
            chain(dve.tensor_scalar(gate, gate, 1.0, None, ALU.add))
            chain(dve.reciprocal(gate, gate))
            chain(dve.tensor_tensor(gate, gate, lnr[:, 4 * NJ:8 * NJ], ALU.mult))
            dve.wait_ge(onehot_ready, 1)
            dve.wait_ge(ranks_done, 2)
            chain(dve.tensor_copy(total, mflat[1][:, 0:NT * E].rearrange("p (t e) -> p e t", e=E)))
            line = "p e t -> p (e t)"
            chain(dve.tensor_tensor_scan(running.rearrange(line), resets.rearrange(line), total.rearrange(line), 0.0,
                                         ALU.mult, ALU.add))
            chain(dve.tensor_copy(count8, running[:, :, NT - 1]))
            chain(dve.tensor_tensor(running, running, total, ALU.subtract))
            ti = tiles8.bitcast(mybir.dt.int32)
            chain(dve.tensor_scalar(ti, count8, float(P - 1), None, ALU.add))
            chain(dve.tensor_scalar(ti, ti, 7, None, ALU.arith_shift_right))
            chain(dve.tensor_copy(tilesf, ti))
            chain(dve.tensor_tensor_scan(ends, ones[:, 0:E], tilesf, 0.0, ALU.mult, ALU.add))
            chain(dve.tensor_tensor(starts, ends, tilesf, ALU.subtract))
            chain(dve.tensor_scalar(starts, starts, float(P), None, ALU.mult))
            chain(dve.tensor_tensor(running, running, wide(starts, NT, 2), ALU.add))
            chain(dve.tensor_tensor(before, mflat[0][:, 0:NT * E].rearrange("p (t e) -> p t e", e=E),
                                    running.rearrange("p e t -> p t e"), ALU.add))
            chain(dve.tensor_tensor(before, before, onehot, ALU.mult))
            chain(dve.tensor_reduce(posf, before, AX.X, ALU.add))
            chain(dve.tensor_copy(posi, posf))
            for t in range(NT):
                dve.tensor_scalar(Y[:, t], x1[:, t], lnm[:, 4 * NJ + t, 0:1], gate[:, t:t + 1],
                                  ALU.subtract, ALU.mult).then_inc(xs_ready, 1)
            chain(dve.tensor_tensor(later, jobno.unsqueeze(2).to_broadcast([P, JOBS + 1, E]), wide(ends, JOBS + 1, 1),
                                    ALU.is_ge))
            chain(dve.tensor_reduce(jobe, later, AX.X, ALU.add))
            chain(dve.tensor_scalar(jobi.bitcast(mybir.dt.int32), jobe, float(E - 1), None, ALU.min))

            def hidden(n, par):
                dve.wait_ge(silu_done, n + 1)
                dve.tensor_tensor(hrow[:, par], sgate[:, par], work[2 * par + 1][:], ALU.mult).then_inc(h_ready, 1)

            hidden(0, 0)
            with dve.Fori(0, (EARLY - 2) // 2) as pair:
                for par in range(2):
                    n = pair * 2 + (par + 1)
                    norm_row(n + (SHARED + 1), n + 1, par)
                    hidden(n, 1 - par)
            hidden(EARLY - 1, 1)
            with dve.Fori(0, JOBS // 2) as pair:
                for par in range(2):
                    hidden(pair * 2 + (EARLY + par), par)
            norm_row(SHARED + LATE, EARLY, LATE % 2)
            hidden(LATE - 1, 0)

            def two(a, p):
                return a[:, 2 * p:2 * p + 2]

            stats_of = {}

            def moe_sum(p):
                dve.wait_ge(y_gathered[p], 32)
                dve.wait_ge(y_out, 2 * p + 2 if 2 * p < EARLY else 2 * p + 2 + JOBS)
                step(dve.tensor_tensor(two(Y, p), two(Y, p), two(shared, p), ALU.add))
                dve.wait_ge(ln_step, done[0])
                stats_of["moe", p] = ln_stats(two(Y, p), slot("moe", p), 2)

            def make_x2(p):
                ln_apply(two(Y, p), two(Y, p), stats_of["moe", p], n=2)
                dve.wait_ge(ln_step, done[0])
                dve.tensor_tensor(two(x1, p), two(x1, p), two(Y, p), ALU.add).then_inc(x1_ready, 1)
                dve.wait_ge(x1_ready, NJ + p + 1)
                stats_of["x2", p] = ln_stats(two(x1, p), slot("x2", p), 2)

            def norm_x2(p):
                ln_apply(two(Y, p), two(x1, p), stats_of["x2", p], xn2_ready, 2)

            def x2_work(i):
                for lag, what in ((2, norm_x2), (1, make_x2), (0, moe_sum)):
                    if 0 <= i - lag < NT // 2:
                        what(i - lag)

            for t in range(EARLY, NT):
                n = t + JOBS
                if t + 1 < NT:
                    norm_row(SHARED + n + 1, t + 1, (n + 1) % 2)
                hidden(n, n % 2)
                if t > EARLY:
                    x2_work(t - EARLY - 1)
            for i in range(NT - EARLY - 1, NT // 2 + 2):
                x2_work(i)
            done[2] = 4 * NT

            def running_sums(b, e):
                c = 3 * (2 * b + e)
                dve.wait_ge(k_copied[e], b + 1)
                dve.wait_ge(qkv_done[e], 3 * b + 3)
                qb, kb, vbk = (work[0:3] if e == 0 else [work[3], flat[0], flat[1]])
                dve.tensor_tensor(kv[:, e], kbuf[:, e], vbk[:, 0:S], ALU.mult).then_inc(kv_step, 1)
                dve.wait_ge(kv_step, 2 * (2 * b + e) + 1)
                dve.tensor_tensor_scan(kvt[:, e], ones[:, 0:1].to_broadcast([P, S]), kv[:, e], 0.0,
                                       ALU.mult, ALU.add).then_inc(kv_step, 1)
                dve.wait_ge(kv_step, 2 * (2 * b + e) + 2)
                dve.scalar_tensor_tensor(out=vh[:, b % 2, e], in0=kvt[:, e], scalar=DENOM, in1=qb[:, 0:S],
                                         op0=ALU.mult, op1=ALU.mult).then_inc(vh_done[e], 1)

            running_sums(0, 0)
            running_sums(0, 1)
            for b in range(B):
                m = b % 2
                pair = lambda jj: mflat[jj][:, 0:2 * D].rearrange("p (x d) -> p x d", x=2)
                k = done[2]
                for x in range(NJ):
                    if x % 2 == 0:
                        dve.wait_ge(o_done, 2 * b + x // 2 + 1)
                    step(dve.bn_stats(lnst[:, x], pair(x // 2)[:, x % 2]))
                for x in range(NJ):
                    dve.wait_ge(ln_step, done[0] - 3)
                    step(dve.bn_aggr(lnm[:, k + x], lnst[:, x]))
                dve.wait_ge(ln_step, done[0])
                dve.tensor_scalar(lnv[:, k:k + 4], lnm[:, k:k + 4, 1], EPS, None, ALU.add).then_inc(ln_var, 1)
                done[1] += 1
                done[2] += 4
                dve.wait_ge(ln_rstd, done[1])
                for x in range(NJ):
                    dve.tensor_scalar(lnout[:, m, x], pair(x // 2)[:, x % 2], lnm[:, k + x, 0:1],
                                      lnr[:, k + x:k + x + 1], ALU.subtract, ALU.mult).then_inc(o_used, 1)
                dve.wait_ge(o_used, NJ * (b + 1))
                dve.wait_ge(x2n_loaded[m], 16 * (b // 2 + 1))
                dve.tensor_tensor(x3[:, m], lnout[:, m], x2n[:, m], ALU.add).then_inc(x3_ready, 1)
                dve.wait_ge(x3_ready, b + 1)
                ln_apply(xn3[:, m], x3[:, m], ln_stats(x3[:, m]), xn3_ready)
                if b + 1 < B:
                    running_sums(b + 1, 0)
                    running_sums(b + 1, 1)
                for jj in range(2):
                    dve.wait_ge(f_done, 2 * b + jj + 1)
                    dve.tensor_tensor(lnout[:, m, 2 * jj:2 * jj + 2], pair(jj), bias.unsqueeze(1).to_broadcast([P, 2, D]),
                                      ALU.add).then_inc(f_used, 1)
                dve.wait_ge(f_used, 2 * b + 2)
                ln_apply(lnout[:, m], lnout[:, m], ln_stats(lnout[:, m]))
                dve.wait_ge(ln_step, done[0])
                if b >= 2:
                    dve.wait_ge(x4_stored[m], 16 * (b // 2))
                dve.tensor_tensor(x4[:, m], lnout[:, m], x3[:, m], ALU.add).then_inc(x4_ready, 1)

        @block.scalar
        def _(act):
            act.wait_ge(loaded_beta, 16)
            act.activation(b1, braw, ACT.Exp, scale=-1.0).then_inc(beta_e, 1)
            for b in range(B):
                for c in range(DC):
                    g = b * DC + c
                    act.wait_ge(xT_written[g % 4], g // 4 + 1)
                    act.copy(xT[:, c, b], work[g % 4][:]).then_inc(xT_copied, 1)
            act.wait_ge(consts, 12)

            def copy_out(n, name, dst):
                k = n.BANK[name]
                act.wait_ge(filled[k], n.turn(name) + 1)
                w = work[k][:]
                if len(dst.shape) == 3:
                    w = w.rearrange("p (j c) -> p j c", j=dst.shape[1])
                act.copy(dst, w).then_inc(freed[k], 1)

            def project_copies(n, b):
                for qk in range(2):
                    name = ("qk"[qk], b)
                    k = n.BANK[name]
                    act.wait_ge(filled[k], n.turn(name) + 1)
                    act.copy(raw[:, qk, b], work[k][:]).then_inc(raw_ready, 1)
                    act.activation(sigma_places(1 - n.par, b, qk), like(work[k][:], qk), ACT.Exp)\
                        .then_inc(freed[k], 1)

            def from_memory(n, i):
                o = own(i)
                for r in range(2):
                    act.wait_ge(rden_ready[r], n.count(NSEG, i + 1))
                    for bb in range(2):
                        b = 2 * r + bb
                        ins = act.activation(fromm[o, (i // 2) % 2, b], readp[r][o, bb, 0:DK], ACT.Copy,
                                             scale=rden[o, i % 2, b:b + 1])
                    ins.then_inc(fromm_ready[r], 1)

            def mem_copy(n, i):
                for r in range(2):
                    act.wait_ge(mem_written[r], n.count(NSEG, i + 2))
                    act.copy(mem[:, 2 * r:2 * r + 2, 0:MEM], memp[r][:, :, 0:MEM]).then_inc(mem_copied[r], 1)

            def body(n):
                m = 1 - n.par
                for i in range(NSEG):
                    if n.chain:
                        from_memory(n, i)
                    if n.heads_on:
                        for b in range(B):
                            if QK_AT[b] == i:
                                project_copies(n, b)
                        for b in range(B):
                            if SC_AT[b] == i:
                                copy_out(n, ("sk", b), skt[:, m, b])
                        for b in range(B):
                            if PT_AT[b] == i:
                                copy_out(n, ("PT", b), pt[:, m, b])
                    if i == 1 and n.tail:
                        act.wait_ge(xs_zeroed, 32)
                        name = ("Wo",)
                        act.wait_ge(filled[n.BANK[name]], n.turn(name) + 1)
                        g = n.first - 1 if n.loop is None else n.first - 1 + 2 * n.loop
                        ins = act.copy(Y[:, ds(g, 1), :].rearrange("p a d -> p (a d)"), work[n.BANK[name]][:, 0:D])
                        ins.then_inc(freed[n.BANK[name]], 1)
                    if i == 0 and n.tail:
                        copy_out(n, ("attT", NJ - 1), attT[:, :, NJ - 1])
                    elif i and i % 2 == 0 and n.chain:
                        j = (i - 2) // 2
                        copy_out(n, ("attT", j), attT[:, :, j])
                    for b in range(B):
                        if n.heads_on and SC_AT[b] == i:
                            act.wait_ge(score_shifted, n.count(B, B + b + 1))
                            for half in range(2):
                                o = slice(SEG * half, SEG * half + SEG)
                                ins = act.activation(pbd[o, b, :, SEG * half:SEG * half + SEG], sm[o, b % 2], ACT.Exp,
                                                     scale=SCALE)
                            ins.then_inc(probs_ready, 1)
                    if n.chain and (i < NSEG - 1 or n.heads_on):
                        mem_copy(n, i)
                if n.first == -1:
                    mem_copy(n, NSEG - 1)

            bodies(act, body)
            act.copy(rowmax[:, 0], rowmax[:, 1]).then_inc(attn_done, 1)

            act.wait_ge(attn_done, 1)
            for w in range(5):
                act.wait_ge(l1_turned, w + 1)
                to = wqkvT[:, w] if w < 3 else wofT[:, w - 3]
                act.copy(to.rearrange("p c d -> p (c d)"), work[w % 4][:]).then_inc(l1_copied, 1)
            act.wait_ge(l1_turned, 6)
            act.copy(rwT.rearrange("p c e -> p (c e)"), work[1][:, 0:DC * E]).then_inc(l1_copied, 1)

            def row_turned(u, par):
                act.wait_ge(x_turned, u + 1)
                if not (isinstance(u, int) and u < 2):
                    act.wait_ge(x_used, u - 1)
                act.copy(xj[:, par], flat[par][:, 0:D]).then_inc(xj_copied, 1)

            for u in range(2):
                row_turned(u, u % 2)
            with act.Fori(1, NT // 2) as pair:
                for par in range(2):
                    row_turned(pair * 2 + par, par)
            row_turned(SHARED, 0)
            act.wait_ge(top_done, 1)
            act.activation(gate, toplogit, ACT.Exp, scale=-1.0).then_inc(gate_exp, 1)

            def silu(n, par):
                act.wait_ge(x_used, n + NT + 1)
                act.activation(sgate[:, par], work[2 * par][:], ACT.Silu).then_inc(silu_done, 1)

            def turned_hidden(n, par):
                act.wait_ge(hT_turned, n + 1)
                act.copy(hcol[:, par], mflat[0][:, 0:F]).then_inc(hT_copied, 1)

            def give_shared(n, t):
                act.wait_ge(down_done, n + 1)
                act.copy(shared[:, ds(t, 1)].rearrange("p a d -> p (a d)"), mflat[1][:, 0:D]).then_inc(y_out, 1)

            row_turned(SHARED + 1, 1)
            silu(0, 0)
            with act.Fori(0, (EARLY - 2) // 2) as pair:
                for par in range(2):
                    n = pair * 2 + (par + 1)
                    turned_hidden(n - 1, par)
                    silu(n, 1 - par)
                    give_shared(n - 1, n - 1)
                    row_turned(n + (SHARED + 1), par)
            for n in (EARLY - 1, EARLY):
                turned_hidden(n - 1, (n - 1) % 2)
                silu(n, n % 2)
                give_shared(n - 1, n - 1)
                row_turned(n + SHARED + 1, (n + 1) % 2)

            def give_routed(j, par, stored):
                act.wait_ge(down_done, j + (EARLY + 1))
                if stored is not None:
                    act.wait_ge(y_stored[par], stored)
                act.copy(yj[:, par], mflat[1][:, 0:D]).then_inc(y_out, 1)

            def routed_tile(pair, par):
                n = pair * 2 + (EARLY + par + 1)
                turned_hidden(n - 1, par)
                silu(n, 1 - par)
                give_routed(pair * 2 + par, par, None if isinstance(pair, int) else pair * 16)
                row_turned(n + (SHARED + 1), par)

            for par in range(2):
                routed_tile(0, par)
            with act.Fori(1, (JOBS - 1) // 2 - 1) as pair:
                for par in range(2):
                    routed_tile(pair, par)
            for j in range(JOBS - 2, JOBS + 1):
                n = EARLY + j
                turned_hidden(n - 1, (n - 1) % 2)
                silu(n, n % 2)
                give_routed(j - 1, (j - 1) % 2, 16 * ((j - 1) // 2))
                row_turned(n + SHARED + 1, (n + 1) % 2)

            x2T_v = x2T.rearrange("p c (g t r) -> p t c g r", t=NT, r=4)

            def copy_x2T(p):
                act.wait_ge(x2_turned, p + 1)
                for x in range(2):
                    ins = act.copy(x2T_v[:, 2 * p + x], flat[(p + X2_LAG + LATE) % 2][:, x * D:(x + 1) * D]
                                   .rearrange("p (c g r) -> p c g r", c=DC, r=4))
                ins.then_inc(x2T_copied, 1)

            for t in range(EARLY + 1, NT + 1):
                n = t + JOBS
                turned_hidden(n - 1, (n - 1) % 2)
                if t < NT:
                    silu(n, n % 2)
                if t - EARLY >= X2_LAG:
                    copy_x2T(t - EARLY - X2_LAG)
                give_shared(n - 1, t - 1)
                if t + 1 < NT:
                    row_turned(n + SHARED + 1, (n + 1) % 2)
            for p in range(NT - EARLY - X2_LAG + 1, NT // 2):
                copy_x2T(p)

            def keys(b, e):
                act.wait_ge(qkv_done[e], 3 * b + 1)
                act.copy(kbuf[:, e], (work[1] if e == 0 else flat[0])[:, 0:S]).then_inc(k_copied[e], 1)

            keys(0, 0)
            keys(0, 1)
            for b in range(B):
                if b + 1 < B:
                    keys(b + 1, 0)
                for jj in range(2):
                    act.wait_ge(t3_done, 2 * b + jj + 1)
                    act.copy(x3T[:, b % 2, 2 * jj:2 * jj + 2].rearrange("p j d -> p (j d)"),
                             mflat[jj][:, 0:2 * D]).then_inc(x3T_copied, 1)
                if b + 1 < B:
                    keys(b + 1, 1)

        @block.tensor
        def _(pe):
            pe.wait_ge(consts, 12)
            for b in range(B):
                pe.wait_ge(x_normed, NJ * (b + 1))
                for c in range(DC):
                    g = b * DC + c
                    if g >= 4:
                        pe.wait_ge(xT_copied, g - 3)
                    for j in range(NJ):
                        ins = pe.transpose(work[g % 4][:, j * P:(j + 1) * P], xnorm[:, b, j, c * P:(c + 1) * P], ident[:])
                    ins.then_inc(xT_written[g % 4], 1)
            pe.wait_ge(xT_copied, DC * B)

            def into(n, name, back=0):
                k = n.BANK[name]
                v = n.turn(name, back)
                if not (isinstance(v, int) and v == 0):
                    pe.wait_ge(freed[k], v)
                return work[k], filled[k]

            def consumed(n, name, back=0):
                k = n.BANK[name]
                pe.wait_ge(freed[k], n.turn(name, back) + 1)

            def project_qk(n, b):
                m = 1 - n.par
                for qk in range(2):
                    w, done = into(n, ("qk"[qk], b))
                    if b == 0 and qk == 0:
                        pe.wait_ge(w_loaded[m], weights_count(n))
                    for c in range(DC):
                        ins = pe.matmul(w[:], wqkv[:, m, qk, c], xT[:, c, b], start=(c == 0), stop=(c == DC - 1))
                    ins.then_inc(done, 1)

            def weights_count(n):
                k = (n.first + 1) // 2 + 1
                return 48 * k if n.loop is None else 48 * k + 48 * n.loop

            def project_v(n, b):
                m = 1 - n.par
                w, done = into(n, ("V", b))
                for j in range(NJ):
                    for c in range(DC):
                        ins = pe.matmul(w[:, j * P:(j + 1) * P], xT[:, c, b, j * P:(j + 1) * P], wqkv[:, m, 2, c],
                                        start=(c == 0), stop=(c == DC - 1))
                ins.then_inc(done, 1)

            def turn_keys(n, b):
                m = 1 - n.par
                pe.wait_ge(sigma_done, n.count(2 * B, 2 * B + 2 * b + 2))
                w, done = into(n, ("sk", b))
                pairs = sqk[:, m, b].rearrange("p s c -> p (s c)").rearrange("p (j x) -> p j x", j=NJ)
                for j in range(NJ):
                    ins = pe.transpose(w[:, j * P:(j + 1) * P], pairs[:, j, SEG:3 * SEG], ident[:])
                ins.then_inc(done, 1)

            def scores(n, b):
                consumed(n, ("k", b))
                w, done = into(n, ("sc", b))
                for i in range(NSEG):
                    c = slice(i * SEG, (i + 1) * SEG)
                    ins = pe.matmul(w[own(i), (i // 2) * SEG:(i // 2 + 1) * SEG], raw[:, 0, b, c], raw[:, 1, b, c],
                                    start=True, stop=True)
                ins.then_inc(done, 1)

            def turn_probs(n, b):
                pe.wait_ge(probs_ready, n.count(B, B + b + 1))
                w, done = into(n, ("PT", b))
                for j in range(NJ):
                    ins = pe.transpose(w[:, j * P:(j + 1) * P], pbd[:, b, j], ident[:])
                    if b == B - 1 and j == 0:
                        ins.then_inc(proj_done, 1)
                ins.then_inc(done, 1)

            def probs_values(n, j):
                w, done = into(n, ("PV", j))
                for b in range(B):
                    ins = pe.matmul(w[:, b * P:(b + 1) * P], pt[:, n.par, b, j], v1[:, n.par, b, j], start=True, stop=True)
                ins.then_inc(done, 1)

            def turn_att(n, j, back):
                pe.wait_ge(att_ready, n.count(NJ, j + 1 - NJ * back))
                consumed(n, ("PV", j), back)
                w, done = into(n, ("attT", j))
                for b in range(B):
                    ins = pe.transpose(w[:, b * P:(b + 1) * P], fromm[:, j % 2, b], ident[:])
                ins.then_inc(done, 1)

            def project_out(n):
                consumed(n, ("attT", NJ - 1))
                if n.first == 1:
                    pe.wait_ge(wo_loaded, 16)
                w, done = into(n, ("Wo",))
                tokens = attT.rearrange("p b j (r c) -> p c (b j r)", c=H)
                for c in range(H):
                    ins = pe.matmul(w[:, 0:D], tokens[:, c], wo[:, c], start=(c == 0), stop=(c == H - 1))
                ins.then_inc(done, 1)

            def seed():
                for r in range(2):
                    pe.matmul(memp[r][:, :, 0:MEM], seed_l[:], seed_r[:], start=True, stop=False,
                              skip_group_check=True).then_inc(mem_written[r], 1)

            def read_memories(n, i):
                for r in range(2):
                    pe.wait_ge(mem_copied[r], n.count(NSEG, i + 1))
                    if not (n.first == 0 and i == 0):
                        pe.wait_ge(fromm_ready[r], n.count(NSEG, i))
                    for bb in range(2):
                        b = 2 * r + bb
                        ins = pe.matmul(readp[r][:, bb, 0:MEM], sqk[:, n.par, b, i], mem[:, b, 0:MEM],
                                        start=True, stop=True)
                    ins.then_inc(read_done[r], 1)

            def update_memories(n, i):
                for r in range(2):
                    pe.wait_ge(delta_ready[r], n.count(NSEG - 1, i + 1))
                    for bb in range(2):
                        b = 2 * r + bb
                        ins = pe.matmul(memp[r][:, bb, 0:MEM], skt[own(i), n.par, b, i // 2], delta[own(i), b, 0:MEM],
                                        start=False, stop=False, skip_group_check=True)
                    ins.then_inc(mem_written[r], 1)

            def body(n):
                for i in range(NSEG):
                    if n.chain:
                        read_memories(n, i)
                    if n.heads_on:
                        for b in range(B):
                            if QK_AT[b] == i:
                                project_qk(n, b)
                        for b in range(B):
                            if SC_AT[b] == i:
                                turn_keys(n, b)
                                scores(n, b)
                        for b in range(B):
                            if V_AT[b] == i:
                                project_v(n, b)
                        for b in range(B):
                            if PT_AT[b] == i:
                                turn_probs(n, b)
                    if i == 1 and n.tail:
                        project_out(n)
                    if i == 0 and n.tail:
                        turn_att(n, NJ - 1, 1)
                    elif i and i % 2 == 0 and n.chain:
                        turn_att(n, (i - 2) // 2, 0)
                    if n.chain and i < NSEG - 1:
                        update_memories(n, i)
                    elif i == NSEG - 1 and n.heads_on:
                        seed()
                    if i % 2 and n.chain:
                        probs_values(n, (i - 1) // 2)

            bodies(pe, body)

            pe.wait_ge(attn_done, 1)
            pe.wait_ge(l1_loaded, 16 * 5)
            for w in range(5):
                if w == 4:
                    pe.wait_ge(wscaled, DC)
                    pe.wait_ge(l1_copied, 1)
                for c in range(DC):
                    for r in range(DC):
                        ins = pe.transpose(work[w % 4][:, c * D + r * P:c * D + (r + 1) * P],
                                           l1raw[:, w, r, c * P:(c + 1) * P], ident[:])
                ins.then_inc(l1_turned, 1)
            pe.wait_ge(small_loaded, 48)
            pe.wait_ge(l1_copied, 2)
            for c in range(DC):
                ins = pe.transpose(work[1][:, c * E:(c + 1) * E], rwraw[0:E, c * P:(c + 1) * P], ident[0:E, 0:E])
            ins.then_inc(l1_turned, 1)
            pe.wait_ge(l1_copied, 6)

            def turn_row(u, par):
                if not (isinstance(u, int) and u < 2):
                    pe.wait_ge(xj_copied, u - 1)
                for c in range(DC):
                    ins = pe.transpose(flat[par][:, c * P:(c + 1) * P], xrow[:, par, c * P:(c + 1) * P], ident[:])
                ins.then_inc(x_turned, 1)

            def turn_norm(u, par):
                pe.wait_ge(xrow_ready, u + 1 - JOBS if isinstance(u, int) and u >= SHARED + LATE else u + 1)
                turn_row(u, par)

            def logits(t, par):
                pe.wait_ge(xj_copied, t + 1)
                if not (isinstance(t, int) and t < 2):
                    pe.wait_ge(logit_copied, t - 1)
                for c in range(DC):
                    ins = pe.matmul(mflat[par][:, 0:E], xj[:, par, c * P:(c + 1) * P], rwT[:, c], start=(c == 0),
                                    stop=(c == DC - 1))
                ins.then_inc(x_used, 1)

            turn_norm(0, 0)
            for t in range(2):
                turn_norm(t + 1, (t + 1) % 2)
                logits(t, t % 2)
            with pe.Fori(1, NT // 2 - 1) as pair:
                for par in range(2):
                    turn_norm(pair * 2 + (par + 1), 1 - par)
                    logits(pair * 2 + par, par)
            for t in range(NT - 2, NT):
                turn_norm(t + 1, (t + 1) % 2)
                logits(t, t % 2)

            def gate_up(n, par, e):
                pe.wait_ge(xj_copied, n + NT + 1)
                if not (isinstance(n, int) and n < 2):
                    pe.wait_ge(h_ready, n - 1)
                for half in range(2):
                    for c in range(DC):
                        ins = pe.matmul(work[2 * par + half][:], xj[:, par, c * P:(c + 1) * P],
                                        wgu[:, e, c, half * F:(half + 1) * F] if isinstance(e, int) else
                                        wgu_flat[:, ds(e * (DC * 2 * F) + (c * 2 * F + half * F), F)],
                                        start=(c == 0), stop=(c == DC - 1))
                ins.then_inc(x_used, 1)

            def turn_hidden(n, par):
                pe.wait_ge(h_ready, n + 1)
                if not (isinstance(n, int) and n == 0):
                    pe.wait_ge(hT_copied, n)
                for k in range(FC):
                    ins = pe.transpose(mflat[0][:, k * P:(k + 1) * P], hrow[:, par, k * P:(k + 1) * P], ident[:])
                ins.then_inc(hT_turned, 1)

            def down(n, par, e):
                pe.wait_ge(hT_copied, n + 1)
                if not (isinstance(n, int) and n == 0):
                    pe.wait_ge(y_out, n)
                for k in range(FC):
                    ins = pe.matmul(mflat[1][:, 0:D], hcol[:, par, k * P:(k + 1) * P],
                                    wdn[:, e, k] if isinstance(e, int) else
                                    wdn_flat[:, ds(e * (FC * D) + k * D, D)],
                                    start=(k == 0), stop=(k == FC - 1))
                ins.then_inc(down_done, 1)

            wgu_flat = wgu.rearrange("p e c n -> p (e c n)")
            wdn_flat = wdn.rearrange("p e k n -> p (e k n)")
            pe.wait_ge(shared_loaded, 32)
            gate_up(0, 0, E)
            turn_norm(SHARED + 1, 1)
            pe.wait_ge(onehot_ready, 1)
            pe.wait_ge(post_consts, 9)
            hot = onehot.rearrange("p t e -> p (t e)")
            pe.matmul(mflat[0][:, 0:NT * E], tri, hot, start=True, stop=True).then_inc(ranks_done, 1)
            pe.matmul(mflat[1][:, 0:NT * E], ones, hot, start=True, stop=True).then_inc(ranks_done, 1)
            pe.wait_ge(xs_ready, 1)
            def shared_tile(n, par):
                turn_hidden(n - 1, par)
                gate_up(n, 1 - par, E)
                down(n - 1, par, E)
                turn_norm(n + (SHARED + 1), par)

            for par in range(2):
                shared_tile(par + 1, par)
            with pe.Fori(1, (EARLY - 2) // 2) as pair:
                for par in range(2):
                    shared_tile(pair * 2 + (par + 1), par)

            jobi_i = jobi.bitcast(mybir.dt.int32)

            def expert(j):
                return pe.value_load(jobi_i[0:1, ds(j, 1)], min_val=0, max_val=E - 1)

            def turn_sorted(j, par, loads):
                pe.wait_ge(xs_loaded[par], loads)
                turn_row(j + ROUTED, par)

            turn_hidden(EARLY - 2, 0)
            gate_up(EARLY - 1, 1, E)
            down(EARLY - 2, 0, E)
            turn_sorted(0, 0, 16)
            pe.wait_ge(experts_loaded, 32 * E)
            turn_hidden(EARLY - 1, 1)
            gate_up(EARLY, 0, expert(0))
            down(EARLY - 1, 1, E)
            turn_sorted(1, 1, 16)
            with pe.Fori(0, (JOBS - 1) // 2 - 1) as pair:
                for par in range(2):
                    j = pair * 2 + (par + 1)
                    turn_hidden(j + (EARLY - 1), par)
                    gate_up(j + EARLY, 1 - par, expert(j))
                    down(j + (EARLY - 1), par, expert(j - 1))
                    turn_sorted(j + 1, par, pair * 16 + 32)
            for j in range(JOBS - 2, JOBS + 1):
                n = EARLY + j
                turn_hidden(n - 1, (n - 1) % 2)
                gate_up(n, n % 2, expert(j) if j < JOBS else E)
                down(n - 1, (n - 1) % 2, expert(j - 1))
                if j + 1 < JOBS:
                    turn_sorted(j + 1, (j + 1) % 2, 16 * ((j + 1) // 2 + 1))
                else:
                    turn_norm(n + SHARED + 1, (n + 1) % 2)

            def turn_x2(p):
                pe.wait_ge(xn2_ready, 2 * p + 2)
                if p >= 2:
                    pe.wait_ge(x2T_copied, p - 1)
                for x in range(2):
                    for c in range(DC):
                        ins = pe.transpose(flat[(p + X2_LAG + LATE) % 2][:, (x * DC + c) * P:(x * DC + c + 1) * P],
                                           Y[:, 2 * p + x, c * P:(c + 1) * P], ident[:])
                ins.then_inc(x2_turned, 1)

            for t in range(EARLY + 1, NT + 1):
                n = t + JOBS
                turn_hidden(n - 1, (n - 1) % 2)
                if t < NT:
                    gate_up(n, n % 2, E)
                if t - EARLY >= X2_LAG:
                    turn_x2(t - EARLY - X2_LAG)
                down(n - 1, (n - 1) % 2, E)
                if t + 1 < NT:
                    if t - EARLY > X2_LAG:
                        pe.wait_ge(x2T_copied, t - EARLY - X2_LAG)
                    turn_norm(n + SHARED + 1, (n + 1) % 2)
            for p in range(NT - EARLY - X2_LAG + 1, NT // 2):
                turn_x2(p)

            def project(b, e):
                banks = [work[0], work[1], work[2]] if e == 0 else [work[3], flat[0], flat[1]]
                if b:
                    pe.wait_ge(vh_done[e], b)
                for w in (1, 2, 0):
                    for c in range(DC):
                        ins = pe.matmul(banks[w][:, 0:S], wqkvT[:, w, c, e * P:(e + 1) * P],
                                        x2T[:, c, b * S:(b + 1) * S], start=(c == 0), stop=(c == DC - 1))
                    ins.then_inc(qkv_done[e], 1)

            pe.wait_ge(x2T_copied, NT // 2)
            project(0, 0)
            project(0, 1)
            pe.wait_ge(y_out, NT + JOBS)
            for b in range(B):
                m = b % 2
                for e in range(2):
                    pe.wait_ge(vh_done[e], b + 1)
                for jj in range(2):
                    if b:
                        pe.wait_ge(f_used, 2 * b)
                    for x in range(2):
                        for e in range(2):
                            j = 2 * jj + x
                            ins = pe.matmul(mflat[jj][:, x * D:(x + 1) * D], vh[:, m, e, j * P:(j + 1) * P], wofT[:, 0, e],
                                            start=(e == 0), stop=(e == 1))
                    ins.then_inc(o_done, 1)
                if b + 1 < B:
                    project(b + 1, 0)
                for jj in range(2):
                    pe.wait_ge(xn3_ready, NJ * b + 2 * jj + 2)
                    pe.wait_ge(o_used, NJ * b + 2 * jj + 2)
                    for x in range(2):
                        for c in range(DC):
                            ins = pe.transpose(mflat[jj][:, (x * DC + c) * P:(x * DC + c + 1) * P],
                                               xn3[:, m, 2 * jj + x, c * P:(c + 1) * P], ident[:])
                    ins.then_inc(t3_done, 1)
                if b + 1 < B:
                    project(b + 1, 1)
                for jj in range(2):
                    pe.wait_ge(x3T_copied, 2 * b + jj + 1)
                    for x in range(2):
                        for c in range(DC):
                            ins = pe.matmul(mflat[jj][:, x * D:(x + 1) * D], x3T[:, m, 2 * jj + x, c * P:(c + 1) * P],
                                            wofT[:, 1, c], start=(c == 0), stop=(c == DC - 1))
                    ins.then_inc(f_done, 1)


_INS = ["L0_attn_x", "L0_attn_Wq", "L0_attn_Wk", "L0_attn_Wv", "L0_attn_Wo", "L0_attn_betas", "L0_ffn_router_w",
        "L0_ffn_w_gate_up", "L0_ffn_w_down", "L0_ffn_shared_gate_up", "L0_ffn_shared_down", "L1_attn_Wq",
        "L1_attn_Wk", "L1_attn_Wv", "L1_attn_Wo", "L1_ffn_weight", "L1_ffn_scale_weight", "L1_ffn_bias"]
_OUTS = [((B, S, D), "float32")]


def kernel(**inputs):
    import numpy as _np
    import concourse.bacc as _bacc
    from concourse import mybir as _mybir
    from concourse.bass_utils import run_bass_kernel_spmd as _run

    nc = _bacc.Bacc("TRN2", target_bir_lowering=False, num_devices=1)
    arrays, dram = {}, {}
    for name in _INS:
        a = _np.ascontiguousarray(inputs[name])
        arrays[f"in_{name}_dram"] = a
        dram[name] = nc.dram_tensor(f"in_{name}_dram", a.shape, _mybir.dt.from_np(a.dtype), kind="ExternalInput").ap()
    (shape, dtype), = _OUTS
    out = nc.dram_tensor("out_0_dram", shape, _mybir.dt.from_np(_np.dtype(dtype)), kind="ExternalOutput").ap()
    sandwich(nc, dram, out)
    return _run(nc, [arrays], core_ids=[0]).results[0]["out_0_dram"]
```

```python
from contextlib import ExitStack

import concourse.bass as bass
from concourse import mybir

P = 128
B, S, D = 4, 512, 256
H, DK, SEG = 16, 128, 64
NSEG = S // SEG
NJ = S // P
NT = B * NJ
DC = D // P
MEM = DK + 1
EPS = 1e-5
E, F = 8, 512
FC = F // P
JOBS = NT + E - 1
EARLY = 3 * NT // 8
LATE = EARLY + JOBS
LNS = 4 * NJ + 3 * B
DENOM = float(D) ** 0.5 / S
SCALE = float(DK) ** -0.5
MASKED = -1e30

ALU = mybir.AluOpType
ACT = mybir.ActivationFunctionType
AX = mybir.AxisListType
F32 = mybir.dt.float32
ds = bass.ds


QK_AT = [0, 1, 2, 4]
SC_AT = [1, 3, 5, 6]
V_AT = [5, 5, 6, 6]
PT_AT = [3, 7, 7, 7]
SUM_AT = [3, 4, 6, 7]
BEHIND = ["PT", "Wo", "attT", "PV"]


def step_products(i):
    names = []
    for kinds, at in ((("q", "k"), QK_AT), (("sk", "sc"), SC_AT), (("V",), V_AT), (("PT",), PT_AT)):
        names += [(kind, b) for b in range(B) if at[b] == i for kind in kinds]
    if i == 1:
        names += [("Wo",)]
    names += [("PV", (i - 1) // 2) if i % 2 else ("attT", (i - 2) // 2 if i else NJ - 1)]
    return [n for n in names if n[0] not in BEHIND], [n for n in names if n[0] in BEHIND]


def in_body(n, name):
    if name[0] in ("q", "k", "sk", "sc", "V", "PT"):
        return n + 1 < H
    if name == ("Wo",) or name == ("attT", NJ - 1):
        return n >= 1
    return 0 <= n < H


def plan_banks():
    full = [name for i in range(NSEG) for names in step_products(i) for name in names]
    used, turn, bank = [0] * 4, {}, {}
    for n in range(-1, H + 1):
        for at, name in enumerate(full):
            if in_body(n, name):
                bank[name] = at % 4
                turn[n, name] = used[at % 4]
                used[at % 4] += 1
    return bank, turn, [sum(at % 4 == k for at in range(len(full))) for k in range(4)]


class Body:
    BANK, TURN, USES = plan_banks()

    def __init__(self, first, loop=None):
        self.first, self.loop = first, loop
        self.par = first % 2
        self.chain = loop is not None or 0 <= first < H
        self.heads_on = loop is not None or first + 1 < H
        self.tail = loop is not None or first >= 1

    def makes(self, name):
        return in_body(self.first, name)

    def count(self, per_body, c=0):
        v = per_body * self.first + c
        return v if self.loop is None else v + 2 * per_body * self.loop

    def turn(self, name, back=0):
        v = self.TURN[self.first - back, name]
        if self.loop is None:
            return v
        uses = self.USES[self.BANK[name]]
        assert v + uses == self.TURN[self.first - back + 1, name]
        return v + 2 * uses * self.loop


def sandwich(nc, dram, out):
    with ExitStack() as ctx:
        def sb(name, shape, dt=F32):
            return ctx.enter_context(nc.sbuf_tensor(name, shape, dt))

        def sem(name):
            return ctx.enter_context(nc.semaphore(name))

        def sems(name, n):
            return [sem(f"{name}{i}") for i in range(n)]

        work = [ctx.enter_context(nc.psum_tensor(f"work{i}", [P, 512], F32)) for i in range(4)]
        readp = [ctx.enter_context(nc.psum_tensor(f"readp{i}", [P, 2, 256], F32)) for i in range(2)]
        memp = [ctx.enter_context(nc.psum_tensor(f"memp{i}", [P, 2, 256], F32)) for i in range(2)]

        ident = sb("ident", [P, P])
        mask = sb("mask", [P, SEG])
        seed_l = sb("seed_l", [P, P])
        seed_r = sb("seed_r", [P, 2, MEM])
        stats = sb("stats", [P, NT, 6])
        mv = sb("mv", [P, NT, 2])
        vareps = sb("vareps", [P, NT])
        rstd = sb("rstd", [P, NT])
        minushalf = sb("minushalf", [P, NJ])
        rden = sb("rden", [P, 2, B])
        rowmax = sb("rowmax", [P, 2, NJ])
        rowsum = sb("rowsum", [P, B, NJ])
        rinv = sb("rinv", [P, 2, B, NJ])
        wqkv = sb("wqkv", [P, 2, 3, DC, DK])
        mem = sb("mem", [P, B, MEM + 1])
        delta = sb("delta", [P, B, MEM + 1])
        Y = sb("Y", [P, H, D])
        ARENA = 45568
        arena = sb("arena", [P, ARENA])
        at = [0]

        def carve(*shape):
            n = 1
            for x in shape:
                n *= x
            v = arena[:, at[0]:at[0] + n]
            at[0] += n
            assert at[0] <= ARENA
            if len(shape) == 1:
                return v
            names = "abcd"[:len(shape)]
            return v.rearrange(f"p ({' '.join(names)}) -> p {' '.join(names)}", **dict(zip(names, shape)))

        xT = carve(DC, B, S)
        raw = carve(2, B, S)
        plus1 = carve(2, S)
        sqk = carve(2, B, NSEG, P)
        skt = carve(2, B, NJ, P)
        vb = carve(2, B, NJ, P)
        v1 = carve(2, B, NJ, P)
        pt = carve(2, B, NJ, P)
        pbd = carve(B, NJ, P)
        sm = carve(2, NJ, SEG)
        fromm = carve(2, B, P)
        attT = carve(B, NJ, P)
        bB = carve(H * P)
        wo = carve(H, D)
        xin = sqk[:, 1].rearrange("p b s c -> p (b s c)").rearrange("p (b j d) -> p b j d", b=B, j=NJ)
        xnorm = raw.rearrange("p a b s -> p (a b s)").rearrange("p (b j d) -> p b j d", b=B, j=NJ)
        braw = skt[:, 1].rearrange("p b j c -> p (b j c)")
        b1 = vb[:, 1].rearrange("p b j c -> p (b j c)")

        at[0] = 0
        x1 = carve(NT, D)
        lnst = carve(4, 6)
        lnm = carve(LNS * 4, 2)
        lnv = carve(LNS * 4)
        lnr = carve(LNS * 4)
        behind_x1 = at[0]
        wgu = carve(E + 1, DC, 2 * F)
        wdn = carve(E + 1, FC, D)
        shared = carve(NT, D)
        xrow = carve(2, D)
        xj = carve(2, D)
        hrow = carve(2, F)
        sgate = carve(2, F)
        hcol = carve(2, F)
        yj = carve(2, D)
        tri = carve(P)
        ones = carve(P)
        rwT = carve(DC, E)
        rwraw = carve(D)
        onehot = carve(NT, E)
        down8 = carve(E)
        logit = carve(NT, E)
        istop = carve(NT, E)
        toplogit = carve(NT)
        chosen = carve(NT)
        gate = carve(NT)
        before = carve(NT, E)
        total = carve(E, NT)
        running = carve(E, NT)
        resets = carve(E, NT)
        count8 = carve(E)
        tiles8 = carve(E)
        tilesf = carve(E)
        ends = carve(E)
        starts = carve(E)
        posf = carve(NT)
        pos = carve(NT)
        jobno = carve(JOBS + 1)
        later = carve(JOBS + 1, E)
        jobe = carve(JOBS + 1)
        jobi = carve(JOBS + 1)
        wqkvT = wqkv[:].rearrange("p a b c d -> p (a b c d)").rearrange("p (w c d) -> p w c d", w=3, c=DC)
        wofT = carve(2, DC, D)
        bias = carve(D)
        wscale = carve(DC)
        l1raw = shared.rearrange("p t d -> p (t d)")[:, 0:5 * DC * D].rearrange("p (w c d) -> p w c d", w=5, c=DC)
        at[0] = behind_x1
        x2T = carve(DC, B * S)
        x2n = carve(2, NJ, D)
        x3 = carve(2, NJ, D)
        xn3 = carve(2, NJ, D)
        x3T = carve(2, NJ, D)
        kbuf = carve(2, S)
        kv = carve(2, S)
        kvt = carve(2, S)
        vh = carve(2, DC, S)
        lnout = carve(2, NJ, D)
        x4 = carve(2, NJ, D)
        xs_d = nc.dram_tensor("rows_by_expert", [JOBS * P, D], F32).ap()
        ys_d = nc.dram_tensor("outputs_by_expert", [JOBS * P, D], F32).ap()
        x2_d = nc.dram_tensor("residual", [B * S, D], F32).ap()

        loaded_x = sems("loaded_x", B)
        loaded_beta = sem("loaded_beta")
        consts = sem("consts")
        beta_e = sem("beta_e")
        beta_step = sem("beta_step")
        x_stats = sem("x_stats")
        x_var = sem("x_var")
        x_rstd = sem("x_rstd")
        x_normed = sem("x_normed")
        xT_written = sems("xT_written", 4)
        xT_copied = sem("xT_copied")
        w_loaded = sems("w_loaded", 2)
        wo_loaded = sem("wo_loaded")
        vb_ready = sem("vb_ready")
        filled = sems("filled", 4)
        freed = sems("freed", 4)
        proj_done = sem("proj_done")
        raw_ready = sem("raw_ready")
        plus1_done = sem("plus1_done")
        sigma_done = sem("sigma_done")
        max_ready = sem("max_ready")
        score_shifted = sem("score_shifted")
        probs_ready = sem("probs_ready")
        sum_ready = sem("sum_ready")
        rinv_ready = sem("rinv_ready")
        mem_written = sems("mem_written", 2)
        mem_copied = sems("mem_copied", 2)
        read_done = sems("read_done", 2)
        rden_ready = sems("rden_ready", 2)
        fromm_ready = sems("fromm_ready", 2)
        delta_ready = sems("delta_ready", 2)
        att_ready = sem("att_ready")
        attn_done = sem("attn_done")

        x_v = dram["L0_attn_x"].rearrange("b (j p) d -> b p j d", p=P)
        w_v = [dram[f"L0_attn_W{c}"].rearrange("(c p) n -> p c n", p=P) for c in "qkv"]
        wo_v = dram["L0_attn_Wo"].rearrange("(c p) n -> p c n", p=P)
        beta_v = dram["L0_attn_betas"].rearrange("a h b d -> (a h b) d").rearrange("h d -> (h d)")

        xs_zeroed = sem("xs_zeroed")
        small_loaded = sem("small_loaded")
        l1_loaded = sem("l1_loaded")
        shared_loaded = sem("shared_loaded")
        experts_loaded = sem("experts_loaded")
        post_consts = sem("post_consts")
        ln_step = sem("ln_step")
        ln_var = sem("ln_var")
        ln_rstd = sem("ln_rstd")
        x1_ready = sem("x1_ready")
        l1_turned = sem("l1_turned")
        l1_copied = sem("l1_copied")
        wscaled = sem("wscaled")
        xrow_ready = sem("xrow_ready")
        x_turned = sem("x_turned")
        xj_copied = sem("xj_copied")
        x_used = sem("x_used")
        xn1_ready = sem("xn1_ready")
        pair_turned = sem("pair_turned")
        pair_copied = sem("pair_copied")
        pair_used = sem("pair_used")
        ranks_copied = sem("ranks_copied")
        top_done = sem("top_done")
        gate_exp = sem("gate_exp")
        route_step = sem("route_step")
        onehot_ready = sem("onehot_ready")
        ranks_done = sem("ranks_done")
        xs_ready = sem("xs_ready")
        xs_scattered = sem("xs_scattered")
        silu_done = sem("silu_done")
        h_ready = sem("h_ready")
        hT_turned = sem("hT_turned")
        hT_copied = sem("hT_copied")
        down_done = sem("down_done")
        y_out = sem("y_out")
        x2_stored = sem("x2_stored")
        xn2_ready = sem("xn2_ready")
        x2_turned = sem("x2_turned")
        x2T_copied = sem("x2T_copied")
        o_done = sem("o_done")
        o_used = sem("o_used")
        x3_ready = sem("x3_ready")
        xn3_ready = sem("xn3_ready")
        t3_done = sem("t3_done")
        x3T_copied = sem("x3T_copied")
        f_done = sem("f_done")
        f_used = sem("f_used")
        x4_ready = sem("x4_ready")
        kv_step = sem("kv_step")
        x1_loaded = sems("x1_loaded", NJ)
        xs_loaded = sems("xs_loaded", 2)
        y_stored = sems("y_stored", 2)
        y_gathered = sems("y_gathered", NT // 2)
        x2n_loaded = sems("x2n_loaded", 2)
        k_copied = sems("k_copied", 2)
        qkv_done = sems("qkv_done", 2)
        vh_done = sems("vh_done", 2)
        x4_stored = sems("x4_stored", 2)

        by_head = "b (i h r) d -> h (b i) r d"
        x_h = dram["L0_attn_x"].rearrange(by_head, h=H, r=4)
        x2_h = x2_d.rearrange("(g h r) d -> h g r d", h=H, r=4)
        flat = [readp[r][:].rearrange("p a c -> p (a c)") for r in range(2)]
        mflat = [memp[r][:].rearrange("p a c -> p (a c)") for r in range(2)]
        posi = pos.bitcast(mybir.dt.uint32)
        ffn_banks = [work[3], flat[0]]

        X2_FROM = 2
        X2_LAG = X2_FROM + 3

        def late_groups():
            for i in range(NT // 2 + 1):
                if i:
                    yield "x2", i - 1
                if i < NT // 2:
                    yield "moe", i

        def slot(kind, p):
            return {"moe": 2 * NT, "x2": 3 * NT}[kind] + 2 * p

        block = ctx.enter_context(nc.Block())

        def own(i):
            return slice(SEG * (i % 2), SEG * (i % 2) + SEG)

        def sigma_places(m, b, qk):
            pairs = sqk[:, m, b].rearrange("p s c -> p (s c)").rearrange("p (j x) -> p j x", j=NJ)
            if qk:
                return pairs[:, :, SEG:3 * SEG]
            return pairs.rearrange("p j (a c) -> p j a c", a=4)[:, :, 0:4:3]

        def like(x, qk):
            x = x.rearrange("p (j x) -> p j x", j=NJ)
            return x if qk else x.rearrange("p j (a c) -> p j a c", a=2)

        def bodies(eng, body):
            body(Body(-1))
            body(Body(0))
            with eng.Fori(0, (H - 2) // 2) as turn:
                body(Body(1, turn))
                body(Body(2, turn))
            body(Body(H - 1))
            body(Body(H))

        @block.sync
        def _(sp):
            def load_w(g, par):
                for c in range(3):
                    sp.dma_start(wqkv[:, par, c], w_v[c][:, :, ds(g * DK, DK)]).then_inc(w_loaded[par], 16)

            for b in range(B):
                sp.dma_start(xin[:, b], x_v[b]).then_inc(loaded_x[b], 16)
                if b == 1:
                    load_w(0, 0)
            sp.dma_start(braw, beta_v.partition_broadcast(P)).then_inc(loaded_beta, 16)
            load_w(1, 1)
            sp.wait_ge(consts, 12)
            xs_t = xs_d.rearrange("(t p) d -> p t d", p=P)
            sp.dma_start(xs_t[:, 0:NT], Y[:]).then_inc(xs_zeroed, 16)
            sp.dma_start(xs_t[:, NT:JOBS], Y[:, 0:JOBS - NT]).then_inc(xs_zeroed, 16)
            sp.dma_start(wo, wo_v).then_inc(wo_loaded, 16)

            def load_next(g, par):
                sp.wait_ge(proj_done, g - 1)
                load_w(g, par)

            with sp.Fori(0, (H - 2) // 2) as turn:
                load_next(turn * 2 + 2, 0)
                load_next(turn * 2 + 3, 1)

            sp.wait_ge(proj_done, H)
            for t in range(NT):
                sp.dma_start(x1[:, t], x_h[t]).then_inc(x1_loaded[t // 4], 16)
            sp.wait_ge(attn_done, 1)
            sp.dma_start(rwraw[0:E, :], dram["L0_ffn_router_w"]).then_inc(small_loaded, 16)
            sp.dma_start(bias, dram["L1_ffn_bias"].partition_broadcast(P)).then_inc(small_loaded, 16)
            with nc.allow_non_contiguous_dma("256 numbers"):
                sp.dma_start(wscale, dram["L1_ffn_scale_weight"].rearrange("(c p) -> p c", p=P)).then_inc(small_loaded, 16)
            for w, name in enumerate(["L1_attn_Wq", "L1_attn_Wk", "L1_attn_Wv", "L1_attn_Wo", "L1_ffn_weight"]):
                sp.dma_start(l1raw[:, w], dram[name].rearrange("(c p) n -> p c n", p=P)).then_inc(l1_loaded, 16)
            sp.dma_start(wgu[:, E], dram["L0_ffn_shared_gate_up"].rearrange("(c p) n -> p c n", p=P))\
                .then_inc(shared_loaded, 16)
            sp.dma_start(wdn[:, E], dram["L0_ffn_shared_down"].rearrange("(c p) n -> p c n", p=P))\
                .then_inc(shared_loaded, 16)
            for e in range(E):
                sp.dma_start(wgu[:, e], dram["L0_ffn_w_gate_up"][e].rearrange("(c p) n -> p c n", p=P))\
                    .then_inc(experts_loaded, 16)
                sp.dma_start(wdn[:, e], dram["L0_ffn_w_down"][e].rearrange("(c p) n -> p c n", p=P))\
                    .then_inc(experts_loaded, 16)

            sp.wait_ge(xs_scattered, 16 * NT)

            def load_rows(j, par):
                sp.wait_ge(x_turned, j + EARLY - 1)
                sp.dma_start(xrow[:, par], xs_d[ds(j * P, P), :]).then_inc(xs_loaded[par], 16)

            with sp.Fori(0, JOBS // 2) as pair:
                load_rows(pair * 2, 0)
                load_rows(pair * 2 + 1, 1)
            load_rows(JOBS - 1, 0)

            for p in range(NT // 2):
                sp.wait_ge(x1_ready, NJ + p + 1)
                for t in (2 * p, 2 * p + 1):
                    sp.dma_start(x2_h[t], x1[:, t]).then_inc(x2_stored, 16)
            sp.wait_ge(x2_stored, 16 * NT)
            x2_v = x2_d.rearrange("(b j p) d -> b p j d", j=NJ, p=P)
            out_v = out.rearrange("b (j p) d -> b p j d", p=P)
            for b in range(2):
                sp.dma_start(x2n[:, b], x2_v[b]).then_inc(x2n_loaded[b], 16)
            for b in range(B):
                sp.wait_ge(x4_ready, b + 1)
                sp.dma_start(out_v[b], x4[:, b % 2]).then_inc(x4_stored[b % 2], 16)
                if b + 2 < B:
                    sp.dma_start(x2n[:, b % 2], x2_v[b + 2]).then_inc(x2n_loaded[b % 2], 16)
            for par in range(2):
                sp.wait_ge(x4_stored[par], 16 * (B // 2))

        @block.gpsimd
        def _(pool):
            pool.memset(ident[:], 0.0).then_inc(consts, 1)
            pool.memset(mask[:], 0.0).then_inc(consts, 1)
            pool.memset(seed_l[:], 1.0 / (DK * P)).then_inc(consts, 1)
            pool.memset(seed_r[:], 0.0).then_inc(consts, 1)
            pool.memset(minushalf[:], -0.5).then_inc(consts, 1)
            pool.memset(delta[:], 1.0).then_inc(consts, 1)
            pool.memset(Y[:], 0.0).then_inc(consts, 1)
            pool.memset(pbd, 0.0).then_inc(consts, 1)
            pool.wait_ge(consts, 8)
            pool.affine_select(out=ident[:], in_=ident[:], compare_op=ALU.not_equal, fill=1.0, base=0,
                               pattern=[[-1, P]], channel_multiplier=1).then_inc(consts, 1)
            for half in range(2):
                pool.wait_ge(consts, 9 + half)
                pool.affine_select(out=mask[SEG * half:SEG * half + SEG, :], in_=mask[SEG * half:SEG * half + SEG, :],
                                   compare_op=ALU.is_ge, fill=MASKED, base=0,
                                   pattern=[[-1, SEG]], channel_multiplier=1).then_inc(consts, 1)
            pool.wait_ge(consts, 11)
            pool.memset(seed_r[:, :, DK:MEM], 1.0).then_inc(consts, 1)
            for b in range(B):
                pool.wait_ge(x_var, b + 1)
                pool.tensor_tensor(rstd[:, b * NJ:(b + 1) * NJ], vareps[:, b * NJ:(b + 1) * NJ], minushalf[:],
                                   ALU.pow).then_inc(x_rstd, 1)

            def body(n):
                if not n.heads_on:
                    return
                for b in range(B):
                    for qk in range(2):
                        t = 2 * b + qk
                        pool.wait_ge(raw_ready, n.count(2 * B, 2 * B + t + 1))
                        if n.first >= 0 or t >= 2:
                            pool.wait_ge(sigma_done, n.count(2 * B, 2 * B + t - 1))
                        pool.tensor_tensor(plus1[:, t % 2], raw[:, qk, b], seed_r[:, 0, DK:MEM].to_broadcast([P, S]),
                                           ALU.add).then_inc(plus1_done, 1)

            pool.wait_ge(consts, 12)
            bodies(pool, body)

            groups = [0]

            def rstds(k, n=4):
                groups[0] += 1
                pool.wait_ge(ln_var, groups[0])
                pool.tensor_tensor(lnr[:, k:k + n], lnv[:, k:k + n], minushalf[:, 0:n], ALU.pow).then_inc(ln_rstd, 1)

            for base in (0, NT):
                for g in range(NJ - 1):
                    rstds(base + 4 * g)
            pool.wait_ge(attn_done, 1)
            pool.memset(tri, 1.0).then_inc(post_consts, 1)
            pool.memset(ones, 1.0).then_inc(post_consts, 1)
            pool.memset(resets, 1.0).then_inc(post_consts, 1)
            pool.iota(chosen[:, 0:E].bitcast(mybir.dt.int32), [[-1, E]], base=E,
                      channel_multiplier=0).then_inc(post_consts, 1)
            pool.iota(jobi.bitcast(mybir.dt.int32), [[1, JOBS + 1]], base=0, channel_multiplier=0).then_inc(post_consts, 1)
            pool.wait_ge(post_consts, 5)
            pool.tensor_copy(down8, chosen[:, 0:E].bitcast(mybir.dt.int32)).then_inc(post_consts, 1)
            pool.tensor_copy(jobno, jobi.bitcast(mybir.dt.int32)).then_inc(post_consts, 1)
            pool.memset(resets[:, :, 0], 0.0).then_inc(post_consts, 1)
            pool.affine_select(out=tri, in_=tri, compare_op=ALU.is_ge, fill=0.0, base=-1,
                               pattern=[[1, P]], channel_multiplier=-1).then_inc(post_consts, 1)

            for base in (0, NT):
                rstds(base + 4 * (NJ - 1))
            pool.wait_ge(xs_zeroed, 32)
            for t in range(NT):
                pool.wait_ge(xs_ready, t + 1)
                pool.indirect_dma_start(out=xs_d, out_offset=bass.IndirectOffsetOnAxis(posi[:, t:t + 1], 0),
                                        in_=Y[:, t], in_offset=None).then_inc(xs_scattered, 16)

            def store_y(j, par):
                pool.wait_ge(y_out, j + EARLY + 1)
                pool.dma_start(ys_d[ds(j * P, P), :], yj[:, par]).then_inc(y_stored[par], 16)

            with pool.Fori(0, JOBS // 2) as pair:
                store_y(pair * 2, 0)
                store_y(pair * 2 + 1, 1)
            store_y(JOBS - 1, 0)
            pool.wait_ge(y_stored[0], 16 * ((JOBS + 1) // 2))
            pool.wait_ge(y_stored[1], 16 * (JOBS // 2))
            for t in range(NT):
                pool.indirect_dma_start(out=Y[:, t], out_offset=None, in_=ys_d,
                                        in_offset=bass.IndirectOffsetOnAxis(posi[:, t:t + 1], 0))\
                    .then_inc(y_gathered[t // 2], 16)
            for kind, p in late_groups():
                rstds(slot(kind, p), 2)
            for k in range(4 * NT, 4 * LNS, 4):
                rstds(k)

        @block.vector
        def _(dve):
            def apply_norm(b):
                dve.wait_ge(x_rstd, b + 1)
                for j in range(NJ):
                    t = b * NJ + j
                    dve.tensor_scalar(xnorm[:, b, j], xin[:, b, j], mv[:, t, 0:1], rstd[:, t:t + 1],
                                      ALU.subtract, ALU.mult).then_inc(x_normed, 1)

            for b in range(B):
                dve.wait_ge(loaded_x[b], 16)
                for j in range(NJ):
                    dve.bn_stats(stats[:, b * NJ + j], xin[:, b, j]).then_inc(x_stats, 1)
                for j in range(NJ):
                    t = b * NJ + j
                    dve.wait_ge(x_stats, NJ * 2 * b + j + 1)
                    dve.bn_aggr(mv[:, t], stats[:, t]).then_inc(x_stats, 1)
                dve.wait_ge(x_stats, NJ * 2 * (b + 1))
                dve.tensor_scalar(vareps[:, b * NJ:(b + 1) * NJ], mv[:, b * NJ:(b + 1) * NJ, 1], EPS, None,
                                  ALU.add).then_inc(x_var, 1)
                if b:
                    apply_norm(b - 1)
            apply_norm(B - 1)
            dve.wait_ge(consts, 12)

            def betas(piece):
                w = slice(2 * P * piece, 2 * P * (piece + 1))
                dve.wait_ge(beta_e, 1)
                dve.tensor_scalar(b1[:, w], b1[:, w], 1.0, None, ALU.add).then_inc(beta_step, 1)
                dve.wait_ge(beta_step, 2 * piece + 1)
                dve.reciprocal(bB[:, w], b1[:, w]).then_inc(beta_step, 1)
                dve.wait_ge(beta_step, 2 * piece + 2)

            def combine(n, j, back):
                m = (n.par + back) % 2
                name = ("PV", j)
                dve.wait_ge(filled[n.BANK[name]], n.turn(name, back) + 1)
                for r in range(2):
                    dve.wait_ge(fromm_ready[r], n.count(NSEG, 2 * j + 2 - NSEG * back))
                dve.wait_ge(rinv_ready, n.count(B, B - B * back))
                w = work[n.BANK[name]]
                for b in range(B):
                    ins = dve.scalar_tensor_tensor(out=fromm[:, j % 2, b], in0=w[:, b * P:(b + 1) * P],
                                                   scalar=rinv[:, m, b, j:j + 1], in1=fromm[:, j % 2, b],
                                                   op0=ALU.mult, op1=ALU.add)
                    if b == B - 2:
                        ins.then_inc(att_ready, 1)
                ins.then_inc(freed[n.BANK[name]], 1)

            def deltas(n, i):
                o, k = own(i), own(i + 1)
                for r in range(2):
                    dve.wait_ge(read_done[r], n.count(NSEG, i + 1))
                    dve.reciprocal(rden[:, i % 2, 2 * r:2 * r + 2], readp[r][:, :, DK]).then_inc(rden_ready[r], 1)
                    if i == NSEG - 1:
                        continue
                    dve.wait_ge(rden_ready[r], n.count(NSEG, i + 1))
                    for bb in range(2):
                        b = 2 * r + bb
                        ins = dve.scalar_tensor_tensor(out=delta[o, b, 0:DK], in0=readp[r][k, bb, 0:DK],
                                                       scalar=rden[k, i % 2, b:b + 1], in1=vb[o, n.par, b, i // 2],
                                                       op0=ALU.mult, op1=ALU.subtract, reverse1=True)
                    ins.then_inc(delta_ready[r], 1)

            def scores_shift(n, b):
                name = ("sc", b)
                w = work[n.BANK[name]][:, 0:NJ * SEG].rearrange("p (j c) -> p j c", j=NJ)
                dve.wait_ge(filled[n.BANK[name]], n.turn(name) + 1)
                dve.tensor_tensor(sm[:, b % 2], w, mask[:].unsqueeze(1).to_broadcast([P, NJ, SEG]),
                                  ALU.add).then_inc(freed[n.BANK[name]], 1)
                dve.wait_ge(freed[n.BANK[name]], n.turn(name) + 1)
                dve.tensor_reduce(rowmax[:, b % 2], sm[:, b % 2], AX.X, ALU.max).then_inc(max_ready, 1)
                dve.wait_ge(max_ready, n.count(B, B + b + 1))
                dve.tensor_tensor(sm[:, b % 2], sm[:, b % 2],
                                  rowmax[:, b % 2].unsqueeze(2).to_broadcast([P, NJ, SEG]),
                                  ALU.subtract).then_inc(score_shifted, 1)

            def row_sums(n, b):
                dve.wait_ge(probs_ready, n.count(B, B + b + 1))
                dve.tensor_reduce(rowsum[:, b], pbd[:, b], AX.X, ALU.add).then_inc(sum_ready, 1)
                dve.wait_ge(sum_ready, n.count(B, B + b + 1))
                dve.reciprocal(rinv[:, 1 - n.par, b], rowsum[:, b]).then_inc(rinv_ready, 1)

            def values(n, b):
                name = ("V", b)
                g = n.first + 1 if n.loop is None else n.first + 1 + 2 * n.loop
                w = work[n.BANK[name]][:].rearrange("p (j c) -> p j c", j=NJ)
                dve.wait_ge(filled[n.BANK[name]], n.turn(name) + 1)
                dve.tensor_tensor(vb[:, 1 - n.par, b], w, bB[:, ds(g * P, P)].unsqueeze(1).to_broadcast([P, NJ, P]),
                                  ALU.mult).then_inc(vb_ready, 1)
                dve.wait_ge(vb_ready, n.count(B, B + b + 1))
                dve.tensor_tensor(v1[:, 1 - n.par, b], w, vb[:, 1 - n.par, b], ALU.subtract).then_inc(freed[n.BANK[name]], 1)

            def sigmas(n, b):
                for qk in range(2):
                    t = 2 * b + qk
                    name = ("qk"[qk], b)
                    dve.wait_ge(freed[n.BANK[name]], n.turn(name) + 1)
                    dve.wait_ge(plus1_done, n.count(2 * B, 2 * B + t + 1))
                    y = sigma_places(1 - n.par, b, qk)
                    more = like(plus1[:, t % 2], qk)
                    for a, c in [(y, more)] if qk else [(y[:, :, e], more[:, :, e]) for e in range(2)]:
                        ins = dve.scalar_tensor_tensor(out=a, in0=a, scalar=1.0, in1=c, op0=ALU.min, op1=ALU.max)
                    ins.then_inc(sigma_done, 1)

            def body(n):
                for i in range(NSEG):
                    if i % 2 == 0:
                        if i == 0 and n.tail:
                            combine(n, NJ - 1, 1)
                        elif i and n.chain:
                            combine(n, (i - 2) // 2, 0)
                    if n.chain:
                        deltas(n, i)
                    for b in range(B):
                        if n.heads_on and SC_AT[b] == i:
                            scores_shift(n, b)
                    if n.first == -1 and i:
                        betas(i - 1)
                    elif n.first == 0 and i == 0:
                        betas(H // 2 - 1)
                    for b in range(B):
                        if n.heads_on and V_AT[b] == i:
                            values(n, b)
                    for b in range(B):
                        if n.heads_on and SUM_AT[b] == i:
                            row_sums(n, b)
                    for b in range(B):
                        if n.heads_on and QK_AT[b] == i:
                            sigmas(n, b)

            bodies(dve, body)

            dve.wait_ge(freed[Body.BANK["Wo",]], Body(H - 1).turn(("Wo",)) + 1)
            done = [0, 0, 0]

            def step(ins):
                done[0] += 1
                ins.then_inc(ln_step, 1)

            def ln_stats(tiles, k=None, n=4):
                if k is None:
                    k = done[2]
                    done[2] += n
                for x in range(n):
                    step(dve.bn_stats(lnst[:, x], tiles[:, x]))
                for x in range(n):
                    dve.wait_ge(ln_step, done[0] - n + 1)
                    step(dve.bn_aggr(lnm[:, k + x], lnst[:, x]))
                dve.wait_ge(ln_step, done[0])
                dve.tensor_scalar(lnv[:, k:k + n], lnm[:, k:k + n, 1], EPS, None, ALU.add).then_inc(ln_var, 1)
                done[1] += 1
                return k, done[1]

            def ln_apply(to, tiles, stats, signal=None, n=4):
                k, count = stats
                dve.wait_ge(ln_rstd, count)
                for x in range(n):
                    ins = dve.tensor_scalar(to[:, x], tiles[:, x], lnm[:, k + x, 0:1],
                                            lnr[:, k + x:k + x + 1], ALU.subtract, ALU.mult)
                    if signal is not None:
                        ins.then_inc(signal, 1)
                    elif x == n - 1:
                        step(ins)

            def group(a, g):
                return a[:, 4 * g:4 * g + 4]

            of_y = [ln_stats(group(Y, g), 4 * g) for g in range(NJ - 1)]
            of_x1 = []

            def make_x1(g):
                dve.wait_ge(x1_loaded[g], 64)
                ln_apply(group(Y, g), group(Y, g), of_y[g])
                dve.wait_ge(ln_step, done[0])
                dve.tensor_tensor(group(x1, g), group(x1, g), group(Y, g), ALU.add).then_inc(x1_ready, 1)
                dve.wait_ge(x1_ready, g + 1)
                of_x1.append(ln_stats(group(x1, g), NT + 4 * g))

            def norm_x1(g):
                ln_apply(group(Y, g), group(x1, g), of_x1[g], xn1_ready)

            for g in range(NJ - 1):
                make_x1(g)
                if g:
                    norm_x1(g - 1)
            dve.wait_ge(attn_done, 1)
            of_y.append(ln_stats(group(Y, NJ - 1), 4 * (NJ - 1)))
            norm_x1(NJ - 2)
            make_x1(NJ - 1)
            norm_x1(NJ - 1)
            dve.wait_ge(l1_loaded, 16 * 5)
            dve.wait_ge(small_loaded, 48)
            for c in range(DC):
                dve.tensor_scalar(l1raw[:, 4, c], l1raw[:, 4, c], wscale[:, c:c + 1], None, ALU.mult).then_inc(wscaled, 1)

            def norm_row(u, t, par):
                if not (isinstance(u, int) and u < 2):
                    dve.wait_ge(x_turned, u - 1)
                dve.tensor_scalar(xrow[:, par], x1[:, ds(t, 1)].rearrange("p a d -> p (a d)"),
                                  lnm[:, ds(t + 4 * NJ, 1), 0], lnr[:, ds(t + 4 * NJ, 1)],
                                  ALU.subtract, ALU.mult).then_inc(xrow_ready, 1)

            norm_row(0, 0, 0)
            norm_row(1, 1, 1)
            dve.wait_ge(post_consts, 9)

            def hidden(n, par):
                dve.wait_ge(silu_done, n + 1)
                dve.tensor_tensor(hrow[:, par], sgate[:, par], work[2 * par + 1][:], ALU.mult).then_inc(h_ready, 1)

            r = [0]

            def chain(ins):
                r[0] += 1
                ins.then_inc(route_step, 1)
                dve.wait_ge(route_step, r[0])

            def wide(a, n, axis):
                shape = [P, E, n] if axis == 2 else [P, n, E]
                return a.unsqueeze(axis).to_broadcast(shape)

            dve.wait_ge(pair_used, NT // 2)
            chain(dve.tensor_copy(logit.rearrange("p t e -> p (t e)"), mflat[0][:, 0:NT * E]))
            dve.tensor_reduce(toplogit, logit, AX.X, ALU.max).then_inc(top_done, 1)
            dve.wait_ge(top_done, 1)
            chain(dve.tensor_tensor(istop, logit, toplogit.unsqueeze(2).to_broadcast([P, NT, E]), ALU.is_equal))
            chain(dve.tensor_tensor(istop, istop, wide(down8, NT, 1), ALU.mult))
            chain(dve.tensor_reduce(chosen, istop, AX.X, ALU.max))
            dve.tensor_tensor(onehot, wide(down8, NT, 1), chosen.unsqueeze(2).to_broadcast([P, NT, E]),
                              ALU.is_equal).then_inc(onehot_ready, 1)
            dve.wait_ge(ranks_done, 2)
            dve.tensor_copy(total, mflat[1][:, 0:NT * E].rearrange("p (t e) -> p e t", e=E)).then_inc(ranks_copied, 1)
            dve.tensor_copy(before, mflat[0][:, 0:NT * E].rearrange("p (t e) -> p t e", e=E)).then_inc(ranks_copied, 1)
            hidden(0, 0)
            norm_row(2, 2, 0)
            dve.wait_ge(gate_exp, 1)
            chain(dve.tensor_scalar(gate, gate, 1.0, None, ALU.add))
            chain(dve.reciprocal(gate, gate))
            chain(dve.tensor_tensor(gate, gate, lnr[:, 4 * NJ:8 * NJ], ALU.mult))
            dve.wait_ge(onehot_ready, 1)
            dve.wait_ge(ranks_copied, 2)
            line = "p e t -> p (e t)"
            chain(dve.tensor_tensor_scan(running.rearrange(line), resets.rearrange(line), total.rearrange(line), 0.0,
                                         ALU.mult, ALU.add))
            chain(dve.tensor_copy(count8, running[:, :, NT - 1]))
            chain(dve.tensor_tensor(running, running, total, ALU.subtract))
            ti = tiles8.bitcast(mybir.dt.int32)
            chain(dve.tensor_scalar(ti, count8, float(P - 1), None, ALU.add))
            chain(dve.tensor_scalar(ti, ti, 7, None, ALU.arith_shift_right))
            chain(dve.tensor_copy(tilesf, ti))
            chain(dve.tensor_tensor_scan(ends, ones[:, 0:E], tilesf, 0.0, ALU.mult, ALU.add))
            chain(dve.tensor_tensor(starts, ends, tilesf, ALU.subtract))
            chain(dve.tensor_scalar(starts, starts, float(P), None, ALU.mult))
            chain(dve.tensor_tensor(running, running, wide(starts, NT, 2), ALU.add))
            chain(dve.tensor_tensor(before, before, running.rearrange("p e t -> p t e"), ALU.add))
            chain(dve.tensor_tensor(before, before, onehot, ALU.mult))
            chain(dve.tensor_reduce(posf, before, AX.X, ALU.add))
            chain(dve.tensor_copy(posi, posf))
            hidden(1, 1)
            norm_row(3, 3, 1)
            for t in range(NT):
                dve.tensor_scalar(Y[:, t], x1[:, t], lnm[:, 4 * NJ + t, 0:1], gate[:, t:t + 1],
                                  ALU.subtract, ALU.mult).then_inc(xs_ready, 1)
            hidden(2, 0)
            norm_row(4, 4, 0)
            chain(dve.tensor_tensor(later, jobno.unsqueeze(2).to_broadcast([P, JOBS + 1, E]), wide(ends, JOBS + 1, 1),
                                    ALU.is_ge))
            chain(dve.tensor_reduce(jobe, later, AX.X, ALU.add))
            chain(dve.tensor_scalar(jobi.bitcast(mybir.dt.int32), jobe, float(E - 1), None, ALU.min))

            for n in range(3, EARLY):
                hidden(n, n % 2)
                if n + 2 < EARLY:
                    norm_row(n + 2, n + 2, n % 2)
            with dve.Fori(0, JOBS // 2) as pair:
                for par in range(2):
                    hidden(pair * 2 + (EARLY + par), par)
            norm_row(LATE, EARLY, LATE % 2)
            hidden(LATE - 1, 0)

            def two(a, p):
                return a[:, 2 * p:2 * p + 2]

            stats_of = {}

            def moe_sum(p):
                dve.wait_ge(y_gathered[p], 32)
                dve.wait_ge(y_out, 2 * p + 2 if 2 * p < EARLY else 2 * p + 2 + JOBS)
                step(dve.tensor_tensor(two(Y, p), two(Y, p), two(shared, p), ALU.add))
                dve.wait_ge(ln_step, done[0])
                stats_of["moe", p] = ln_stats(two(Y, p), slot("moe", p), 2)

            def make_x2(p):
                ln_apply(two(Y, p), two(Y, p), stats_of["moe", p], n=2)
                dve.wait_ge(ln_step, done[0])
                dve.tensor_tensor(two(x1, p), two(x1, p), two(Y, p), ALU.add).then_inc(x1_ready, 1)
                dve.wait_ge(x1_ready, NJ + p + 1)
                stats_of["x2", p] = ln_stats(two(x1, p), slot("x2", p), 2)

            def norm_x2(p):
                ln_apply(two(Y, p), two(x1, p), stats_of["x2", p], xn2_ready, 2)

            def x2_work(i):
                for lag, what in ((2, norm_x2), (1, make_x2), (0, moe_sum)):
                    if 0 <= i - lag < NT // 2:
                        what(i - lag)

            for t in range(EARLY, NT):
                n = t + JOBS
                if t + 1 < NT:
                    norm_row(n + 1, t + 1, (n + 1) % 2)
                hidden(n, n % 2)
                if t >= EARLY + X2_FROM:
                    x2_work(t - EARLY - X2_FROM)
            for i in range(NT - EARLY - X2_FROM, NT // 2 + 2):
                x2_work(i)
            done[2] = 4 * NT

            def running_sums(b, e):
                dve.wait_ge(k_copied[e], b + 1)
                dve.wait_ge(qkv_done[e], 3 * b + 2)
                qb, kb, vbk = (work[0:3] if e == 0 else [work[3], flat[0], flat[1]])
                dve.tensor_tensor(kv[:, e], kbuf[:, e], vbk[:, 0:S], ALU.mult).then_inc(kv_step, 1)
                dve.wait_ge(kv_step, 2 * (2 * b + e) + 1)
                dve.tensor_tensor_scan(kvt[:, e], ones[:, 0:1].to_broadcast([P, S]), kv[:, e], 0.0,
                                       ALU.mult, ALU.add).then_inc(kv_step, 1)
                dve.wait_ge(kv_step, 2 * (2 * b + e) + 2)
                dve.wait_ge(qkv_done[e], 3 * b + 3)
                dve.scalar_tensor_tensor(out=vh[:, b % 2, e], in0=kvt[:, e], scalar=DENOM, in1=qb[:, 0:S],
                                         op0=ALU.mult, op1=ALU.mult).then_inc(vh_done[e], 1)

            def pair(bank):
                return bank[:, 0:2 * D].rearrange("p (x d) -> p x d", x=2)

            def o_stats(b):
                k = done[2]
                for x in range(NJ):
                    if x % 2 == 0:
                        dve.wait_ge(o_done, 2 * b + x // 2 + 1)
                    step(dve.bn_stats(lnst[:, x], pair(mflat[x // 2])[:, x % 2]))
                for x in range(NJ):
                    dve.wait_ge(ln_step, done[0] - 3)
                    step(dve.bn_aggr(lnm[:, k + x], lnst[:, x]))
                dve.wait_ge(ln_step, done[0])
                dve.tensor_scalar(lnv[:, k:k + 4], lnm[:, k:k + 4, 1], EPS, None, ALU.add).then_inc(ln_var, 1)
                done[1] += 1
                done[2] += 4
                return k, done[1]

            def make_x3(b, stats):
                m = b % 2
                k, count = stats
                dve.wait_ge(ln_rstd, count)
                for x in range(NJ):
                    dve.tensor_scalar(lnout[:, m, x], pair(mflat[x // 2])[:, x % 2], lnm[:, k + x, 0:1],
                                      lnr[:, k + x:k + x + 1], ALU.subtract, ALU.mult).then_inc(o_used, 1)
                dve.wait_ge(o_used, NJ * (b + 1))
                dve.wait_ge(x2n_loaded[m], 16 * (b // 2 + 1))
                dve.tensor_tensor(x3[:, m], lnout[:, m], x2n[:, m], ALU.add).then_inc(x3_ready, 1)
                dve.wait_ge(x3_ready, b + 1)
                return ln_stats(x3[:, m])

            def ffn_stats(b):
                m = b % 2
                for jj in range(2):
                    dve.wait_ge(f_done, 2 * b + jj + 1)
                    dve.tensor_tensor(lnout[:, m, 2 * jj:2 * jj + 2], pair(ffn_banks[jj]),
                                      bias.unsqueeze(1).to_broadcast([P, 2, D]), ALU.add).then_inc(f_used, 1)
                dve.wait_ge(f_used, 2 * b + 2)
                return ln_stats(lnout[:, m])

            def make_x4(b, stats):
                m = b % 2
                ln_apply(lnout[:, m], lnout[:, m], stats)
                dve.wait_ge(ln_step, done[0])
                if b >= 2:
                    dve.wait_ge(x4_stored[m], 16 * (b // 2))
                dve.tensor_tensor(x4[:, m], lnout[:, m], x3[:, m], ALU.add).then_inc(x4_ready, 1)

            running_sums(0, 0)
            running_sums(0, 1)
            for b in range(B + 1):
                if b < B:
                    of_o = o_stats(b)
                if b and b != B - 1:
                    of_f = ffn_stats(b - 1)
                if b < B:
                    of_x3 = make_x3(b, of_o)
                if b == B - 1:
                    of_f = ffn_stats(b - 1)
                if b + 1 < B:
                    running_sums(b + 1, 0)
                if b < B:
                    ln_apply(xn3[:, b % 2], x3[:, b % 2], of_x3, xn3_ready)
                if b + 1 < B:
                    running_sums(b + 1, 1)
                if b:
                    make_x4(b - 1, of_f)

        @block.scalar
        def _(act):
            for b in range(B):
                for c in range(DC):
                    g = b * DC + c
                    act.wait_ge(xT_written[g % 4], g // 4 + 1)
                    act.copy(xT[:, c, b], work[g % 4][:]).then_inc(xT_copied, 1)
            act.wait_ge(consts, 12)

            def copy_out(n, name, dst):
                k = n.BANK[name]
                act.wait_ge(filled[k], n.turn(name) + 1)
                w = work[k][:]
                if len(dst.shape) == 3:
                    w = w.rearrange("p (j c) -> p j c", j=dst.shape[1])
                act.copy(dst, w).then_inc(freed[k], 1)

            def project_copies(n, b):
                for qk in range(2):
                    name = ("qk"[qk], b)
                    k = n.BANK[name]
                    act.wait_ge(filled[k], n.turn(name) + 1)
                    act.copy(raw[:, qk, b], work[k][:]).then_inc(raw_ready, 1)
                    act.activation(sigma_places(1 - n.par, b, qk), like(work[k][:], qk), ACT.Exp)\
                        .then_inc(freed[k], 1)

            def from_memory(n, i):
                o = own(i)
                for r in range(2):
                    act.wait_ge(rden_ready[r], n.count(NSEG, i + 1))
                    for bb in range(2):
                        b = 2 * r + bb
                        ins = act.activation(fromm[o, (i // 2) % 2, b], readp[r][o, bb, 0:DK], ACT.Copy,
                                             scale=rden[o, i % 2, b:b + 1])
                    ins.then_inc(fromm_ready[r], 1)

            def mem_copy(n, i):
                for r in range(2):
                    act.wait_ge(mem_written[r], n.count(NSEG, i + 2))
                    act.copy(mem[:, 2 * r:2 * r + 2, 0:MEM], memp[r][:, :, 0:MEM]).then_inc(mem_copied[r], 1)

            def take(n, name):
                if not n.makes(name):
                    return
                m = 1 - n.par
                kind = name[0]
                if kind == "q":
                    project_copies(n, name[1])
                elif kind == "sk":
                    copy_out(n, name, skt[:, m, name[1]])
                elif kind == "PT":
                    copy_out(n, name, pt[:, m, name[1]])
                elif kind == "attT":
                    copy_out(n, name, attT[:, :, name[1]])
                elif kind == "Wo":
                    act.wait_ge(xs_zeroed, 32)
                    act.wait_ge(filled[n.BANK[name]], n.turn(name) + 1)
                    g = n.first - 1 if n.loop is None else n.first - 1 + 2 * n.loop
                    ins = act.copy(Y[:, ds(g, 1), :].rearrange("p a d -> p (a d)"), work[n.BANK[name]][:, 0:D])
                    ins.then_inc(freed[n.BANK[name]], 1)

            def body(n):
                for i in range(NSEG):
                    before, behind = step_products(i)
                    if n.chain:
                        from_memory(n, i)
                    for name in before:
                        take(n, name)
                    for b in range(B):
                        if n.heads_on and SC_AT[b] == i:
                            act.wait_ge(score_shifted, n.count(B, B + b + 1))
                            for half in range(2):
                                o = slice(SEG * half, SEG * half + SEG)
                                ins = act.activation(pbd[o, b, :, SEG * half:SEG * half + SEG], sm[o, b % 2], ACT.Exp,
                                                     scale=SCALE)
                            ins.then_inc(probs_ready, 1)
                    if n.chain and (i < NSEG - 1 or n.heads_on):
                        mem_copy(n, i)
                    for name in behind:
                        take(n, name)
                    if n.first == -1 and i == 0:
                        act.wait_ge(loaded_beta, 16)
                        act.activation(b1, braw, ACT.Exp, scale=-1.0).then_inc(beta_e, 1)
                if n.first == -1:
                    mem_copy(n, NSEG - 1)

            bodies(act, body)
            act.copy(rowmax[:, 0], rowmax[:, 1]).then_inc(attn_done, 1)

            act.wait_ge(attn_done, 1)
            act.wait_ge(l1_turned, 1)
            act.copy(rwT.rearrange("p c e -> p (c e)"), flat[0][:, 0:DC * E]).then_inc(l1_copied, 1)

            def l1_weight(w):
                act.wait_ge(l1_turned, w + 2)
                to = wqkvT[:, w] if w < 3 else wofT[:, w - 3]
                act.copy(to.rearrange("p c d -> p (c d)"), work[w % 4][:]).then_inc(l1_copied, 1)

            for w in range(4):
                l1_weight(w)
            for p in range(NT // 2):
                act.wait_ge(pair_turned, p + 1)
                if p >= 2:
                    act.wait_ge(pair_used, p - 1)
                act.copy(hcol[:, p % 2], flat[p % 2]).then_inc(pair_copied, 1)
            l1_weight(4)

            def row_turned(u, par):
                act.wait_ge(x_turned, u + 1)
                if not (isinstance(u, int) and u < 2):
                    act.wait_ge(x_used, u - 1)
                act.copy(xj[:, par], flat[par][:, 0:D]).then_inc(xj_copied, 1)

            row_turned(0, 0)
            row_turned(1, 1)
            act.wait_ge(top_done, 1)
            act.activation(gate, toplogit, ACT.Exp, scale=-1.0).then_inc(gate_exp, 1)

            def silu(n, par):
                act.wait_ge(x_used, n + 1)
                act.activation(sgate[:, par], work[2 * par][:], ACT.Silu).then_inc(silu_done, 1)

            def turned_hidden(n, par):
                act.wait_ge(hT_turned, n + 1)
                act.copy(hcol[:, par], mflat[0][:, 0:F]).then_inc(hT_copied, 1)

            def give_shared(n, t):
                act.wait_ge(down_done, n + 1)
                act.copy(shared[:, ds(t, 1)].rearrange("p a d -> p (a d)"), mflat[1][:, 0:D]).then_inc(y_out, 1)

            silu(0, 0)
            with act.Fori(0, (EARLY - 2) // 2) as pair:
                for par in range(2):
                    n = pair * 2 + (par + 1)
                    turned_hidden(n - 1, par)
                    silu(n, 1 - par)
                    give_shared(n - 1, n - 1)
                    row_turned(n + 1, par)
            for n in (EARLY - 1, EARLY):
                turned_hidden(n - 1, (n - 1) % 2)
                silu(n, n % 2)
                give_shared(n - 1, n - 1)
                row_turned(n + 1, (n + 1) % 2)

            def give_routed(j, par, stored):
                act.wait_ge(down_done, j + (EARLY + 1))
                if stored is not None:
                    act.wait_ge(y_stored[par], stored)
                act.copy(yj[:, par], mflat[1][:, 0:D]).then_inc(y_out, 1)

            def routed_tile(pair, par):
                n = pair * 2 + (EARLY + par + 1)
                turned_hidden(n - 1, par)
                silu(n, 1 - par)
                give_routed(pair * 2 + par, par, None if isinstance(pair, int) else pair * 16)
                row_turned(n + 1, par)

            for par in range(2):
                routed_tile(0, par)
            with act.Fori(1, (JOBS - 1) // 2 - 1) as pair:
                for par in range(2):
                    routed_tile(pair, par)
            for j in range(JOBS - 2, JOBS + 1):
                n = EARLY + j
                turned_hidden(n - 1, (n - 1) % 2)
                silu(n, n % 2)
                give_routed(j - 1, (j - 1) % 2, 16 * ((j - 1) // 2))
                row_turned(n + 1, (n + 1) % 2)

            x2T_v = x2T.rearrange("p c (g t r) -> p t c g r", t=NT, r=4)

            def copy_x2T(p):
                act.wait_ge(x2_turned, p + 1)
                for x in range(2):
                    ins = act.copy(x2T_v[:, 2 * p + x], flat[(p + X2_LAG + LATE) % 2][:, x * D:(x + 1) * D]
                                   .rearrange("p (c g r) -> p c g r", c=DC, r=4))
                ins.then_inc(x2T_copied, 1)

            for t in range(EARLY + 1, NT + 1):
                n = t + JOBS
                turned_hidden(n - 1, (n - 1) % 2)
                if t < NT:
                    silu(n, n % 2)
                if t - EARLY >= X2_LAG:
                    copy_x2T(t - EARLY - X2_LAG)
                give_shared(n - 1, t - 1)
                if t + 1 < NT:
                    row_turned(n + 1, (n + 1) % 2)
            for p in range(NT - EARLY - X2_LAG + 1, NT // 2):
                copy_x2T(p)

            def keys(b, e):
                act.wait_ge(qkv_done[e], 3 * b + 1)
                act.copy(kbuf[:, e], (work[1] if e == 0 else flat[0])[:, 0:S]).then_inc(k_copied[e], 1)

            keys(0, 0)
            keys(0, 1)
            for b in range(B):
                if b + 1 < B:
                    keys(b + 1, 0)
                    keys(b + 1, 1)
                for jj in range(2):
                    act.wait_ge(t3_done, 2 * b + jj + 1)
                    act.copy(x3T[:, b % 2, 2 * jj:2 * jj + 2].rearrange("p j d -> p (j d)"),
                             mflat[jj][:, 0:2 * D]).then_inc(x3T_copied, 1)

        @block.tensor
        def _(pe):
            pe.wait_ge(consts, 12)
            for b in range(B):
                pe.wait_ge(x_normed, NJ * (b + 1))
                for c in range(DC):
                    g = b * DC + c
                    if g >= 4:
                        pe.wait_ge(xT_copied, g - 3)
                    for j in range(NJ):
                        ins = pe.transpose(work[g % 4][:, j * P:(j + 1) * P], xnorm[:, b, j, c * P:(c + 1) * P], ident[:])
                    ins.then_inc(xT_written[g % 4], 1)
            pe.wait_ge(xT_copied, DC * B)

            def into(n, name, back=0):
                k = n.BANK[name]
                v = n.turn(name, back)
                if not (isinstance(v, int) and v == 0):
                    pe.wait_ge(freed[k], v)
                return work[k], filled[k]

            def consumed(n, name, back=0):
                k = n.BANK[name]
                pe.wait_ge(freed[k], n.turn(name, back) + 1)

            def project_qk(n, b):
                m = 1 - n.par
                for qk in range(2):
                    w, done = into(n, ("qk"[qk], b))
                    if b == 0 and qk == 0:
                        pe.wait_ge(w_loaded[m], weights_count(n))
                    for c in range(DC):
                        ins = pe.matmul(w[:], wqkv[:, m, qk, c], xT[:, c, b], start=(c == 0), stop=(c == DC - 1))
                    ins.then_inc(done, 1)

            def weights_count(n):
                k = (n.first + 1) // 2 + 1
                return 48 * k if n.loop is None else 48 * k + 48 * n.loop

            def project_v(n, b):
                m = 1 - n.par
                w, done = into(n, ("V", b))
                for j in range(NJ):
                    for c in range(DC):
                        ins = pe.matmul(w[:, j * P:(j + 1) * P], xT[:, c, b, j * P:(j + 1) * P], wqkv[:, m, 2, c],
                                        start=(c == 0), stop=(c == DC - 1))
                ins.then_inc(done, 1)

            def turn_keys(n, b):
                m = 1 - n.par
                pe.wait_ge(sigma_done, n.count(2 * B, 2 * B + 2 * b + 2))
                w, done = into(n, ("sk", b))
                pairs = sqk[:, m, b].rearrange("p s c -> p (s c)").rearrange("p (j x) -> p j x", j=NJ)
                for j in range(NJ):
                    ins = pe.transpose(w[:, j * P:(j + 1) * P], pairs[:, j, SEG:3 * SEG], ident[:])
                ins.then_inc(done, 1)

            def scores(n, b):
                consumed(n, ("k", b))
                w, done = into(n, ("sc", b))
                for i in range(NSEG):
                    c = slice(i * SEG, (i + 1) * SEG)
                    ins = pe.matmul(w[own(i), (i // 2) * SEG:(i // 2 + 1) * SEG], raw[:, 0, b, c], raw[:, 1, b, c],
                                    start=True, stop=True)
                ins.then_inc(done, 1)

            def turn_probs(n, b):
                pe.wait_ge(probs_ready, n.count(B, B + b + 1))
                w, done = into(n, ("PT", b))
                for j in range(NJ):
                    ins = pe.transpose(w[:, j * P:(j + 1) * P], pbd[:, b, j], ident[:])
                    if b == B - 1 and j == 0:
                        ins.then_inc(proj_done, 1)
                ins.then_inc(done, 1)

            def probs_values(n, j):
                w, done = into(n, ("PV", j))
                for b in range(B):
                    ins = pe.matmul(w[:, b * P:(b + 1) * P], pt[:, n.par, b, j], v1[:, n.par, b, j], start=True, stop=True)
                ins.then_inc(done, 1)

            def turn_att(n, j, back):
                pe.wait_ge(att_ready, n.count(NJ, j + 1 - NJ * back))
                consumed(n, ("PV", j), back)
                w, done = into(n, ("attT", j))
                for b in range(B):
                    ins = pe.transpose(w[:, b * P:(b + 1) * P], fromm[:, j % 2, b], ident[:])
                ins.then_inc(done, 1)

            def project_out(n):
                consumed(n, ("attT", NJ - 1))
                if n.first == 1:
                    pe.wait_ge(wo_loaded, 16)
                w, done = into(n, ("Wo",))
                tokens = attT.rearrange("p b j (r c) -> p c (b j r)", c=H)
                for c in range(H):
                    ins = pe.matmul(w[:, 0:D], tokens[:, c], wo[:, c], start=(c == 0), stop=(c == H - 1))
                ins.then_inc(done, 1)

            def seed():
                for r in range(2):
                    pe.matmul(memp[r][:, :, 0:MEM], seed_l[:], seed_r[:], start=True, stop=False,
                              skip_group_check=True).then_inc(mem_written[r], 1)

            def read_memories(n, i):
                for r in range(2):
                    pe.wait_ge(mem_copied[r], n.count(NSEG, i + 1))
                    if not (n.first == 0 and i == 0):
                        pe.wait_ge(fromm_ready[r], n.count(NSEG, i))
                    for bb in range(2):
                        b = 2 * r + bb
                        ins = pe.matmul(readp[r][:, bb, 0:MEM], sqk[:, n.par, b, i], mem[:, b, 0:MEM],
                                        start=True, stop=True)
                    ins.then_inc(read_done[r], 1)

            def update_memories(n, i):
                for r in range(2):
                    pe.wait_ge(delta_ready[r], n.count(NSEG - 1, i + 1))
                    for bb in range(2):
                        b = 2 * r + bb
                        ins = pe.matmul(memp[r][:, bb, 0:MEM], skt[own(i), n.par, b, i // 2], delta[own(i), b, 0:MEM],
                                        start=False, stop=False, skip_group_check=True)
                    ins.then_inc(mem_written[r], 1)

            def make(n, name):
                if not n.makes(name):
                    return
                kind = name[0]
                if kind == "q":
                    project_qk(n, name[1])
                elif kind == "sk":
                    turn_keys(n, name[1])
                elif kind == "sc":
                    scores(n, name[1])
                elif kind == "V":
                    project_v(n, name[1])
                elif kind == "PT":
                    turn_probs(n, name[1])
                elif kind == "Wo":
                    project_out(n)
                elif kind == "attT":
                    turn_att(n, name[1], int(name[1] == NJ - 1))
                elif kind == "PV":
                    probs_values(n, name[1])

            def body(n):
                for i in range(NSEG):
                    before, behind = step_products(i)
                    if n.chain:
                        read_memories(n, i)
                    for name in before:
                        make(n, name)
                    if n.chain and i < NSEG - 1:
                        update_memories(n, i)
                    elif i == NSEG - 1 and n.heads_on:
                        seed()
                    for name in behind:
                        make(n, name)

            bodies(pe, body)

            pe.wait_ge(attn_done, 1)
            pe.wait_ge(small_loaded, 48)
            for c in range(DC):
                ins = pe.transpose(flat[0][:, c * E:(c + 1) * E], rwraw[0:E, c * P:(c + 1) * P], ident[0:E, 0:E])
            ins.then_inc(l1_turned, 1)
            pe.wait_ge(l1_loaded, 16 * 5)

            def l1_weight(w):
                for c in range(DC):
                    for r in range(DC):
                        ins = pe.transpose(work[w % 4][:, c * D + r * P:c * D + (r + 1) * P],
                                           l1raw[:, w, r, c * P:(c + 1) * P], ident[:])
                ins.then_inc(l1_turned, 1)

            for w in range(4):
                l1_weight(w)
            pe.wait_ge(l1_copied, 1)

            def turn_pair(p):
                pe.wait_ge(xn1_ready, 2 * p + 2)
                if p >= 2:
                    pe.wait_ge(pair_copied, p - 1)
                for x in range(2):
                    for c in range(DC):
                        ins = pe.transpose(flat[p % 2][:, (x * DC + c) * P:(x * DC + c + 1) * P],
                                           Y[:, 2 * p + x, c * P:(c + 1) * P], ident[:])
                ins.then_inc(pair_turned, 1)

            def logits(p):
                pe.wait_ge(pair_copied, p + 1)
                for x in range(2):
                    t = 2 * p + x
                    for c in range(DC):
                        ins = pe.matmul(mflat[0][:, t * E:(t + 1) * E],
                                        hcol[:, p % 2, (x * DC + c) * P:(x * DC + c + 1) * P], rwT[:, c],
                                        start=(c == 0), stop=(c == DC - 1))
                ins.then_inc(pair_used, 1)

            turn_pair(0)
            for p in range(NT // 2):
                if p + 1 < NT // 2:
                    turn_pair(p + 1)
                logits(p)
            pe.wait_ge(wscaled, DC)
            pe.wait_ge(l1_copied, 2)
            l1_weight(4)
            pe.wait_ge(l1_copied, 6)

            def turn_row(u, par):
                if not (isinstance(u, int) and u < 2):
                    pe.wait_ge(xj_copied, u - 1)
                for c in range(DC):
                    ins = pe.transpose(flat[par][:, c * P:(c + 1) * P], xrow[:, par, c * P:(c + 1) * P], ident[:])
                ins.then_inc(x_turned, 1)

            def turn_norm(u, par):
                pe.wait_ge(xrow_ready, u + 1 - JOBS if isinstance(u, int) and u >= LATE else u + 1)
                turn_row(u, par)

            def gate_up(n, par, e):
                pe.wait_ge(xj_copied, n + 1)
                if not (isinstance(n, int) and n < 2):
                    pe.wait_ge(h_ready, n - 1)
                for half in range(2):
                    for c in range(DC):
                        ins = pe.matmul(work[2 * par + half][:], xj[:, par, c * P:(c + 1) * P],
                                        wgu[:, e, c, half * F:(half + 1) * F] if isinstance(e, int) else
                                        wgu_flat[:, ds(e * (DC * 2 * F) + (c * 2 * F + half * F), F)],
                                        start=(c == 0), stop=(c == DC - 1))
                ins.then_inc(x_used, 1)

            def turn_hidden(n, par):
                pe.wait_ge(h_ready, n + 1)
                if not (isinstance(n, int) and n == 0):
                    pe.wait_ge(hT_copied, n)
                for k in range(FC):
                    ins = pe.transpose(mflat[0][:, k * P:(k + 1) * P], hrow[:, par, k * P:(k + 1) * P], ident[:])
                ins.then_inc(hT_turned, 1)

            def down(n, par, e):
                pe.wait_ge(hT_copied, n + 1)
                if not (isinstance(n, int) and n == 0):
                    pe.wait_ge(y_out, n)
                for k in range(FC):
                    ins = pe.matmul(mflat[1][:, 0:D], hcol[:, par, k * P:(k + 1) * P],
                                    wdn[:, e, k] if isinstance(e, int) else
                                    wdn_flat[:, ds(e * (FC * D) + k * D, D)],
                                    start=(k == 0), stop=(k == FC - 1))
                ins.then_inc(down_done, 1)

            wgu_flat = wgu.rearrange("p e c n -> p (e c n)")
            wdn_flat = wdn.rearrange("p e k n -> p (e k n)")
            pe.wait_ge(shared_loaded, 32)
            turn_norm(0, 0)
            turn_norm(1, 1)
            gate_up(0, 0, E)
            pe.wait_ge(onehot_ready, 1)
            pe.wait_ge(post_consts, 9)
            hot = onehot.rearrange("p t e -> p (t e)")
            pe.matmul(mflat[0][:, 0:NT * E], tri, hot, start=True, stop=True).then_inc(ranks_done, 1)
            pe.matmul(mflat[1][:, 0:NT * E], ones, hot, start=True, stop=True).then_inc(ranks_done, 1)
            pe.wait_ge(ranks_copied, 2)
            def shared_tile(n, par):
                turn_hidden(n - 1, par)
                gate_up(n, 1 - par, E)
                down(n - 1, par, E)
                turn_norm(n + 1, par)

            for par in range(2):
                shared_tile(par + 1, par)
            with pe.Fori(1, (EARLY - 2) // 2) as pair:
                for par in range(2):
                    shared_tile(pair * 2 + (par + 1), par)

            jobi_i = jobi.bitcast(mybir.dt.int32)

            def expert(j):
                return pe.value_load(jobi_i[0:1, ds(j, 1)], min_val=0, max_val=E - 1)

            def turn_sorted(j, par, loads):
                pe.wait_ge(xs_loaded[par], loads)
                turn_row(j + EARLY, par)

            turn_hidden(EARLY - 2, 0)
            gate_up(EARLY - 1, 1, E)
            down(EARLY - 2, 0, E)
            turn_sorted(0, 0, 16)
            pe.wait_ge(experts_loaded, 32 * E)
            turn_hidden(EARLY - 1, 1)
            gate_up(EARLY, 0, expert(0))
            down(EARLY - 1, 1, E)
            turn_sorted(1, 1, 16)
            with pe.Fori(0, (JOBS - 1) // 2 - 1) as pair:
                for par in range(2):
                    j = pair * 2 + (par + 1)
                    turn_hidden(j + (EARLY - 1), par)
                    gate_up(j + EARLY, 1 - par, expert(j))
                    down(j + (EARLY - 1), par, expert(j - 1))
                    turn_sorted(j + 1, par, pair * 16 + 32)
            for j in range(JOBS - 2, JOBS + 1):
                n = EARLY + j
                turn_hidden(n - 1, (n - 1) % 2)
                gate_up(n, n % 2, expert(j) if j < JOBS else E)
                down(n - 1, (n - 1) % 2, expert(j - 1))
                if j + 1 < JOBS:
                    turn_sorted(j + 1, (j + 1) % 2, 16 * ((j + 1) // 2 + 1))
                else:
                    turn_norm(n + 1, (n + 1) % 2)

            def turn_x2(p):
                pe.wait_ge(xn2_ready, 2 * p + 2)
                if p >= 2:
                    pe.wait_ge(x2T_copied, p - 1)
                for x in range(2):
                    for c in range(DC):
                        ins = pe.transpose(flat[(p + X2_LAG + LATE) % 2][:, (x * DC + c) * P:(x * DC + c + 1) * P],
                                           Y[:, 2 * p + x, c * P:(c + 1) * P], ident[:])
                ins.then_inc(x2_turned, 1)

            for t in range(EARLY + 1, NT + 1):
                n = t + JOBS
                turn_hidden(n - 1, (n - 1) % 2)
                if t < NT:
                    gate_up(n, n % 2, E)
                if t - EARLY >= X2_LAG:
                    turn_x2(t - EARLY - X2_LAG)
                down(n - 1, (n - 1) % 2, E)
                if t + 1 < NT:
                    if t - EARLY > X2_LAG:
                        pe.wait_ge(x2T_copied, t - EARLY - X2_LAG)
                    turn_norm(n + 1, (n + 1) % 2)
            for p in range(NT - EARLY - X2_LAG + 1, NT // 2):
                turn_x2(p)

            def project(b, e):
                banks = [work[0], work[1], work[2]] if e == 0 else [work[3], flat[0], flat[1]]
                if b:
                    pe.wait_ge(vh_done[e], b)
                for w in (1, 2, 0):
                    for c in range(DC):
                        ins = pe.matmul(banks[w][:, 0:S], wqkvT[:, w, c, e * P:(e + 1) * P],
                                        x2T[:, c, b * S:(b + 1) * S], start=(c == 0), stop=(c == DC - 1))
                    ins.then_inc(qkv_done[e], 1)

            pe.wait_ge(x2T_copied, NT // 2)
            project(0, 0)
            project(0, 1)
            pe.wait_ge(y_out, NT + JOBS)
            def project_o(b):
                m = b % 2
                for e in range(2):
                    pe.wait_ge(vh_done[e], b + 1)
                for jj in range(2):
                    if b:
                        pe.wait_ge(x3T_copied, 2 * b - 1 + jj)
                    for x in range(2):
                        for e in range(2):
                            j = 2 * jj + x
                            ins = pe.matmul(mflat[jj][:, x * D:(x + 1) * D], vh[:, m, e, j * P:(j + 1) * P], wofT[:, 0, e],
                                            start=(e == 0), stop=(e == 1))
                    ins.then_inc(o_done, 1)

            def ffn(b):
                for jj in range(2):
                    pe.wait_ge(x3T_copied, 2 * b + jj + 1)
                    for x in range(2):
                        for c in range(DC):
                            ins = pe.matmul(ffn_banks[jj][:, x * D:(x + 1) * D],
                                            x3T[:, b % 2, 2 * jj + x, c * P:(c + 1) * P],
                                            wofT[:, 1, c], start=(c == 0), stop=(c == DC - 1))
                    ins.then_inc(f_done, 1)

            def turn_x3(b):
                for jj in range(2):
                    pe.wait_ge(xn3_ready, NJ * b + 2 * jj + 2)
                    pe.wait_ge(o_used, NJ * b + 2 * jj + 2)
                    for x in range(2):
                        for c in range(DC):
                            ins = pe.transpose(mflat[jj][:, (x * DC + c) * P:(x * DC + c + 1) * P],
                                               xn3[:, b % 2, 2 * jj + x, c * P:(c + 1) * P], ident[:])
                    ins.then_inc(t3_done, 1)

            for b in range(B + 1):
                if b < B:
                    project_o(b)
                if b:
                    ffn(b - 1)
                if b + 1 < B:
                    project(b + 1, 0)
                    if b:
                        pe.wait_ge(f_used, 2 * b)
                    project(b + 1, 1)
                if b < B:
                    turn_x3(b)


_INS = ["L0_attn_x", "L0_attn_Wq", "L0_attn_Wk", "L0_attn_Wv", "L0_attn_Wo", "L0_attn_betas", "L0_ffn_router_w",
        "L0_ffn_w_gate_up", "L0_ffn_w_down", "L0_ffn_shared_gate_up", "L0_ffn_shared_down", "L1_attn_Wq",
        "L1_attn_Wk", "L1_attn_Wv", "L1_attn_Wo", "L1_ffn_weight", "L1_ffn_scale_weight", "L1_ffn_bias"]
_OUTS = [((B, S, D), "float32")]


def kernel(**inputs):
    import numpy as _np
    import concourse.bacc as _bacc
    from concourse import mybir as _mybir
    from concourse.bass_utils import run_bass_kernel_spmd as _run

    nc = _bacc.Bacc("TRN2", target_bir_lowering=False, num_devices=1)
    arrays, dram = {}, {}
    for name in _INS:
        a = _np.ascontiguousarray(inputs[name])
        arrays[f"in_{name}_dram"] = a
        dram[name] = nc.dram_tensor(f"in_{name}_dram", a.shape, _mybir.dt.from_np(a.dtype), kind="ExternalInput").ap()
    (shape, dtype), = _OUTS
    out = nc.dram_tensor("out_0_dram", shape, _mybir.dt.from_np(_np.dtype(dtype)), kind="ExternalOutput").ap()
    sandwich(nc, dram, out)
    return _run(nc, [arrays], core_ids=[0]).results[0]["out_0_dram"]
```
